# Optimizing a Trainium2 kernel written in Bass

```python
import numpy as np
import jax
import jax.numpy as jnp

def _softmax(x, axis=-1):
    return jax.nn.softmax(x, axis=axis)

def _gelu(x):
    return jax.nn.gelu(x, approximate=True)

def _silu(x):
    return jax.nn.silu(x)

def _sigmoid(x):
    return jax.nn.sigmoid(x)

def _layernorm(x, axis=-1, eps=1e-05):
    m = jnp.mean(x, axis=axis, keepdims=True)
    v = jnp.var(x, axis=axis, keepdims=True)
    return (x - m) / jnp.sqrt(v + eps)

def _scatter_add(tgt, idx, src, axis=0):
    return tgt.at[idx].add(src)

def _segment_sum(src, seg, n):
    return jax.ops.segment_sum(src, seg, n)
kernel_name = 'mk_gnn_resnorm_d1_gnn_r32_cc2a6d'

def setup_inputs(seed: int=0):
    np.random.seed(seed)
    _w = jnp.asarray

    def _rec_inputs():
        import jax
        import jax.numpy as jnp
        _gk = jax.random.key(seed)
        x = 8.953e-05 + 1 * jax.random.normal(jax.random.fold_in(_gk, 1), (3125, 32), jnp.float32)
        src = jax.random.randint(jax.random.fold_in(_gk, 2), (100000,), 0, 3125, jnp.int32)
        dst = jax.random.randint(jax.random.fold_in(_gk, 3), (100000,), 0, 3125, jnp.int32)
        _o = jnp.argsort(dst, stable=True)
        src = src[_o]
        dst = dst[_o]
        edge_attr_3 = jax.random.uniform(jax.random.fold_in(_gk, 11), (100000, 3), jnp.float32, 0.0, 0.999998)
        return (x, src, dst, edge_attr_3)
    x, src, dst, edge_attr_3 = _rec_inputs()

    def _L0_gnn_setup():
        import jax, jax.numpy as jnp
        import numpy as np
        D = 3
        KS = 5
        K = KS ** D
        S = 2 ** D
        _COMBOS = np.array([[s >> d & 1 for d in range(D)] for s in range(S)], dtype=np.int32)
        _STRIDES = np.array([KS ** (D - 1 - d) for d in range(D)], dtype=np.int32)

        def spline_basis(pseudo):
            pos = pseudo * (KS - 1)
            i0 = jnp.clip(jnp.floor(pos), 0, KS - 2).astype(jnp.int32)
            frac = pos - i0
            combos = jnp.asarray(_COMBOS)
            basis = jnp.prod(jnp.where(combos[None] == 1, frac[:, None, :], 1.0 - frac[:, None, :]), axis=-1)
            idx = jnp.sum((i0[:, None, :] + combos[None]) * jnp.asarray(_STRIDES)[None, None, :], axis=-1)
            return (basis, idx)

        def spline_conv(x, row, col, basis, idx, W, b):
            N = x.shape[0]
            Fout = W.shape[2]
            z = jnp.einsum('ni,kio->nko', x, W).reshape(N * K, Fout)
            gathered = z[col[:, None] * K + idx]
            msg = jnp.einsum('es,eso->eo', basis, gathered)
            out = jax.ops.segment_sum(msg, row, num_segments=N)
            deg = jax.ops.segment_sum(jnp.ones_like(msg[:, 0]), row, num_segments=N)
            return out / jnp.maximum(deg, 1.0)[:, None] + b
        key = jax.random.key(seed)
        ks = jax.random.split(key, 13)
        N, E, Fin, Fout = (625, 10000, 32, 32)

        def u(k, shape, size):
            bound = 1.0 / np.sqrt(size)
            return jax.random.uniform(k, shape, jnp.float32, -bound, bound)
        return dict(x=jax.random.normal(ks[0], (N, Fin), jnp.float32), edge_index=jax.random.randint(ks[1], (2, E), 0, N, dtype=jnp.int32), pseudo=jax.random.uniform(ks[2], (E, D), jnp.float32), stn1_w=u(ks[3], (K, 1, 64), 1 * S), stn1_b=u(ks[4], (64,), 1 * S), stn2_w=u(ks[5], (K, 64, 64), 64 * S), stn2_b=u(ks[6], (64,), 64 * S), stn3_w=u(ks[7], (64, 64), 64), stn3_b=u(ks[8], (64,), 64), stn4_w=u(ks[9], (64, 3), 64), stn4_b=u(ks[10], (3,), 64), conv_w=u(ks[11], (K, Fin, Fout), Fin * S), conv_b=u(ks[12], (Fout,), Fin * S))
    _L0_gnn_all = _L0_gnn_setup()
    _L0_gnn_in = {k: v for k, v in _L0_gnn_all.items() if k in ('stn1_w', 'stn1_b', 'stn2_w', 'stn2_b', 'stn3_w', 'stn3_b', 'stn4_w', 'stn4_b', 'conv_w', 'conv_b')}
    del _L0_gnn_all
    return {'x': x, 'src': src, 'dst': dst, 'edge_attr_3': edge_attr_3, 'L0_gnn_stn1_w': _L0_gnn_in['stn1_w'], 'L0_gnn_stn1_b': _L0_gnn_in['stn1_b'], 'L0_gnn_stn2_w': _L0_gnn_in['stn2_w'], 'L0_gnn_stn2_b': _L0_gnn_in['stn2_b'], 'L0_gnn_stn3_w': _L0_gnn_in['stn3_w'], 'L0_gnn_stn3_b': _L0_gnn_in['stn3_b'], 'L0_gnn_stn4_w': _L0_gnn_in['stn4_w'], 'L0_gnn_stn4_b': _L0_gnn_in['stn4_b'], 'L0_gnn_conv_w': _L0_gnn_in['conv_w'], 'L0_gnn_conv_b': _L0_gnn_in['conv_b']}

def reference(x, src, dst, edge_attr_3, L0_gnn_stn1_w, L0_gnn_stn1_b, L0_gnn_stn2_w, L0_gnn_stn2_b, L0_gnn_stn3_w, L0_gnn_stn3_b, L0_gnn_stn4_w, L0_gnn_stn4_b, L0_gnn_conv_w, L0_gnn_conv_b):
    import jax
    import jax.numpy as jnp

    def _L0_gnn_ref(x, edge_index, pseudo, stn1_w, stn1_b, stn2_w, stn2_b, stn3_w, stn3_b, stn4_w, stn4_b, conv_w, conv_b):
        import jax, jax.numpy as jnp
        import numpy as np
        D = 3
        KS = 5
        K = KS ** D
        S = 2 ** D
        _COMBOS = np.array([[s >> d & 1 for d in range(D)] for s in range(S)], dtype=np.int32)
        _STRIDES = np.array([KS ** (D - 1 - d) for d in range(D)], dtype=np.int32)

        def spline_basis(pseudo):
            pos = pseudo * (KS - 1)
            i0 = jnp.clip(jnp.floor(pos), 0, KS - 2).astype(jnp.int32)
            frac = pos - i0
            combos = jnp.asarray(_COMBOS)
            basis = jnp.prod(jnp.where(combos[None] == 1, frac[:, None, :], 1.0 - frac[:, None, :]), axis=-1)
            idx = jnp.sum((i0[:, None, :] + combos[None]) * jnp.asarray(_STRIDES)[None, None, :], axis=-1)
            return (basis, idx)

        def spline_conv(x, row, col, basis, idx, W, b):
            N = x.shape[0]
            Fout = W.shape[2]
            z = jnp.einsum('ni,kio->nko', x, W).reshape(N * K, Fout)
            gathered = z[col[:, None] * K + idx]
            msg = jnp.einsum('es,eso->eo', basis, gathered)
            out = jax.ops.segment_sum(msg, row, num_segments=N)
            deg = jax.ops.segment_sum(jnp.ones_like(msg[:, 0]), row, num_segments=N)
            return out / jnp.maximum(deg, 1.0)[:, None] + b
        N = x.shape[0]
        row, col = (edge_index[0], edge_index[1])
        basis, idx = spline_basis(pseudo)
        h = jnp.ones((N, 1), x.dtype)
        h = jax.nn.elu(spline_conv(h, row, col, basis, idx, stn1_w, stn1_b))
        h = jax.nn.elu(spline_conv(h, row, col, basis, idx, stn2_w, stn2_b))
        h = jax.nn.elu(h @ stn3_w + stn3_b)
        t = h @ stn4_w + stn4_b
        new_pseudo = jnp.clip(pseudo + t[col] - t[row], 0.0, 1.0)
        basis2, idx2 = spline_basis(new_pseudo)
        return spline_conv(x, row, col, basis2, idx2, conv_w, conv_b)
    edge_index = jnp.stack([src, dst])
    x = _layernorm(x + _L0_gnn_ref(x, edge_index, edge_attr_3, L0_gnn_stn1_w, L0_gnn_stn1_b, L0_gnn_stn2_w, L0_gnn_stn2_b, L0_gnn_stn3_w, L0_gnn_stn3_b, L0_gnn_stn4_w, L0_gnn_stn4_b, L0_gnn_conv_w, L0_gnn_conv_b), axis=-1)
    return x

_drawn_inputs = setup_inputs


def setup_inputs(seed=0):
    import zlib

    import numpy as np

    out = dict(_drawn_inputs(seed))
    spreads = {}
    factors = {'edge_attr_3': 2.844,
     'L0_gnn_stn1_w': 8.0,
     'L0_gnn_stn1_b': 8.0,
     'L0_gnn_stn2_w': 8.0,
     'L0_gnn_stn2_b': 8.0,
     'L0_gnn_stn3_w': 8.0,
     'L0_gnn_stn3_b': 8.0,
     'L0_gnn_stn4_w': 8.0,
     'L0_gnn_stn4_b': 8.0,
     'L0_gnn_conv_w': 2.803}
    for name, (base, spread) in spreads.items():
        noise = np.random.default_rng([zlib.crc32(name.encode()), seed]).standard_normal(out[name].shape)
        drawn = base * np.exp(spread * noise) if base else spread * noise
        out[name] = jnp.asarray(drawn.astype(out[name].dtype))
    for name, factor in factors.items():
        out[name] = (out[name] * factor).astype(out[name].dtype)
    return out
```

```python
import concourse.bass as bass
from concourse import mybir
from contextlib import ExitStack

F32 = mybir.dt.float32
BF16 = mybir.dt.bfloat16
I32 = mybir.dt.int32
ALU = mybir.AluOpType
ACT = mybir.ActivationFunctionType
AX = mybir.AxisListType

P = 128
N, FIN, FH = 3125, 32, 64
E, D = 100000, 3
KS = 5
K = KS ** D
NT = -(-N // P)
EP, ET = 125, E // 125
Q = 32
OV0 = NT * P
BT = 2 * NT
assert -(-E // Q) <= NT * P
TPB = P // (P // Q)
ST = BT * TPB
W = 8
A0, VALID, COL, ROW, CLO, CHI = 0, 3, 4, 5, 6, 7
HX = FH + FIN
BIG = 3.0e38


class Chain:

    def __init__(self, eng, sem):
        self.eng, self.sem, self.base, self.n = eng, sem, 0, 0

    def did(self, ins):
        ins.then_inc(self.sem, 1)
        self.n += 1
        return self.sem, self.base + self.n

    def need(self, ticket):
        self.eng.wait_ge(*ticket)

    def turn(self, start, it, per):
        self.base, self.n = start + it * per, 0

    def close(self, start, turns, per):
        assert self.n == per, (self.n, per)
        self.base, self.n = start + turns * per, 0

    def now(self):
        return self.base + self.n


def hold(eng, sem, value, held):
    eng.wait_ge(sem, value)
    eng.sem_inc(held, 1)


def spline_net(nc, x, src, dst, attr, w1, b1, w2, b2, w3, b3, w4, b4, wc, bc, out):
    with ExitStack() as ctx:
        def sb(name, shape, dt=F32, c=ctx):
            return c.enter_context(nc.sbuf_tensor(name, shape, dt))

        def ps(name, shape, dt=F32, c=ctx):
            return c.enter_context(nc.psum_tensor(name, shape, dt))

        def sem(name):
            return ctx.enter_context(nc.semaphore(name))

        slots = nc.dram_tensor("slots", (P * ST, W), F32, kind="Internal").ap()
        held = {e: sem(f"held_{e}") for e in ("pe", "act", "dve", "pool", "sp")}

        iota = sb("iota", [P, P])
        pid = sb("pid", [P, 1])
        npid = sb("npid", [P, 1])
        one = sb("one", [P, 1])
        ident = sb("ident", [P, P])
        deg = sb("deg", [P, NT])

        with ExitStack() as ab:
            place_edges(nc, ab, sb, ps, sem, held, src, dst, attr, slots, iota, pid, npid, one, ident, deg)

        rec = sb("rec", [P, ST, W])
        blocks = sb("blocks", [P, BT, FH])
        hid = sb("hid", [P, NT, FH])
        x_nodes = sb("x_nodes", [P, NT, FIN])
        wt1 = sb("wt1", [KS * KS, KS * FH])
        wt2 = sb("wt2", [K, FH * FH])
        wtc = sb("wtc", [K, FIN * FIN])
        wt3, wt4 = sb("wt3", [FH, FH]), sb("wt4", [FH, D])
        bt1, bt2, btc, bt4 = sb("bt1", [P, FH]), sb("bt2", [P, FH]), sb("btc", [P, FIN]), sb("bt4", [P, D])
        bt3 = sb("bt3", [FH, 1])
        ovn, ov_lo, ov_hi = sb("ovn", [P, NT]), sb("ov_lo", [P, NT]), sb("ov_hi", [P, NT])
        ovn_i, ov_i = sb("ovn_i", [P, NT], I32), sb("ov_i", [P, NT], I32)
        inv_degree = sb("inv_degree", [P, NT])
        of_block = sb("of_block", [P, P // Q])
        up_c, down_c, up_floor, down_floor = [sb(n, [P, D, KS]) for n in ("up_c", "down_c", "up_floor", "down_floor")]
        table = nc.dram_tensor("table", (NT * P, HX), F32, kind="Internal").ap()
        x_slots = nc.dram_tensor("x_slots", (P, ST * FIN), F32, kind="Internal").ap()
        t_nodes = nc.dram_tensor("t_nodes", (NT * P, D), F32, kind="Internal").ap()
        t_blocks = nc.dram_tensor("t_blocks", (P, BT * D), F32, kind="Internal").ap()

        hat_consts = (up_c, down_c, up_floor, down_floor)
        first_layer(nc, sb, ps, sem, held, locals())
        gather_overflow(nc, sb, ps, sem, held, iota, blocks, ov_lo, ov_hi, inv_degree, bt1, FH, hid, "one")
        to_table(nc, sem, hid, x_nodes, table)
        conv(nc, sb, ps, sem, held, "two", FH, rec, None, hat_consts, blocks, wt2, table, x_slots)
        gather_overflow(nc, sb, ps, sem, held, iota, blocks, ov_lo, ov_hi, inv_degree, bt2, FH, hid, "two")
        with ExitStack() as c3:
            moved = sb("moved", [P, ST, D], F32, c3)
            t_node(nc, sb, ps, sem, held, hid, wt3, bt3, wt4, bt4, ident, ovn_i, t_nodes, t_blocks,
                   rec, moved, iota, npid, one)
            conv(nc, sb, ps, sem, held, "three", FIN, rec, moved, hat_consts, blocks, wtc, None, x_slots)
        gather_overflow(nc, sb, ps, sem, held, iota, blocks, ov_lo, ov_hi, inv_degree, btc, FIN, None, "three",
                        x_nodes, out)




def place_edges(nc, ab, sb, ps, sem, held, src, dst, attr, slots, iota, pid, npid, one, ident, deg):
    G = 20
    GN = ET // G
    C = 8
    SC = 40
    SN, CN = ET // SC, SC // C

    iota_i = sb("iota_i", [P, P], I32, ab)
    pid_i = sb("pid_i", [P, 1], I32, ab)
    lower = sb("lower", [P, P], F32, ab)
    upper = sb("upper", [P, P], F32, ab)
    ones = sb("ones", [P, P], F32, ab)
    zeros = sb("zeros", [P, ST], F32, ab)
    src_i = sb("src_i", [EP, ET], I32, ab)
    dst_i = sb("dst_i", [EP, ET], I32, ab)
    tmp_i = sb("tmp_i", [EP, ET], I32, ab)
    edge_attr = sb("edge_attr", [EP, ET * D], F32, ab)
    row = sb("row", [EP, ET], F32, ab)
    row_lo = sb("row_lo", [EP, ET], F32, ab)
    row_hi = sb("row_hi", [EP, ET], F32, ab)
    hot_lo = sb("hot_lo", [EP, 2, G, P], BF16, ab)
    hot_hi = sb("hot_hi", [EP, 2, G, NT], BF16, ab)
    before = sb("before", [P, ET + 1, NT], F32, ab)
    onescan = sb("onescan", [P, ET], F32, ab)
    over_i = sb("over_i", [P, NT], I32, ab)
    over = sb("over", [P, NT], F32, ab)
    over_at = sb("over_at", [P, NT], F32, ab)
    hi_sum = sb("hi_sum", [P, NT], F32, ab)

    src_in, dst_in, attr_in, cleared = sem("src_in"), sem("dst_in"), sem("attr_in"), sem("cleared")
    zero_ready, const_ready, hot_ready, hist_ready = sem("zero_ready"), sem("const_ready"), sem("hot_ready"), sem("hist_ready")
    hist_free, dve_a, pool_a, over_ready, pre_ready = sem("hist_free"), sem("dve_a"), sem("pool_a"), sem("over_ready"), sem("pre_ready")

    with ExitStack() as pa:
        hist = ps("hist", [P, 2, 512], F32, pa)
        over_ps = ps("over_ps", [P, 512], F32, pa)
        block = pa.enter_context(nc.Block())

        @block.sync
        def _(sp):
            sp.dma_start(src_i[:, :], src.rearrange("(p t) -> p t", p=EP)).then_inc(src_in, 16)
            sp.dma_start(dst_i[:, :], dst.rearrange("(p t) -> p t", p=EP)).then_inc(dst_in, 16)
            sp.dma_start(edge_attr[:, :], attr.rearrange("(p t) d -> p (t d)", p=EP)).then_inc(attr_in, 16)
            sp.wait_ge(zero_ready, 1)
            sp.dma_start(slots.rearrange("(p w t) c -> p w (t c)", p=P, w=W),
                         zeros[:, :].unsqueeze(1).to_broadcast([P, W, ST])).then_inc(cleared, 16)
            sp.wait_ge(cleared, 16)

        @block.gpsimd
        def _(pool):
            ch = Chain(pool, pool_a)
            pool.iota(iota_i[:, :], [[1, P]], base=0, channel_multiplier=0)
            pool.iota(pid_i[:, :], [[0, 1]], base=0, channel_multiplier=1)
            nc.gpsimd.memset(ones[:, :], 1.0)
            t = ch.did(nc.gpsimd.memset(ident[:, :], 0.0))
            ch.need(t)
            ch.did(nc.gpsimd.affine_select(out=ident[:, :], in_=ident[:, :], compare_op=ALU.not_equal, fill=1.0,
                                           base=0, pattern=[[-1, P]], channel_multiplier=1))
            ch.did(nc.gpsimd.affine_select(out=lower[:, :], in_=ones[:, :], compare_op=ALU.is_gt, fill=0.0,
                                           base=0, pattern=[[-1, P]], channel_multiplier=1))
            t = ch.did(nc.gpsimd.affine_select(out=upper[:, :], in_=ones[:, :], compare_op=ALU.is_gt, fill=0.0,
                                               base=0, pattern=[[1, P]], channel_multiplier=-1))
            ch.need(t)
            nc.gpsimd.memset(one[:, :], 1.0).then_inc(const_ready, 1)

        @block.vector
        def _(dve):
            ch = Chain(dve, dve_a)
            nc.vector.memset(zeros[:, :], 0.0).then_inc(zero_ready, 1)
            nc.vector.memset(onescan[:, :], 1.0)
            nc.vector.memset(before[:, 0, :], 0.0)
            dve.wait_ge(src_in, 16)
            t = ch.did(nc.vector.tensor_scalar(tmp_i[:, :], src_i[:, :], P - 1, None, ALU.bitwise_and))
            nc.vector.tensor_copy(row[:, :], src_i[:, :])
            ch.need(t)
            t = ch.did(nc.vector.tensor_copy(row_lo[:, :], tmp_i[:, :]))
            ch.need(t)
            t = ch.did(nc.vector.tensor_scalar(tmp_i[:, :], src_i[:, :], 7, None, ALU.arith_shift_right))
            ch.need(t)
            ch.did(nc.vector.tensor_copy(row_hi[:, :], tmp_i[:, :]))
            dve.wait_ge(const_ready, 1)
            ch.did(nc.vector.tensor_copy(iota[:, :], iota_i[:, :]))
            t = ch.did(nc.vector.tensor_copy(pid[:, :], pid_i[:, :]))
            ch.need(t)
            t = ch.did(nc.vector.tensor_scalar(npid[:, :], pid[:, :], -1.0, None, ALU.mult))
            ch.need(t)
            with dve.Fori(0, GN // 2) as it:
                for u in range(2):
                    g = it * 2 + u
                    dve.wait_ge(hist_ready, g + 1)
                    nc.vector.tensor_tensor(hot_lo[:, u], iota[:EP, :].unsqueeze(1).to_broadcast([EP, G, P]),
                                            row_lo[:, bass.ds(g * G, G)].unsqueeze(2).to_broadcast([EP, G, P]),
                                            ALU.is_equal)
                    nc.vector.tensor_tensor(hot_hi[:, u], iota[:EP, 0:NT].unsqueeze(1).to_broadcast([EP, G, NT]),
                                            row_hi[:, bass.ds(g * G, G)].unsqueeze(2).to_broadcast([EP, G, NT]),
                                            ALU.is_equal).then_inc(hot_ready, 1)
            dve.wait_ge(hist_free, GN + 2)
            for h in range(NT):
                last = ch.did(nc.vector.tensor_tensor_scan(before[:, 1:ET + 1, h], onescan[:, :], before[:, 1:ET + 1, h],
                                                           0.0, ALU.mult, ALU.add))
            ch.need(last)
            t = ch.did(nc.vector.tensor_copy(deg[:, :], before[:, ET, :]))
            ch.need(t)
            t = ch.did(nc.vector.tensor_scalar(over[:, :], deg[:, :], -1.0, 0.0, ALU.add, ALU.max))
            ch.need(t)
            t = ch.did(nc.vector.tensor_copy(over_i[:, :], over[:, :]))
            ch.need(t)
            t = ch.did(nc.vector.tensor_scalar(over_i[:, :], over_i[:, :], 5, None, ALU.arith_shift_right))
            ch.need(t)
            nc.vector.tensor_copy(over[:, :], over_i[:, :]).then_inc(over_ready, 1)
            dve.wait_ge(pre_ready, 1)
            t = ch.did(nc.vector.tensor_tensor_scan(hi_sum[:, :], onescan[:, 0:NT], over_ps[:, NT:2 * NT],
                                                    0.0, ALU.mult, ALU.add))
            ch.need(t)
            t = ch.did(nc.vector.tensor_tensor(over_at[:, :], hi_sum[:, :], over_ps[:, NT:2 * NT], ALU.subtract))
            ch.need(t)
            t = ch.did(nc.vector.scalar_tensor_tensor(out=over_at[:, :], in0=over_at[:, :], scalar=float(OV0 - 1),
                                                      in1=over_ps[:, 0:NT], op0=ALU.add, op1=ALU.add))
            ch.need(t)

        @block.tensor
        def _(pe):
            pe.sem_inc(hist_ready, 2)
            with pe.Fori(0, GN // 2) as it:
                for u in range(2):
                    g = it * 2 + u
                    hold(pe, hot_ready, g + 1, held["pe"])
                    hold(pe, hist_free, g + 1, held["pe"])
                    for j in range(G):
                        last = nc.tensor.matmul(hist[:, u, j * NT:(j + 1) * NT], hot_lo[:, u, j], hot_hi[:, u, j],
                                                start=True, stop=True)
                    last.then_inc(hist_ready, 1)
            pe.wait_ge(over_ready, 1)
            nc.tensor.matmul(over_ps[:, 0:NT], upper[:, :], over[:, :], start=True, stop=True)
            nc.tensor.matmul(over_ps[:, NT:2 * NT], ones[:, :], over[:, :], start=True, stop=True).then_inc(pre_ready, 1)

        @block.scalar
        def _(act):
            act.sem_inc(hist_free, 2)
            with act.Fori(0, GN // 2) as it:
                for u in range(2):
                    g = it * 2 + u
                    hold(act, hist_ready, g + 3, held["act"])
                    nc.scalar.copy(before[:, bass.ds(g * G + 1, G), :].rearrange("p t h -> p (t h)"),
                                   hist[:, u, 0:G * NT]).then_inc(hist_free, 1)

    record = sb("record", [EP, 2, SC, W], F32, ab)
    slot_i = sb("slot_i", [EP, 2, SC], I32, ab)
    cols = sb("cols", [EP, 2, C], F32, ab)
    col_f = sb("col_f", [EP, ET], F32, ab)
    col_lo = sb("col_lo", [EP, ET], F32, ab)
    col_hi = sb("col_hi", [EP, ET], F32, ab)
    hot_t = sb("hot_t", [P, C, P], F32, ab)
    away = sb("away", [P, C, P], F32, ab)
    junk = sb("junk", [EP, C, P], F32, ab)
    hi_mask = sb("hi_mask", [EP, C, NT], F32, ab)
    masked = sb("masked", [EP, C, 2, NT], F32, ab)
    within = sb("within", [EP, SC], F32, ab)
    found = sb("found", [EP, SC, 2], F32, ab)
    rank = sb("rank", [EP, SC], F32, ab)
    rank_i = sb("rank_i", [EP, SC], I32, ab)
    q_i = sb("q_i", [EP, SC], I32, ab)
    r_i = sb("r_i", [EP, SC], I32, ab)
    qf = sb("qf", [EP, SC], F32, ab)
    rf = sb("rf", [EP, SC], F32, ab)
    far = sb("far", [EP, SC], F32, ab)
    blk_i = sb("blk_i", [EP, SC], I32, ab)
    part_i = sb("part_i", [EP, 3, SC], I32, ab)
    part = sb("part", [EP, 3, SC], F32, ab)

    cols_ready, bc_ready, hot_t_ready, found_ready, lookup_free = [sem(n) for n in (
        "cols_ready", "bc_ready", "hot_t_ready", "found_ready", "lookup_free")]
    dve_b, act_b, rec_ready, bc_free, rec_free = sem("dve_b"), sem("act_b"), sem("rec_ready"), sem("bc_free"), sem("rec_free")
    sent = [sem("sent0"), sem("sent1")]
    with ExitStack() as pb:
        row_bc = ps("row_bc", [P, C, P], F32, pb)
        lo_bc = ps("lo_bc", [P, C, P], F32, pb)
        lookup = ps("lookup", [P, 512], F32, pb)
        block = pb.enter_context(nc.Block())

        @block.scalar
        def _(act):
            ch = Chain(act, act_b)
            with act.Fori(0, ET // C) as c:
                ch.turn(0, c, 1)
                hold(act, bc_ready, c + 1, held["act"])
                hold(act, bc_free, c + 1, held["act"])
                nc.scalar.copy(cols[:, 0, :], row[:, bass.ds(c * C, C)])
                nc.scalar.copy(cols[:, 1, :], row_lo[:, bass.ds(c * C, C)]).then_inc(cols_ready, 1)
                act.wait_ge(bc_ready, c + 2)
                t = ch.did(nc.scalar.activation(away[:, :, 0:EP], lo_bc[:, :, 0:EP], ACT.Abs, bias=npid[:, :]))
                ch.need(t)
                nc.scalar.activation(hot_t[:, :, 0:EP], away[:, :, 0:EP], ACT.Relu, scale=-1.0,
                                     bias=one[:, :]).then_inc(hot_t_ready, 1)
            ch.close(0, ET // C, 1)

        @block.tensor
        def _(pe):
            pe.sem_inc(bc_ready, 1)
            with pe.Fori(0, ET // C) as c:
                hold(pe, cols_ready, c + 1, held["pe"])
                hold(pe, bc_free, c + 1, held["pe"])
                for j in range(C):
                    nc.tensor.transpose(row_bc[:, j, 0:EP], cols[:, 0, j:j + 1].to_broadcast([EP, P]), ident[:EP, :EP])
                for j in range(C):
                    last = nc.tensor.transpose(lo_bc[:, j, 0:EP], cols[:, 1, j:j + 1].to_broadcast([EP, P]), ident[:EP, :EP])
                last.then_inc(bc_ready, 1)
                hold(pe, hot_t_ready, c + 1, held["pe"])
                hold(pe, lookup_free, c + 1, held["pe"])
                for j in range(C):
                    nc.tensor.matmul(lookup[:EP, j * 2 * NT:j * 2 * NT + NT], hot_t[:, j, 0:EP],
                                     before[:, bass.ds(c * C + j, 1), :].rearrange("p t h -> p (t h)"), start=True, stop=True)
                    last = nc.tensor.matmul(lookup[:EP, j * 2 * NT + NT:(j + 1) * 2 * NT], hot_t[:, j, 0:EP],
                                            over_at[:, :], start=True, stop=True)
                last.then_inc(found_ready, 1)

        @block.vector
        def _(dve):
            ch = Chain(dve, dve_b)
            dve.sem_inc(bc_free, 1)
            dve.sem_inc(lookup_free, 1)
            dve.wait_ge(dst_in, 16)
            dve.wait_ge(attr_in, 16)
            t = ch.did(nc.vector.tensor_scalar(tmp_i[:, :], dst_i[:, :], P - 1, None, ALU.bitwise_and))
            nc.vector.tensor_copy(col_f[:, :], dst_i[:, :])
            nc.vector.memset(record[:, :, :, VALID], 1.0)
            ch.need(t)
            t = ch.did(nc.vector.tensor_copy(col_lo[:, :], tmp_i[:, :]))
            ch.need(t)
            t = ch.did(nc.vector.tensor_scalar(tmp_i[:, :], dst_i[:, :], 7, None, ALU.arith_shift_right))
            ch.need(t)
            t = ch.did(nc.vector.tensor_copy(col_hi[:, :], tmp_i[:, :]))
            ch.need(t)
            start = ch.n
            per = 2 * (CN * 2 + 18)
            with dve.Fori(0, SN // 2) as it:
                ch.turn(start, it, per)
                for u in range(2):
                    s = it * 2 + u
                    for cc in range(CN):
                        c = s * CN + cc
                        js = slice(cc * C, (cc + 1) * C)
                        ch.did(nc.vector.tensor_tensor(hi_mask[:, :, :], iota[:EP, 0:NT].unsqueeze(1).to_broadcast([EP, C, NT]),
                                                       row_hi[:, bass.ds(c * C, C)].unsqueeze(2).to_broadcast([EP, C, NT]),
                                                       ALU.is_equal))
                        dve.wait_ge(bc_ready, c + 2)
                        for j in range(C):
                            last = nc.vector.scalar_tensor_tensor(
                                out=junk[:, j, 0:EP], in0=row_bc[:EP, j, 0:EP], scalar=cols[:, 0, j:j + 1],
                                in1=lower[:EP, 0:EP], op0=ALU.is_equal, op1=ALU.mult,
                                accum_out=within[:, cc * C + j:cc * C + j + 1])
                        hm = bc_free, c + 2
                        last.then_inc(bc_free, 1)
                        dve.wait_ge(found_ready, c + 1)
                        ch.need(hm)
                        nc.vector.tensor_tensor(
                            masked[:, :, :, :], lookup[:EP, 0:C * 2 * NT].rearrange("p (c w h) -> p c w h", c=C, w=2),
                            hi_mask[:, :, :].unsqueeze(2).to_broadcast([EP, C, 2, NT]), ALU.mult).then_inc(lookup_free, 1)
                        ch.need((lookup_free, c + 2))
                        t = ch.did(nc.vector.tensor_reduce(found[:, js, :], masked[:, :, :, :], AX.X, ALU.add))
                    e = bass.ds(s * SC, SC)
                    ch.need(t)
                    t = ch.did(nc.vector.tensor_tensor(rank[:, :], found[:, :, 0], within[:, :], ALU.add))
                    ch.need(t)
                    t = ch.did(nc.vector.tensor_copy(rank_i[:, :], rank[:, :]))
                    ch.need(t)
                    tq = ch.did(nc.vector.tensor_scalar(q_i[:, :], rank_i[:, :], 5, None, ALU.arith_shift_right))
                    tr = ch.did(nc.vector.tensor_scalar(r_i[:, :], rank_i[:, :], Q - 1, None, ALU.bitwise_and))
                    ch.need(tq)
                    tq = ch.did(nc.vector.tensor_copy(qf[:, :], q_i[:, :]))
                    ch.need(tr)
                    ch.did(nc.vector.tensor_copy(rf[:, :], r_i[:, :]))
                    ch.need(tq)
                    t = ch.did(nc.vector.tensor_tensor(far[:, :], found[:, :, 1], qf[:, :], ALU.add))
                    ch.need(t)
                    t = ch.did(nc.vector.tensor_tensor(far[:, :], far[:, :], row[:, e], ALU.subtract))
                    ch.need(t)
                    t = ch.did(nc.vector.scalar_tensor_tensor(out=far[:, :], in0=qf[:, :], scalar=1.0, in1=far[:, :],
                                                              op0=ALU.min, op1=ALU.mult))
                    ch.need(t)
                    t = ch.did(nc.vector.tensor_tensor(blk_i[:, :], far[:, :], row[:, e], ALU.add))
                    ch.need(t)
                    ch.did(nc.vector.tensor_scalar(part_i[:, 0, :], blk_i[:, :], 5, 3, ALU.arith_shift_right, ALU.bitwise_and))
                    ch.did(nc.vector.tensor_scalar(part_i[:, 1, :], blk_i[:, :], 7, None, ALU.arith_shift_right))
                    t = ch.did(nc.vector.tensor_scalar(part_i[:, 2, :], blk_i[:, :], 31, None, ALU.bitwise_and))
                    ch.need(t)
                    t = ch.did(nc.vector.tensor_copy(part[:, :, :], part_i[:, :, :]))
                    ch.need(t)
                    t = ch.did(nc.vector.scalar_tensor_tensor(out=part[:, 0, :], in0=part[:, 0, :], scalar=float(Q),
                                                              in1=rf[:, :], op0=ALU.mult, op1=ALU.add))
                    ch.need(t)
                    t = ch.did(nc.vector.scalar_tensor_tensor(out=part[:, 0, :], in0=part[:, 0, :], scalar=float(ST),
                                                              in1=part[:, 2, :], op0=ALU.mult, op1=ALU.add))
                    dve.wait_ge(rec_free, s + 1)
                    ch.need(t)
                    ch.did(nc.vector.scalar_tensor_tensor(out=slot_i[:, u, :], in0=part[:, 1, :], scalar=float(TPB),
                                                          in1=part[:, 0, :], op0=ALU.mult, op1=ALU.add))
                    ch.did(nc.vector.tensor_scalar(record[:, u, :, A0:A0 + D],
                                                   edge_attr[:, bass.ds(s * (SC * D), SC * D)].rearrange("p (t d) -> p t d", d=D),
                                                   float(KS - 1), None, ALU.mult))
                    for word, of in ((COL, col_f), (ROW, row), (CLO, col_lo), (CHI, col_hi)):
                        last = nc.vector.tensor_scalar(record[:, u, :, word], of[:, e], 1.0, None, ALU.mult)
                    last.then_inc(rec_ready, 1)
            ch.close(start, SN // 2, per)

        @block.gpsimd
        def _(pool):
            pool.sem_inc(rec_free, 2)
            with pool.Fori(0, SN // 2) as it:
                for u in range(2):
                    hold(pool, rec_ready, it * 2 + u + 1, held["pool"])
                    for j in range(SC):
                        pool.indirect_dma_start(slots, bass.IndirectOffsetOnAxis(ap=slot_i[:, u, j:j + 1], axis=0),
                                                record[:, u, j, :], None).then_inc(sent[u], 16)
                        if u == 1 and j == 4:
                            hold(pool, sent[0], (it + 1) * (16 * SC), held["pool"])
                            pool.sem_inc(rec_free, 1)
                hold(pool, sent[1], (it + 1) * (16 * SC), held["pool"])
                pool.sem_inc(rec_free, 1)




def hats(ch, at, shape, hat_consts, up, down, hat, valid):
    up_c, down_c, up_floor, down_floor = [c[:, :, :].unsqueeze(1).to_broadcast(shape) for c in hat_consts]
    wide = at.unsqueeze(3).to_broadcast(shape)
    v = ch.eng
    a = ch.did(v.tensor_tensor(up[:, :, :, :], wide, up_c, ALU.subtract))
    b = ch.did(v.tensor_tensor(down[:, :, :, :], down_c, wide, ALU.subtract))
    ch.need(a)
    ch.did(v.tensor_tensor(up[:, :, :, :], up[:, :, :, :], up_floor, ALU.max))
    ch.need(b)
    b = ch.did(v.tensor_tensor(down[:, :, :, :], down[:, :, :, :], down_floor, ALU.max))
    ch.need(b)
    a = ch.did(v.tensor_tensor(hat[:, :, :, :], up[:, :, :, :], down[:, :, :, :], ALU.min))
    ch.need(a)
    return ch.did(v.tensor_tensor(hat[:, :, 0, :], hat[:, :, 0, :], valid.unsqueeze(2).to_broadcast([P, TPB, KS]), ALU.mult))


HATS = 6


def first_layer(nc, sb, ps, sem, held, g):
    rec, slots, blocks = g["rec"], g["slots"], g["blocks"]
    PIECES = 5
    with ExitStack() as c:
        up, down = sb("up1", [P, TPB, D, KS], F32, c), sb("down1", [P, TPB, D, KS], F32, c)
        hat = sb("hat1", [P, TPB, D, KS], F32, c)
        hat01 = sb("hat01_1", [P, 2, TPB, KS * KS], F32, c)
        hat2 = sb("hat2_1", [P, 2, TPB, P // Q, KS], F32, c)
        sums = sb("sums", [KS * KS, P // Q, TPB, KS], F32, c)
        sum_ps = ps("sum_ps", [P, 2, 512], F32, c)
        row_ps = ps("row_ps", [P, 512], F32, c)
        rec_in, small_in, const_done, w_in = sem("rec_in"), sem("small_in"), sem("const_done"), sem("w_in")
        hats_ready, sum_ready, sums_copied, row_ready, dve_c = [sem(n) for n in (
            "hats_ready", "sum_ready", "sums_copied", "row_ready", "dve_c")]
        block = c.enter_context(nc.Block())

        @block.sync
        def _(sp):
            s = slots.rearrange("(p t) c -> p t c", p=P)
            sp.dma_start(g["wt1"][:, :], g["w1"].rearrange("(a b) i f -> a (b i f)", b=KS)).then_inc(w_in, 16)
            step = ST // PIECES
            for i in range(PIECES):
                sp.dma_start(rec[:, i * step:(i + 1) * step, :], s[:, i * step:(i + 1) * step, :]).then_inc(rec_in, 16)
            for q in range(P // Q):
                sp.dma_start(g["ovn"][q * Q:(q + 1) * Q, :],
                             s[q * Q, ST // 2:ST, ROW].rearrange("(b j) -> j b", j=TPB),
                             allow_slow_non_contiguous=True).then_inc(small_in, 16)
            sp.dma_start(g["wt2"][:, :], g["w2"].rearrange("k i o -> k (i o)")).then_inc(small_in, 16)
            sp.dma_start(g["wtc"][:, :], g["wc"].rearrange("k i o -> k (i o)")).then_inc(small_in, 16)
            sp.dma_start(g["wt3"][:, :], g["w3"]).then_inc(small_in, 16)
            sp.dma_start(g["wt4"][:, :], g["w4"]).then_inc(small_in, 16)
            sp.dma_start(g["bt3"][:, :], g["b3"].unsqueeze(1)).then_inc(small_in, 16)
            for to, of, n in (("bt1", "b1", FH), ("bt2", "b2", FH), ("btc", "bc", FIN), ("bt4", "b4", D)):
                sp.dma_start(g[to][:, :], g[of].unsqueeze(0).to_broadcast([P, n])).then_inc(small_in, 16)
            sp.wait_ge(const_done, 1)
            full = N // P
            sp.dma_start(g["x_nodes"][:, 0:full, :], g["x"][0:full * P, :].rearrange("(t p) f -> p t f", p=P)).then_inc(small_in, 16)
            sp.dma_start(g["x_nodes"][0:N - full * P, full, :], g["x"][full * P:N, :]).then_inc(small_in, 16)
            sp.wait_ge(small_in, 16 * 15)

        @block.vector
        def _(dve):
            nc.vector.memset(g["x_nodes"][:, :, :], 0.0).then_inc(const_done, 1)
            ch = Chain(nc.vector, dve_c)
            t = ch.did(nc.vector.tensor_scalar(g["inv_degree"][:, :], g["deg"][:, :], 1.0, None, ALU.max))
            ch.need(t)
            ch.did(nc.vector.reciprocal(g["inv_degree"][:, :], g["inv_degree"][:, :]))
            nc.vector.memset(g["of_block"][:, :], 0.0)
            for j in range(KS):
                nc.vector.memset(g["up_c"][:, :, j], float(j - 1))
                nc.vector.memset(g["down_c"][:, :, j], float(j + 1))
                nc.vector.memset(g["up_floor"][:, :, j], BIG if j == 0 else -BIG if j == 1 else 0.0)
                t = ch.did(nc.vector.memset(g["down_floor"][:, :, j], BIG if j == KS - 1 else -BIG if j == KS - 2 else 0.0))
            ch.need(t)
            for q in range(P // Q):
                t = ch.did(nc.vector.memset(g["of_block"][q * Q:(q + 1) * Q, q:q + 1], 1.0))
            dve.wait_ge(rec_in, 16 * PIECES)
            ch.need(t)
            start, per = ch.n, 2 * HATS
            with dve.Fori(0, BT // 2) as it:
                ch.turn(start, it, per)
                for u in range(2):
                    c = it * 2 + u
                    e = bass.ds(c * TPB, TPB)
                    t = hats(ch, rec[:, e, A0:A0 + D], [P, TPB, D, KS], g["hat_consts"], up, down, hat, rec[:, e, VALID])
                    dve.wait_ge(sum_ready, c + 1)
                    nc.vector.tensor_tensor(hat2[:, u], hat[:, :, 2, :].unsqueeze(2).to_broadcast([P, TPB, P // Q, KS]),
                                            g["of_block"][:, :].unsqueeze(1).unsqueeze(3).to_broadcast([P, TPB, P // Q, KS]),
                                            ALU.mult)
                    ch.need(t)
                    nc.vector.tensor_tensor(hat01[:, u].rearrange("p t (a b) -> p t a b", a=KS),
                                            hat[:, :, 0, :].unsqueeze(3).to_broadcast([P, TPB, KS, KS]),
                                            hat[:, :, 1, :].unsqueeze(2).to_broadcast([P, TPB, KS, KS]),
                                            ALU.mult).then_inc(hats_ready, 1)
            ch.close(start, BT // 2, per)
            dve.wait_ge(small_in, 16 * 15)
            t = ch.did(nc.vector.tensor_copy(g["ovn_i"][:, :], g["ovn"][:, :]))
            ch.need(t)
            t = ch.did(nc.vector.tensor_scalar(g["ov_i"][:, :], g["ovn_i"][:, :], P - 1, None, ALU.bitwise_and))
            ch.need(t)
            t = ch.did(nc.vector.tensor_copy(g["ov_lo"][:, :], g["ov_i"][:, :]))
            ch.need(t)
            t = ch.did(nc.vector.tensor_scalar(g["ov_i"][:, :], g["ovn_i"][:, :], 7, None, ALU.arith_shift_right))
            ch.need(t)
            ch.did(nc.vector.tensor_copy(g["ov_hi"][:, :], g["ov_i"][:, :]))

        @block.tensor
        def _(pe):
            pe.sem_inc(sum_ready, 2)
            pe.wait_ge(w_in, 16)
            with pe.Fori(0, BT // 2) as it:
                for u in range(2):
                    c = it * 2 + u
                    hold(pe, hats_ready, c + 1, held["pe"])
                    for j in range(TPB):
                        h, jj = divmod(j, TPB // 2)
                        last = nc.tensor.matmul(sum_ps[0:KS * KS, h, jj * 20:(jj + 1) * 20], hat01[:, u, j, :],
                                                hat2[:, u, j].rearrange("p q k -> p (q k)"), start=True, stop=True)
                    last.then_inc(sum_ready, 1)
                    hold(pe, sums_copied, c * 2 + 1, held["pe"])
                    for k in range(KS):
                        last = nc.tensor.matmul(row_ps[:, 0:FH], sums[:, :, :, k].rearrange("p q t -> p (q t)"),
                                                g["wt1"][:, k * FH:(k + 1) * FH], start=(k == 0), stop=(k == KS - 1))
                    last.then_inc(row_ready, 1)

        @block.scalar
        def _(act):
            with act.Fori(0, BT) as c:
                act.wait_ge(sum_ready, c + 3)
                nc.scalar.copy(sums[:, :, 0:TPB // 2, :].rearrange("p q t k -> p t q k"),
                               sum_ps[0:KS * KS, 0, 0:320].rearrange("p (t q k) -> p t q k", q=P // Q, k=KS))
                nc.scalar.copy(sums[:, :, TPB // 2:TPB, :].rearrange("p q t k -> p t q k"),
                               sum_ps[0:KS * KS, 1, 0:320].rearrange("p (t q k) -> p t q k", q=P // Q, k=KS)).then_inc(sums_copied, 1)
                hold(act, row_ready, c + 1, held["act"])
                nc.scalar.copy(blocks[:, bass.ds(c, 1), :].rearrange("p t f -> p (t f)"), row_ps[:, 0:FH]).then_inc(sums_copied, 1)


def gather_overflow(nc, sb, ps, sem, held, iota, blocks, ov_lo, ov_hi, inv_degree, bias, F, hid, name, x_nodes=None, out=None):
    with ExitStack() as c:
        hot = sb("ov_hot_" + name, [P, NT, P], F32, c)
        mask = sb("ov_mask_" + name, [P, NT, NT], F32, c)
        spread = sb("ov_spread_" + name, [P, 2, NT, F], F32, c)
        node = sb("node_" + name, [P, NT, F], F32, c)
        pos = sb("node_pos_" + name, [P, NT, F], F32, c)
        neg = sb("node_neg_" + name, [P, NT, F], F32, c)
        stat = sb("stat_" + name, [P, 3, NT], F32, c)
        eps = sb("eps_" + name, [P, 1], F32, c)
        add_ps = ps("add_ps_" + name, [P, 4 * 512], F32, c)
        s_spread, s_added, s_dve, s_neg, s_exp, s_out = [sem(n + name) for n in (
            "spread_ready_", "added_", "dve_g_", "neg_ready_", "exp_ready_", "out_stored_")]
        per_bank = 512 // F
        final = []
        banks = [(h, min(h + per_bank, NT)) for h in range(0, NT, per_bank)]
        block = c.enter_context(nc.Block())

        @block.vector
        def _(dve):
            ch = Chain(nc.vector, s_dve)
            nc.vector.memset(eps[:, :], 1e-5)
            ch.did(nc.vector.tensor_tensor(hot[:, :, :], iota[:, :].unsqueeze(1).to_broadcast([P, NT, P]),
                                           ov_lo[:, :].unsqueeze(2).to_broadcast([P, NT, P]), ALU.is_equal))
            t = ch.did(nc.vector.tensor_tensor(mask[:, :, :], iota[:, 0:NT].unsqueeze(1).to_broadcast([P, NT, NT]),
                                               ov_hi[:, :].unsqueeze(2).to_broadcast([P, NT, NT]), ALU.is_equal))
            ch.need(t)
            for o in range(NT):
                if o >= 2:
                    dve.wait_ge(s_added, o - 1)
                nc.vector.tensor_tensor(spread[:, o % 2], blocks[:, NT + o, 0:F].unsqueeze(1).to_broadcast([P, NT, F]),
                                        mask[:, o, :].unsqueeze(2).to_broadcast([P, NT, F]), ALU.mult).then_inc(s_spread, 1)
            dve.wait_ge(s_added, NT)
            t = ch.did(nc.vector.tensor_tensor(node[:, :, :], blocks[:, 0:NT, 0:F],
                                               add_ps[:, 0:NT * F].rearrange("p (t f) -> p t f", f=F), ALU.add))
            ch.need(t)
            t = ch.did(nc.vector.tensor_tensor(node[:, :, :], node[:, :, :], inv_degree[:, :].unsqueeze(2).to_broadcast([P, NT, F]), ALU.mult))
            ch.need(t)
            t = ch.did(nc.vector.tensor_tensor(node[:, :, :], node[:, :, :], bias[:, :].unsqueeze(1).to_broadcast([P, NT, F]), ALU.add))
            ch.need(t)
            if out is None:
                nc.vector.tensor_scalar(neg[:, :, :], node[:, :, :], 0.0, None, ALU.min).then_inc(s_neg, 1)
                t = ch.did(nc.vector.tensor_scalar(pos[:, :, :], node[:, :, :], 0.0, None, ALU.max))
                dve.wait_ge(s_exp, 1)
                ch.need(t)
                ch.did(nc.vector.scalar_tensor_tensor(out=hid[:, :, :], in0=neg[:, :, :], scalar=-1.0, in1=pos[:, :, :],
                                                      op0=ALU.add, op1=ALU.add))
                return
            t = ch.did(nc.vector.tensor_tensor(node[:, :, :], node[:, :, :], x_nodes[:, :, :], ALU.add))
            ch.need(t)
            t = ch.did(nc.vector.tensor_reduce(stat[:, 0, :], node[:, :, :], AX.X, ALU.add))
            ch.need(t)
            t = ch.did(nc.vector.tensor_scalar(stat[:, 0, :], stat[:, 0, :], 1.0 / F, None, ALU.mult))
            ch.need(t)
            t = ch.did(nc.vector.tensor_tensor(node[:, :, :], node[:, :, :], stat[:, 0, :].unsqueeze(2).to_broadcast([P, NT, F]), ALU.subtract))
            ch.need(t)
            t = ch.did(nc.vector.tensor_tensor(pos[:, :, :], node[:, :, :], node[:, :, :], ALU.mult))
            ch.need(t)
            t = ch.did(nc.vector.tensor_reduce(stat[:, 1, :], pos[:, :, :], AX.X, ALU.add))
            ch.need(t)
            nc.vector.tensor_scalar(stat[:, 1, :], stat[:, 1, :], 1.0 / F, 1e-5, ALU.mult, ALU.add).then_inc(s_neg, 1)
            dve.wait_ge(s_exp, 1)
            t = ch.did(nc.vector.reciprocal(stat[:, 2, :], stat[:, 2, :]))
            ch.need(t)
            ch.did(nc.vector.tensor_tensor(neg[:, :, :], node[:, :, :], stat[:, 2, :].unsqueeze(2).to_broadcast([P, NT, F]), ALU.mult))
            final.append(ch.now())

        @block.tensor
        def _(pe):
            for o in range(NT):
                pe.wait_ge(s_spread, o + 1)
                for b0, b1 in banks:
                    last = nc.tensor.matmul(add_ps[:, b0 * F:b1 * F], hot[:, o, :],
                                            spread[:, o % 2, b0:b1, :].rearrange("p t f -> p (t f)"),
                                            start=(o == 0), stop=(o == NT - 1))
                last.then_inc(s_added, 1)

        @block.scalar
        def _(act):
            act.wait_ge(s_neg, 1)
            if out is None:
                nc.scalar.activation(neg[:, :, :], neg[:, :, :], ACT.Exp).then_inc(s_exp, 1)
            else:
                nc.scalar.activation(stat[:, 2, :], stat[:, 1, :], ACT.Sqrt).then_inc(s_exp, 1)

        if out is not None:
            @block.sync
            def _(sp):
                sp.wait_ge(s_dve, final[0])
                full = N // P
                sp.dma_start(out[0:full * P, :].rearrange("(t p) f -> p t f", p=P), neg[:, 0:full, :]).then_inc(s_out, 16)
                sp.dma_start(out[full * P:N, :], neg[0:N - full * P, full, :]).then_inc(s_out, 16)
                sp.wait_ge(s_out, 32)


def to_table(nc, sem, hid, x_nodes, table):
    stored = sem("table_stored")
    t = table.rearrange("(t p) f -> p t f", p=P)
    with nc.Block() as block:
        @block.sync
        def _(sp):
            sp.dma_start(t[:, :, 0:FH], hid[:, :, :]).then_inc(stored, 16)
            sp.dma_start(t[:, :, FH:HX], x_nodes[:, :, :]).then_inc(stored, 16)
            sp.wait_ge(stored, 32)


def conv(nc, sb, ps, sem, held, name, F, rec, moved, hat_consts, blocks, wt, table, x_slots):
    TS = 512 // F
    NS = TPB // TS
    with ExitStack() as c:
        up, down = sb("up" + name, [P, TPB, D, KS], F32, c), sb("down" + name, [P, TPB, D, KS], F32, c)
        hat = sb("hat" + name, [P, TPB, D, KS], F32, c)
        hat01 = sb("hat01" + name, [P, TPB, KS * KS], F32, c)
        basis = sb("basis" + name, [P, 2, TS, K], F32, c)
        wide = HX if table is not None else F
        feat = sb("feat" + name, [P, 2, TPB, wide], F32, c)
        agg = sb("agg" + name, [K, P // Q, TPB, F], F32, c)
        agg_ps = ps("agg_ps" + name, [P, P // Q, 512], F32, c)
        row_ps = ps("row_ps" + name, [P, 512], F32, c)
        b_ready, sub_ready, act_copied, dve_copied, row_ready, s_dve = [sem(n + name) for n in (
            "basis_ready_", "sub_ready_", "act_copied_", "dve_copied_", "row_ready_", "dve_h_")]
        came = [sem("came0_" + name), sem("came1_" + name)]
        if table is not None:
            index = sb("index", [P, 2, TPB], I32, c)
            x_part = sb("x_part", [P, 2, TPB, FIN], F32, c)
            x_ready, x_free, x_stored, index_ready = [sem(n) for n in ("x_ready", "x_free", "x_stored", "index_ready")]
        block = c.enter_context(nc.Block())

        @block.vector
        def _(dve):
            ch = Chain(nc.vector, s_dve)
            dve.sem_inc(dve_copied, 1)
            per = 2 * (HATS + 1)

            def sub_basis(c, s):
                g = c * NS + s
                dve.wait_ge(sub_ready, g + 1)
                nc.vector.tensor_tensor(basis[:, s % 2].rearrange("p t (a b) -> p t a b", b=KS),
                                        hat01[:, s * TS:(s + 1) * TS, :].unsqueeze(3).to_broadcast([P, TS, KS * KS, KS]),
                                        hat[:, s * TS:(s + 1) * TS, 2, :].unsqueeze(2).to_broadcast([P, TS, KS * KS, KS]),
                                        ALU.mult).then_inc(b_ready, 1)

            with dve.Fori(0, BT // 2) as it:
                ch.turn(0, it, per)
                for u in range(2):
                    c = it * 2 + u
                    e = bass.ds(c * TPB, TPB)
                    at = rec[:, e, A0:A0 + D] if moved is None else moved[:, e, :]
                    t = hats(ch, at, [P, TPB, D, KS], hat_consts, up, down, hat, rec[:, e, VALID])
                    ch.need(t)
                    t = ch.did(nc.vector.tensor_tensor(hat01[:, :, :].rearrange("p t (a b) -> p t a b", a=KS),
                                                       hat[:, :, 0, :].unsqueeze(3).to_broadcast([P, TPB, KS, KS]),
                                                       hat[:, :, 1, :].unsqueeze(2).to_broadcast([P, TPB, KS, KS]),
                                                       ALU.mult))
                    ch.need(t)
                    sub_basis(c, 0)
                    for s in range(NS):
                        if s + 1 < NS:
                            sub_basis(c, s + 1)
                        dve.wait_ge(sub_ready, c * NS + s + 3)
                        nc.vector.tensor_copy(agg[:, 2:4, s * TS:(s + 1) * TS, :].rearrange("p q t f -> p q (t f)"),
                                              agg_ps[:K, 2:4, :]).then_inc(dve_copied, 1)
            ch.close(0, BT // 2, per)

        @block.scalar
        def _(act):
            act.sem_inc(act_copied, 1)
            with act.Fori(0, BT // 2) as it:
                for u in range(2):
                    c = it * 2 + u
                    if table is not None:
                        act.wait_ge(came[u], (it + 1) * (16 * TPB))
                        hold(act, x_free, c + 1, held["act"])
                        nc.scalar.copy(x_part[:, u], feat[:, u, :, FH:HX]).then_inc(x_ready, 1)
                    for s in range(NS):
                        act.wait_ge(sub_ready, c * NS + s + 3)
                        nc.scalar.copy(agg[:, 0:2, s * TS:(s + 1) * TS, :].rearrange("p q t f -> p q (t f)"),
                                       agg_ps[:K, 0:2, :]).then_inc(act_copied, 1)
                    hold(act, row_ready, c + 3, held["act"])
                    nc.scalar.copy(blocks[:, bass.ds(c, 1), 0:F].rearrange("p t f -> p (t f)"), row_ps[:, 0:F])

        @block.tensor
        def _(pe):
            pe.sem_inc(sub_ready, 2)
            pe.sem_inc(row_ready, 2)
            with pe.Fori(0, BT // 2) as it:
                for u in range(2):
                    c = it * 2 + u
                    hold(pe, came[u], (it + 1) * (16 * (TPB if table is not None else 1)), held["pe"])
                    for s in range(NS):
                        g = c * NS + s
                        hold(pe, b_ready, g + 1, held["pe"])
                        hold(pe, act_copied, g + 1, held["pe"])
                        hold(pe, dve_copied, g + 1, held["pe"])
                        for j in range(TS):
                            for q in range(P // Q):
                                last = nc.tensor.matmul(agg_ps[:K, q, j * F:(j + 1) * F], basis[q * Q:(q + 1) * Q, s % 2, j, :],
                                                        feat[q * Q:(q + 1) * Q, u, s * TS + j, 0:F], start=True, stop=True)
                        last.then_inc(sub_ready, 1)
                    hold(pe, act_copied, c * NS + NS + 1, held["pe"])
                    hold(pe, dve_copied, c * NS + NS + 1, held["pe"])
                    rows = agg[:, :, :, :].rearrange("p q t f -> p (q t) f")
                    for f in range(F):
                        last = nc.tensor.matmul(row_ps[:, 0:F], rows[:, :, f], wt[:, f * F:(f + 1) * F],
                                                start=(f == 0), stop=(f == F - 1))
                    last.then_inc(row_ready, 1)

        if table is not None:
            @block.gpsimd
            def _(pool):
                with pool.Fori(0, BT // 2) as it:
                    for u in range(2):
                        c = it * 2 + u
                        hold(pool, row_ready, c + 1, held["pool"])
                        nc.gpsimd.tensor_copy(index[:, u, :], rec[:, bass.ds(c * TPB, TPB), COL]).then_inc(index_ready, 1)
                        hold(pool, index_ready, c + 1, held["pool"])
                        for j in range(TPB):
                            pool.indirect_dma_start(feat[:, u, j, :], None, table,
                                                    bass.IndirectOffsetOnAxis(ap=index[:, u, j:j + 1], axis=0)).then_inc(came[u], 16)

            @block.sync
            def _(sp):
                sp.sem_inc(x_free, 2)
                with sp.Fori(0, BT // 2) as it:
                    for u in range(2):
                        c = it * 2 + u
                        hold(sp, x_ready, c + 1, held["sp"])
                        sp.dma_start(x_slots[:, bass.ds(c * (TPB * FIN), TPB * FIN)],
                                     x_part[:, u].rearrange("p t f -> p (t f)")).then_inc(x_stored, 16)
                        hold(sp, x_stored, c * 16 + 16, held["sp"])
                        sp.sem_inc(x_free, 1)
        else:
            @block.sync
            def _(sp):
                with sp.Fori(0, BT // 2) as it:
                    for u in range(2):
                        c = it * 2 + u
                        hold(sp, row_ready, c + 1, held["sp"])
                        sp.dma_start(feat[:, u].rearrange("p t f -> p (t f)"),
                                     x_slots[:, bass.ds(c * (TPB * FIN), TPB * FIN)]).then_inc(came[u], 16)


def t_node(nc, sb, ps, sem, held, hid, wt3, bt3, wt4, bt4, ident, ovn_i, t_nodes, t_blocks, rec, moved, iota, npid, one):
    with ExitStack() as cc:
        t_sb = sb("t_sb", [P, BT, D], F32, cc)
        with ExitStack() as c:
            hid_t = sb("hid_t", [FH, NT * P], F32, c)
            pos, neg, act3 = [sb(n, [FH, NT * P], F32, c) for n in ("t_pos", "t_neg", "act3")]
            tr_ps = ps("tr_ps", [P, 2, 512], F32, c)
            w3_ps = ps("w3_ps", [P, 2, 512], F32, c)
            w4_ps = ps("w4_ps", [P, 512], F32, c)
            s_tr, s_trc, s_w3, s_neg, s_exp, s_act3, s_w4, s_dve, s_tsb, s_st, s_st2, s_ov = [sem("t_" + n) for n in (
                "transposed", "transposed_copied", "w3_ready", "neg_ready", "exp_ready", "act3_ready", "w4_ready", "dve", "sb", "stored", "stored2", "overflow_in")]
            GR = [(i, min(i + 4, NT)) for i in range(0, NT, 4)]
            block = c.enter_context(nc.Block())

            @block.tensor
            def _(pe):
                for i, (a, b) in enumerate(GR):
                    if i >= 2:
                        pe.wait_ge(s_trc, i - 1)
                    for n in range(a, b):
                        last = nc.tensor.transpose(tr_ps[0:FH, i % 2, (n - a) * P:(n - a + 1) * P], hid[:, n, :], ident[:, :])
                    last.then_inc(s_tr, 1)
                for i, (a, b) in enumerate(GR):
                    pe.wait_ge(s_trc, i + 1)
                    if i >= 2:
                        pe.wait_ge(s_neg, i - 1)
                    nc.tensor.matmul(w3_ps[0:FH, i % 2, 0:(b - a) * P], wt3[:, :], hid_t[:, a * P:b * P],
                                     start=True, stop=True).then_inc(s_w3, 1)
                pe.wait_ge(s_act3, len(GR))
                for n in range(NT):
                    last = nc.tensor.matmul(w4_ps[:, n * D:(n + 1) * D], act3[:, n * P:(n + 1) * P], wt4[:, :], start=True, stop=True)
                last.then_inc(s_w4, 1)

            @block.scalar
            def _(act):
                for i, (a, b) in enumerate(GR):
                    act.wait_ge(s_tr, i + 1)
                    nc.scalar.copy(hid_t[:, a * P:b * P], tr_ps[0:FH, i % 2, 0:(b - a) * P]).then_inc(s_trc, 1)
                for i, (a, b) in enumerate(GR):
                    act.wait_ge(s_neg, i + 1)
                    nc.scalar.activation(neg[:, a * P:b * P], neg[:, a * P:b * P], ACT.Exp).then_inc(s_exp, 1)

            @block.vector
            def _(dve):
                for i, (a, b) in enumerate(GR):
                    dve.wait_ge(s_w3, i + 1)
                    y = w3_ps[0:FH, i % 2, 0:(b - a) * P]
                    nc.vector.tensor_scalar(pos[:, a * P:b * P], y, bt3[:, :], 0.0, ALU.add, ALU.max)
                    nc.vector.tensor_scalar(neg[:, a * P:b * P], y, bt3[:, :], 0.0, ALU.add, ALU.min).then_inc(s_neg, 1)
                for i, (a, b) in enumerate(GR):
                    dve.wait_ge(s_exp, i + 1)
                    nc.vector.scalar_tensor_tensor(out=act3[:, a * P:b * P], in0=neg[:, a * P:b * P], scalar=-1.0,
                                                   in1=pos[:, a * P:b * P], op0=ALU.add, op1=ALU.add).then_inc(s_act3, 1)
                dve.wait_ge(s_w4, 1)
                nc.vector.tensor_tensor(t_sb[:, 0:NT, :], w4_ps[:, 0:NT * D].rearrange("p (t d) -> p t d", d=D),
                                        bt4[:, :].unsqueeze(1).to_broadcast([P, NT, D]), ALU.add).then_inc(s_tsb, 1)

            @block.sync
            def _(sp):
                sp.wait_ge(s_tsb, 1)
                sp.dma_start(t_nodes.rearrange("(t p) d -> p t d", p=P), t_sb[:, 0:NT, :]).then_inc(s_st, 16)
                sp.wait_ge(s_ov, 16 * NT)
                sp.dma_start(t_blocks, t_sb[:, :, :].rearrange("p t d -> p (t d)")).then_inc(s_st2, 16)
                sp.wait_ge(s_st2, 16)

            @block.gpsimd
            def _(pool):
                pool.wait_ge(s_st, 16)
                for o in range(NT):
                    pool.indirect_dma_start(t_sb[:, NT + o, :], None, t_nodes,
                                            bass.IndirectOffsetOnAxis(ap=ovn_i[:, o:o + 1], axis=0)).then_inc(s_ov, 16)
                pool.wait_ge(s_ov, 16 * NT)

        with ExitStack() as c:
            C = 8
            G = ST // C
            t_quad = sb("t_quad", [P // Q, ST * D], F32, c)
            expand = sb("expand", [P // Q, P], F32, c)
            low = sb("low", [P, 2, C], F32, c)
            hi_mask = sb("hi_mask3", [P, 2, C, NT], F32, c)
            away = sb("away3", [P, 2, C, P], F32, c)
            hot = sb("hot3", [P, 2, C, P], F32, c)
            masked = sb("masked3", [P, C, NT, D], F32, c)
            low_ready, bc_ready, hot_ready, got_ready, masked_ready, s_act, s_dve, s_pool, s_quad, s_exp, s_red = [sem("e_" + n) for n in (
                "low_ready", "bc_ready", "hot_ready", "got_ready", "masked_ready", "act", "dve", "pool", "quad_in", "expanded", "reduced")]
            with ExitStack() as pc:
                lo_bc = ps("lo_bc3", [P, 2, C, P], F32, pc)
                got = ps("got", [P, 2, C, P], F32, pc)
                block = pc.enter_context(nc.Block())

                @block.sync
                def _(sp):
                    for q in range(P // Q):
                        sp.dma_start(t_quad[q:q + 1, :].rearrange("o (b j d) -> o b j d", b=BT, d=D),
                                     t_blocks[q * Q:(q + 1) * Q, :].rearrange("j (b d) -> b j d", d=D).unsqueeze(0)).then_inc(s_quad, 16)
                    sp.wait_ge(s_quad, 64)

                @block.gpsimd
                def _(pool):
                    ch = Chain(nc.gpsimd, s_pool)
                    t = ch.did(nc.gpsimd.memset(expand[:, :], 1.0))
                    ch.need(t)
                    t = ch.did(nc.gpsimd.affine_select(out=expand[:, :], in_=expand[:, :], compare_op=ALU.is_ge, fill=0.0,
                                                       base=0, pattern=[[1, P]], channel_multiplier=-Q))
                    ch.need(t)
                    ch.did(nc.gpsimd.affine_select(out=expand[:, :], in_=expand[:, :], compare_op=ALU.is_ge, fill=0.0,
                                                   base=Q - 1, pattern=[[-1, P]], channel_multiplier=Q))
                    with pool.Fori(0, G // 2) as it:
                        for u in range(2):
                            g = it * 2 + u
                            hold(pool, bc_ready, g + 1, held["pool"])
                            nc.gpsimd.tensor_copy(low[:, u, :], rec[:, bass.ds(g * C, C), CLO]).then_inc(low_ready, 1)

                @block.tensor
                def _(pe):
                    pe.sem_inc(bc_ready, 2)

                    def turn_low(g, u):
                        hold(pe, low_ready, g + 1, held["pe"])
                        hold(pe, hot_ready, g + 1, held["pe"])
                        for j in range(C):
                            last = nc.tensor.transpose(lo_bc[:, u, j, :], low[:, u, j:j + 1].to_broadcast([P, P]), ident[:, :])
                        last.then_inc(bc_ready, 1)

                    def fetch(g, u):
                        hold(pe, hot_ready, g + 3, held["pe"])
                        hold(pe, masked_ready, g + 1, held["pe"])
                        for j in range(C):
                            last = nc.tensor.matmul(got[:, u, j, 0:NT * D], hot[:, u, j, :],
                                                    t_sb[:, 0:NT, :].rearrange("p t d -> p (t d)"), start=True, stop=True)
                        last.then_inc(got_ready, 1)

                    turn_low(0, 0)
                    with pe.Fori(0, G // 2 - 1) as it:
                        turn_low(it * 2 + 1, 1)
                        fetch(it * 2, 0)
                        turn_low(it * 2 + 2, 0)
                        fetch(it * 2 + 1, 1)
                    turn_low(G - 1, 1)
                    fetch(G - 2, 0)
                    fetch(G - 1, 1)

                @block.scalar
                def _(act):
                    act.sem_inc(hot_ready, 2)
                    ch = Chain(nc.scalar, s_act)
                    with act.Fori(0, G // 2) as it:
                        ch.turn(0, it, 2)
                        for u in range(2):
                            g = it * 2 + u
                            act.wait_ge(bc_ready, g + 3)
                            t = ch.did(nc.scalar.activation(away[:, u], lo_bc[:, u], ACT.Abs, bias=npid[:, :]))
                            act.wait_ge(got_ready, g + 1)
                            ch.need(t)
                            nc.scalar.activation(hot[:, u], away[:, u], ACT.Relu, scale=-1.0, bias=one[:, :]).then_inc(hot_ready, 1)

                @block.vector
                def _(dve):
                    dve.sem_inc(masked_ready, 2)
                    dve.sem_inc(got_ready, 2)
                    ch = Chain(nc.vector, s_dve)
                    with dve.Fori(0, G // 2) as it:
                        ch.turn(0, it, 2)
                        for u in range(2):
                            g = it * 2 + u
                            t = ch.did(nc.vector.tensor_tensor(hi_mask[:, u], iota[:, 0:NT].unsqueeze(1).to_broadcast([P, C, NT]),
                                                               rec[:, bass.ds(g * C, C), CHI].unsqueeze(2).to_broadcast([P, C, NT]),
                                                               ALU.is_equal))
                            ch.need(t)
                            dve.wait_ge(got_ready, g + 3)
                            nc.vector.tensor_tensor(masked[:, :, :, :], got[:, u, :, 0:NT * D].rearrange("p c (h d) -> p c h d", d=D),
                                                    hi_mask[:, u].unsqueeze(3).to_broadcast([P, C, NT, D]), ALU.mult).then_inc(masked_ready, 1)
                            dve.wait_ge(masked_ready, g + 3)
                            nc.vector.tensor_reduce(moved[:, bass.ds(g * C, C), :], masked[:, :, :, :].rearrange("p c h d -> p c d h"), AX.X, ALU.add).then_inc(s_red, 1)

            with ExitStack() as pc:
                row_t = ps("row_t", [P, 8, 512], F32, pc)
                s_row, s_new, s_ch = sem("row_t_ready"), sem("new_ready"), sem("dve_n")
                CW = 480
                block = pc.enter_context(nc.Block())
                CH = ST * D // CW

                @block.tensor
                def _(pe):
                    for i in range(CH):
                        if i >= 8:
                            pe.wait_ge(s_new, i - 7)
                        nc.tensor.matmul(row_t[:, i % 8, 0:CW], expand[:, :], t_quad[:, i * CW:(i + 1) * CW], start=True, stop=True).then_inc(s_row, 1)

                @block.vector
                def _(dve):
                    ch = Chain(nc.vector, s_ch)
                    t = ch.did(nc.vector.scalar_tensor_tensor(out=moved[:, :, :], in0=rec[:, :, A0:A0 + D], scalar=1.0 / (KS - 1),
                                                              in1=moved[:, :, :], op0=ALU.mult, op1=ALU.add))
                    ch.need(t)
                    flat = moved[:, :, :].rearrange("p t d -> p (t d)")
                    for i in range(CH):
                        dve.wait_ge(s_row, i + 1)
                        nc.vector.tensor_tensor(flat[:, i * CW:(i + 1) * CW], flat[:, i * CW:(i + 1) * CW], row_t[:, i % 8, 0:CW],
                                                ALU.subtract).then_inc(s_new, 1)
                    dve.wait_ge(s_new, CH)
                    t = ch.did(nc.vector.tensor_scalar(flat, flat, 0.0, 1.0, ALU.max, ALU.min))
                    ch.need(t)
                    ch.did(nc.vector.tensor_scalar(flat, flat, float(KS - 1), None, ALU.mult))


_INS = ["x", "src", "dst", "edge_attr_3"] + ["L0_gnn_" + n for n in (
    "stn1_w", "stn1_b", "stn2_w", "stn2_b", "stn3_w", "stn3_b", "stn4_w", "stn4_b", "conv_w", "conv_b")]


def kernel(**inputs):
    import numpy as np
    import concourse.bacc as bacc
    from concourse.bass_utils import run_bass_kernel_spmd

    nc = bacc.Bacc("TRN2", target_bir_lowering=False, num_devices=1)
    arrays, args = {}, []
    for name in _INS:
        a = np.ascontiguousarray(inputs[name])
        arrays[f"in_{name}"] = a
        args.append(nc.dram_tensor(f"in_{name}", a.shape, mybir.dt.from_np(a.dtype), kind="ExternalInput").ap())
    args.append(nc.dram_tensor("out", (N, FIN), F32, kind="ExternalOutput").ap())
    spline_net(nc, *args)
    r = run_bass_kernel_spmd(nc, [arrays], core_ids=[0])
    return r.results[0]["out"]
```

```python
import concourse.bass as bass
from concourse import mybir
from contextlib import ExitStack

F32 = mybir.dt.float32
BF16 = mybir.dt.bfloat16
I32 = mybir.dt.int32
ALU = mybir.AluOpType
ACT = mybir.ActivationFunctionType
AX = mybir.AxisListType

P = 128
N, FIN, FH = 3125, 32, 64
E, D = 100000, 3
KS = 5
K = KS ** D
NT = -(-N // P)
EP, ET = 125, E // 125
Q = 32
OV0 = NT * P
BT = 2 * NT
assert -(-E // Q) <= NT * P
TPB = P // (P // Q)
ST = BT * TPB
W = 8
A0, VALID, COL, ROW, CLO, CHI = 0, 3, 4, 5, 6, 7
HX = FH + FIN
BIG = 3.0e38
AHEAD = 8


class Chain:

    def __init__(self, eng, sem):
        self.eng, self.sem, self.base, self.n = eng, sem, 0, 0

    def did(self, ins):
        ins.then_inc(self.sem, 1)
        self.n += 1
        return self.sem, self.base + self.n

    def need(self, ticket):
        self.eng.wait_ge(*ticket)

    def turn(self, start, it, per):
        self.base, self.n = start + it * per, 0

    def close(self, start, turns, per):
        assert self.n == per, (self.n, per)
        self.base, self.n = start + turns * per, 0

    def now(self):
        return self.base + self.n


def hold(eng, sem, value, held):
    eng.wait_ge(sem, value)
    eng.sem_inc(held, 1)


def spline_net(nc, x, src, dst, attr, w1, b1, w2, b2, w3, b3, w4, b4, wc, bc, out):
    with ExitStack() as ctx:
        def sb(name, shape, dt=F32, c=ctx):
            return c.enter_context(nc.sbuf_tensor(name, shape, dt))

        def ps(name, shape, dt=F32, c=ctx):
            return c.enter_context(nc.psum_tensor(name, shape, dt))

        def sem(name):
            return ctx.enter_context(nc.semaphore(name))

        slots = nc.dram_tensor("slots", (P * ST, W), F32, kind="Internal").ap()
        held = {e: sem(f"held_{e}") for e in ("pe", "act", "dve", "pool", "sp")}

        iota = sb("iota", [P, P])
        pid = sb("pid", [P, 1])
        npid = sb("npid", [P, 1])
        one = sb("one", [P, 1])
        ident = sb("ident", [P, P])
        deg = sb("deg", [P, NT])
        pairs = sb("pairs", [P, 1], I32)

        with ExitStack() as ab:
            place_edges(nc, ab, sb, ps, sem, held, src, dst, attr, slots, iota, pid, npid, one, ident, deg, pairs)

        rec = sb("rec", [P, ST + AHEAD, W])
        blocks = sb("blocks", [P, BT, FH])
        hid = sb("hid", [P, NT, FH])
        x_nodes = sb("x_nodes", [P, NT, FIN])
        wt1 = sb("wt1", [KS * KS, KS * FH])
        wt3, wt4 = sb("wt3", [FH, FH]), sb("wt4", [FH, D])
        bt1, bt2, btc, bt4 = sb("bt1", [P, FH]), sb("bt2", [P, FH]), sb("btc", [P, FIN]), sb("bt4", [P, D])
        bt3 = sb("bt3", [FH, 1])
        ovn, ov_lo, ov_hi = sb("ovn", [P, NT]), sb("ov_lo", [P, NT]), sb("ov_hi", [P, NT])
        ovn_i, ov_i = sb("ovn_i", [P, NT], I32), sb("ov_i", [P, NT], I32)
        inv_degree = sb("inv_degree", [P, NT])
        of_block = sb("of_block", [P, P // Q])
        up_c, down_c, up_floor, down_floor = [sb(n, [P, D, KS]) for n in ("up_c", "down_c", "up_floor", "down_floor")]
        table = nc.dram_tensor("table", (NT * P, HX), F32, kind="Internal").ap()
        x_slots = nc.dram_tensor("x_slots", (P, ST * FIN), F32, kind="Internal").ap()
        t_nodes = nc.dram_tensor("t_nodes", (NT * P, D), F32, kind="Internal").ap()
        t_blocks = nc.dram_tensor("t_blocks", (P, BT * D), F32, kind="Internal").ap()

        hat_consts = (up_c, down_c, up_floor, down_floor)
        first_layer(nc, sb, ps, sem, held, locals())
        gather_overflow(nc, sb, ps, sem, held, iota, blocks, pairs, ov_lo, ov_hi, inv_degree, bt1, FH, hid, "one")
        to_table(nc, sem, hid, x_nodes, table)
        conv(nc, sb, ps, sem, held, "two", FH, rec, None, hat_consts, of_block, ident, pairs, blocks, w2, table, x_slots)
        gather_overflow(nc, sb, ps, sem, held, iota, blocks, pairs, ov_lo, ov_hi, inv_degree, bt2, FH, hid, "two")
        with ExitStack() as c3:
            moved = sb("moved", [P, ST, D], F32, c3)
            t_node(nc, sb, ps, sem, held, hid, wt3, bt3, wt4, bt4, ident, ovn_i, t_nodes, t_blocks,
                   rec, moved, iota, npid, one, pairs)
            conv(nc, sb, ps, sem, held, "three", FIN, rec, moved, hat_consts, of_block, ident, pairs, blocks, wc, None, x_slots)
        gather_overflow(nc, sb, ps, sem, held, iota, blocks, pairs, ov_lo, ov_hi, inv_degree, btc, FIN, None, "three",
                        x_nodes, out)




def place_edges(nc, ab, sb, ps, sem, held, src, dst, attr, slots, iota, pid, npid, one, ident, deg, pairs):
    G = 20
    GN = ET // G
    C = 8
    SC = 16
    SN, CN = ET // SC, SC // C
    BC = 2 * CN

    iota_i = sb("iota_i", [P, P], I32, ab)
    pid_i = sb("pid_i", [P, 1], I32, ab)
    lower = sb("lower", [P, P], F32, ab)
    upper = sb("upper", [P, P], F32, ab)
    ones = sb("ones", [P, P], F32, ab)
    zeros = sb("zeros", [P, ST], F32, ab)
    src_i = sb("src_i", [EP, ET], I32, ab)
    dst_i = sb("dst_i", [EP, ET], I32, ab)
    tmp_i = sb("tmp_i", [EP, ET], I32, ab)
    edge_attr = sb("edge_attr", [EP, ET * D], F32, ab)
    row = sb("row", [EP, ET + C], F32, ab)
    row_lo = sb("row_lo", [EP, ET + C], F32, ab)
    row_hi = sb("row_hi", [EP, ET], F32, ab)
    hot_lo = sb("hot_lo", [EP, 2, G, P], BF16, ab)
    hot_hi = sb("hot_hi", [EP, 2, G, NT], BF16, ab)
    before = sb("before", [P, ET + 1, NT], F32, ab)
    onescan = sb("onescan", [P, ET], F32, ab)
    over_i = sb("over_i", [P, NT], I32, ab)
    over = sb("over", [P, NT], F32, ab)
    over_at = sb("over_at", [P, NT], F32, ab)
    hi_sum = sb("hi_sum", [P, NT], F32, ab)

    src_in, dst_in, attr_in, cleared = sem("src_in"), sem("dst_in"), sem("attr_in"), sem("cleared")
    zero_ready, const_ready, hot_ready, hist_ready = sem("zero_ready"), sem("const_ready"), sem("hot_ready"), sem("hist_ready")
    hist_free, dve_a, pool_a, over_ready, pre_ready = sem("hist_free"), sem("dve_a"), sem("pool_a"), sem("over_ready"), sem("pre_ready")

    with ExitStack() as pa:
        hist = ps("hist", [P, 2, 512], F32, pa)
        over_ps = ps("over_ps", [P, 512], F32, pa)
        block = pa.enter_context(nc.Block())

        @block.sync
        def _(sp):
            sp.dma_start(src_i[:, :], src.rearrange("(p t) -> p t", p=EP)).then_inc(src_in, 16)
            sp.dma_start(dst_i[:, :], dst.rearrange("(p t) -> p t", p=EP)).then_inc(dst_in, 16)
            sp.dma_start(edge_attr[:, :], attr.rearrange("(p t) d -> p (t d)", p=EP)).then_inc(attr_in, 16)
            sp.wait_ge(zero_ready, 1)
            sp.dma_start(slots.rearrange("(p w t) c -> p w (t c)", p=P, w=W),
                         zeros[:, :].unsqueeze(1).to_broadcast([P, W, ST])).then_inc(cleared, 16)
            sp.wait_ge(cleared, 16)

        @block.gpsimd
        def _(pool):
            ch = Chain(pool, pool_a)
            pool.iota(iota_i[:, :], [[1, P]], base=0, channel_multiplier=0)
            pool.iota(pid_i[:, :], [[0, 1]], base=0, channel_multiplier=1)
            nc.gpsimd.memset(ones[:, :], 1.0)
            t = ch.did(nc.gpsimd.memset(ident[:, :], 0.0))
            ch.need(t)
            ch.did(nc.gpsimd.affine_select(out=ident[:, :], in_=ident[:, :], compare_op=ALU.not_equal, fill=1.0,
                                           base=0, pattern=[[-1, P]], channel_multiplier=1))
            ch.did(nc.gpsimd.affine_select(out=lower[:, :], in_=ones[:, :], compare_op=ALU.is_gt, fill=0.0,
                                           base=0, pattern=[[-1, P]], channel_multiplier=1))
            t = ch.did(nc.gpsimd.affine_select(out=upper[:, :], in_=ones[:, :], compare_op=ALU.is_gt, fill=0.0,
                                               base=0, pattern=[[1, P]], channel_multiplier=-1))
            ch.need(t)
            nc.gpsimd.memset(one[:, :], 1.0).then_inc(const_ready, 1)

        @block.vector
        def _(dve):
            ch = Chain(dve, dve_a)
            nc.vector.memset(zeros[:, :], 0.0).then_inc(zero_ready, 1)
            nc.vector.memset(onescan[:, :], 1.0)
            nc.vector.memset(row[:, ET:ET + C], 0.0)
            nc.vector.memset(row_lo[:, ET:ET + C], 0.0)
            nc.vector.memset(before[:, 0, :], 0.0)
            dve.wait_ge(src_in, 16)
            t = ch.did(nc.vector.tensor_scalar(tmp_i[:, :], src_i[:, :], P - 1, None, ALU.bitwise_and))
            nc.vector.tensor_copy(row[:, 0:ET], src_i[:, :])
            ch.need(t)
            t = ch.did(nc.vector.tensor_copy(row_lo[:, 0:ET], tmp_i[:, :]))
            ch.need(t)
            t = ch.did(nc.vector.tensor_scalar(tmp_i[:, :], src_i[:, :], 7, None, ALU.arith_shift_right))
            ch.need(t)
            ch.did(nc.vector.tensor_copy(row_hi[:, :], tmp_i[:, :]))
            dve.wait_ge(const_ready, 1)
            ch.did(nc.vector.tensor_copy(iota[:, :], iota_i[:, :]))
            t = ch.did(nc.vector.tensor_copy(pid[:, :], pid_i[:, :]))
            ch.need(t)
            t = ch.did(nc.vector.tensor_scalar(npid[:, :], pid[:, :], -1.0, None, ALU.mult))
            ch.need(t)
            with dve.Fori(0, GN // 2) as it:
                for u in range(2):
                    g = it * 2 + u
                    dve.wait_ge(hist_ready, g + 1)
                    nc.vector.tensor_tensor(hot_lo[:, u], iota[:EP, :].unsqueeze(1).to_broadcast([EP, G, P]),
                                            row_lo[:, bass.ds(g * G, G)].unsqueeze(2).to_broadcast([EP, G, P]),
                                            ALU.is_equal)
                    nc.vector.tensor_tensor(hot_hi[:, u], iota[:EP, 0:NT].unsqueeze(1).to_broadcast([EP, G, NT]),
                                            row_hi[:, bass.ds(g * G, G)].unsqueeze(2).to_broadcast([EP, G, NT]),
                                            ALU.is_equal).then_inc(hot_ready, 1)
            dve.wait_ge(hist_free, GN + 2)
            for h in range(NT):
                last = ch.did(nc.vector.tensor_tensor_scan(before[:, 1:ET + 1, h], onescan[:, :], before[:, 1:ET + 1, h],
                                                           0.0, ALU.mult, ALU.add))
            ch.need(last)
            t = ch.did(nc.vector.tensor_copy(deg[:, :], before[:, ET, :]))
            ch.need(t)
            t = ch.did(nc.vector.tensor_scalar(over[:, :], deg[:, :], -1.0, 0.0, ALU.add, ALU.max))
            ch.need(t)
            t = ch.did(nc.vector.tensor_copy(over_i[:, :], over[:, :]))
            ch.need(t)
            t = ch.did(nc.vector.tensor_scalar(over_i[:, :], over_i[:, :], 5, None, ALU.arith_shift_right))
            ch.need(t)
            nc.vector.tensor_copy(over[:, :], over_i[:, :]).then_inc(over_ready, 1)
            dve.wait_ge(pre_ready, 1)
            t = ch.did(nc.vector.tensor_tensor_scan(hi_sum[:, :], onescan[:, 0:NT], over_ps[:, NT:2 * NT],
                                                    0.0, ALU.mult, ALU.add))
            ch.need(t)
            t = ch.did(nc.vector.tensor_scalar(pairs[:, :], hi_sum[:, NT - 1:NT], float(OV0 + 2 * P - 1), None, ALU.add))
            ch.need(t)
            ch.did(nc.vector.tensor_scalar(pairs[:, :], pairs[:, :], 8, None, ALU.arith_shift_right))
            t = ch.did(nc.vector.tensor_tensor(over_at[:, :], hi_sum[:, :], over_ps[:, NT:2 * NT], ALU.subtract))
            ch.need(t)
            t = ch.did(nc.vector.scalar_tensor_tensor(out=over_at[:, :], in0=over_at[:, :], scalar=float(OV0 - 1),
                                                      in1=over_ps[:, 0:NT], op0=ALU.add, op1=ALU.add))
            ch.need(t)

        @block.tensor
        def _(pe):
            pe.sem_inc(hist_ready, 2)
            with pe.Fori(0, GN // 2) as it:
                for u in range(2):
                    g = it * 2 + u
                    hold(pe, hot_ready, g + 1, held["pe"])
                    hold(pe, hist_free, g + 1, held["pe"])
                    for j in range(G):
                        last = nc.tensor.matmul(hist[:, u, j * NT:(j + 1) * NT], hot_lo[:, u, j], hot_hi[:, u, j],
                                                start=True, stop=True)
                    last.then_inc(hist_ready, 1)
            pe.wait_ge(over_ready, 1)
            nc.tensor.matmul(over_ps[:, 0:NT], upper[:, :], over[:, :], start=True, stop=True)
            nc.tensor.matmul(over_ps[:, NT:2 * NT], ones[:, :], over[:, :], start=True, stop=True).then_inc(pre_ready, 1)

        @block.scalar
        def _(act):
            act.sem_inc(hist_free, 2)
            with act.Fori(0, GN // 2) as it:
                for u in range(2):
                    g = it * 2 + u
                    hold(act, hist_ready, g + 3, held["act"])
                    nc.scalar.copy(before[:, bass.ds(g * G + 1, G), :].rearrange("p t h -> p (t h)"),
                                   hist[:, u, 0:G * NT]).then_inc(hist_free, 1)

    record = sb("record", [EP, 2, SC, W], F32, ab)
    slot_i = sb("slot_i", [EP, 2, SC], I32, ab)
    col_row = sb("col_row", [EP, 2, C], F32, ab)
    col_lo_b = sb("col_lo_b", [EP, 2, C], BF16, ab)
    ident_ab = sb("ident_ab", [P, P], BF16, ab)
    places = sb("places", [P, 2, C, 2, NT], F32, ab)
    col_f = sb("col_f", [EP, ET], F32, ab)
    col_lo = sb("col_lo", [EP, ET], F32, ab)
    col_hi = sb("col_hi", [EP, ET], F32, ab)
    hot_t = sb("hot_t", [P, 2, C, P], F32, ab)
    away = sb("away", [P, 2, C, P], BF16, ab)
    junk = sb("junk", [EP, C, P], BF16, ab)
    hi_mask = sb("hi_mask", [EP, C, NT], F32, ab)
    masked = sb("masked", [EP, C, 2, NT], F32, ab)
    within = sb("within", [EP, SC], F32, ab)
    found = sb("found", [EP, SC, 2], F32, ab)
    rank = sb("rank", [EP, SC], F32, ab)
    rank_i = sb("rank_i", [EP, SC], I32, ab)
    q_i = sb("q_i", [EP, SC], I32, ab)
    r_i = sb("r_i", [EP, SC], I32, ab)
    qf = sb("qf", [EP, SC], F32, ab)
    rf = sb("rf", [EP, SC], F32, ab)
    far = sb("far", [EP, SC], F32, ab)
    blk_i = sb("blk_i", [EP, SC], I32, ab)
    part_i = sb("part_i", [EP, 3, SC], I32, ab)
    part = sb("part", [EP, 3, SC], F32, ab)

    cols_ready, bc_ready, hot_t_ready, found_ready, lookup_free = [sem(n) for n in (
        "cols_ready", "bc_ready", "hot_t_ready", "found_ready", "lookup_free")]
    dve_const, dve_b, act_b, rec_ready, bc_free, rec_free = sem("dve_const"), sem("dve_b"), sem("act_b"), sem("rec_ready"), sem("bc_free"), sem("rec_free")
    sent = [sem("sent0"), sem("sent1")]
    with ExitStack() as pb:
        row_bc = ps("row_bc", [P, 2, C, P], F32, pb)
        lo_bc = ps("lo_bc", [P, 2, C, P], BF16, pb)
        lookup = ps("lookup", [P, 2, 512], F32, pb)
        block = pb.enter_context(nc.Block())

        @block.scalar
        def _(act):
            ch = Chain(act, act_b)
            act.wait_ge(dve_const, 2)

            def take_cols(c, u):
                nc.scalar.copy(col_row[:, u, :], row[:, bass.ds(c * C, C)])
                nc.scalar.copy(col_lo_b[:, u, :], row_lo[:, bass.ds(c * C, C)]).then_inc(cols_ready, 1)

            take_cols(0, 0)
            with act.Fori(0, ET // C // BC) as it:
                ch.turn(0, it, BC)
                for i in range(BC):
                    c, u = it * BC + i, i % 2
                    hold(act, bc_ready, c + 2, held["act"])
                    hold(act, bc_free, c + 2, held["act"])
                    take_cols(c + 1, 1 - u)
                    hold(act, found_ready, c + 1, held["act"])
                    nc.scalar.copy(places[:, u, :, 0, :], before[:, bass.ds(c * C, C), :])
                    act.wait_ge(bc_ready, c + 3)
                    t = ch.did(nc.scalar.activation(away[:, u, :, 0:EP], lo_bc[:, u, :, 0:EP], ACT.Abs, bias=npid[:, :]))
                    ch.need(t)
                    nc.scalar.activation(hot_t[:, u, :, 0:EP], away[:, u, :, 0:EP], ACT.Relu, scale=-1.0,
                                         bias=one[:, :]).then_inc(hot_t_ready, 1)

        @block.tensor
        def _(pe):
            pe.sem_inc(bc_ready, 2)
            pe.sem_inc(found_ready, 2)

            def turn(c, u):
                hold(pe, cols_ready, c + 1, held["pe"])
                hold(pe, bc_free, c + 1, held["pe"])
                for j in range(C):
                    nc.tensor.transpose(row_bc[:, u, j, 0:EP], col_row[:, u, j:j + 1].to_broadcast([EP, P]), ident[:EP, :EP])
                for j in range(C):
                    last = nc.tensor.transpose(lo_bc[:, u, j, 0:EP], col_lo_b[:, u, j:j + 1].to_broadcast([EP, P]), ident_ab[:EP, :EP])
                last.then_inc(bc_ready, 1)

            turn(0, 0)
            with pe.Fori(0, ET // C // BC) as it:
                for i in range(BC):
                    c, u = it * BC + i, i % 2
                    turn(c + 1, 1 - u)
                    hold(pe, hot_t_ready, c + 1, held["pe"])
                    hold(pe, lookup_free, c + 1, held["pe"])
                    for j in range(C):
                        last = nc.tensor.matmul(lookup[:EP, u, j * 2 * NT:(j + 1) * 2 * NT], hot_t[:, u, j, 0:EP],
                                                places[:, u, j].rearrange("p w h -> p (w h)"), start=True, stop=True)
                    last.then_inc(found_ready, 1)

        @block.vector
        def _(dve):
            ch = Chain(dve, dve_b)
            dve.sem_inc(bc_free, 2)
            dve.sem_inc(lookup_free, 2)
            dve.sem_inc(rec_free, 2)
            nc.vector.tensor_copy(ident_ab[:, :], ident[:, :]).then_inc(dve_const, 1)
            nc.vector.tensor_copy(places[:, :, :, 1, :].rearrange("p u c h -> p (u c) h"),
                                  over_at[:, :].unsqueeze(1).to_broadcast([P, 2 * C, NT])).then_inc(dve_const, 1)
            dve.wait_ge(dst_in, 16)
            dve.wait_ge(attr_in, 16)
            t = ch.did(nc.vector.tensor_scalar(tmp_i[:, :], dst_i[:, :], P - 1, None, ALU.bitwise_and))
            nc.vector.tensor_copy(col_f[:, :], dst_i[:, :])
            nc.vector.memset(record[:, :, :, VALID], 1.0)
            ch.need(t)
            t = ch.did(nc.vector.tensor_copy(col_lo[:, :], tmp_i[:, :]))
            ch.need(t)
            t = ch.did(nc.vector.tensor_scalar(tmp_i[:, :], dst_i[:, :], 7, None, ALU.arith_shift_right))
            ch.need(t)
            t = ch.did(nc.vector.tensor_copy(col_hi[:, :], tmp_i[:, :]))
            ch.need(t)
            start = ch.n
            per = 2 * (CN * 2 + 18)
            with dve.Fori(0, SN // 2) as it:
                ch.turn(start, it, per)
                for u in range(2):
                    s = it * 2 + u
                    for cc in range(CN):
                        c, v = s * CN + cc, (u * CN + cc) % 2
                        js = slice(cc * C, (cc + 1) * C)
                        ch.did(nc.vector.tensor_tensor(hi_mask[:, :, :], iota[:EP, 0:NT].unsqueeze(1).to_broadcast([EP, C, NT]),
                                                       row_hi[:, bass.ds(c * C, C)].unsqueeze(2).to_broadcast([EP, C, NT]),
                                                       ALU.is_equal))
                        dve.wait_ge(bc_ready, c + 3)
                        for j in range(C):
                            last = nc.vector.scalar_tensor_tensor(
                                out=junk[:, j, 0:EP], in0=row_bc[:EP, v, j, 0:EP], scalar=col_row[:, v, j:j + 1],
                                in1=lower[:EP, 0:EP], op0=ALU.is_equal, op1=ALU.mult,
                                accum_out=within[:, cc * C + j:cc * C + j + 1])
                        hm = bc_free, c + 3
                        last.then_inc(bc_free, 1)
                        dve.wait_ge(found_ready, c + 3)
                        ch.need(hm)
                        nc.vector.tensor_tensor(
                            masked[:, :, :, :], lookup[:EP, v, 0:C * 2 * NT].rearrange("p (c w h) -> p c w h", c=C, w=2),
                            hi_mask[:, :, :].unsqueeze(2).to_broadcast([EP, C, 2, NT]), ALU.mult).then_inc(lookup_free, 1)
                        ch.need((lookup_free, c + 3))
                        t = ch.did(nc.vector.tensor_reduce(found[:, js, :], masked[:, :, :, :], AX.X, ALU.add))
                    e = bass.ds(s * SC, SC)
                    ch.need(t)
                    t = ch.did(nc.vector.tensor_tensor(rank[:, :], found[:, :, 0], within[:, :], ALU.add))
                    ch.need(t)
                    t = ch.did(nc.vector.tensor_copy(rank_i[:, :], rank[:, :]))
                    ch.need(t)
                    tq = ch.did(nc.vector.tensor_scalar(q_i[:, :], rank_i[:, :], 5, None, ALU.arith_shift_right))
                    tr = ch.did(nc.vector.tensor_scalar(r_i[:, :], rank_i[:, :], Q - 1, None, ALU.bitwise_and))
                    ch.need(tq)
                    tq = ch.did(nc.vector.tensor_copy(qf[:, :], q_i[:, :]))
                    ch.need(tr)
                    ch.did(nc.vector.tensor_copy(rf[:, :], r_i[:, :]))
                    ch.need(tq)
                    t = ch.did(nc.vector.tensor_tensor(far[:, :], found[:, :, 1], qf[:, :], ALU.add))
                    ch.need(t)
                    t = ch.did(nc.vector.tensor_tensor(far[:, :], far[:, :], row[:, e], ALU.subtract))
                    ch.need(t)
                    t = ch.did(nc.vector.scalar_tensor_tensor(out=far[:, :], in0=qf[:, :], scalar=1.0, in1=far[:, :],
                                                              op0=ALU.min, op1=ALU.mult))
                    ch.need(t)
                    t = ch.did(nc.vector.tensor_tensor(blk_i[:, :], far[:, :], row[:, e], ALU.add))
                    ch.need(t)
                    ch.did(nc.vector.tensor_scalar(part_i[:, 0, :], blk_i[:, :], 5, 3, ALU.arith_shift_right, ALU.bitwise_and))
                    ch.did(nc.vector.tensor_scalar(part_i[:, 1, :], blk_i[:, :], 7, None, ALU.arith_shift_right))
                    t = ch.did(nc.vector.tensor_scalar(part_i[:, 2, :], blk_i[:, :], 31, None, ALU.bitwise_and))
                    ch.need(t)
                    t = ch.did(nc.vector.tensor_copy(part[:, :, :], part_i[:, :, :]))
                    ch.need(t)
                    t = ch.did(nc.vector.scalar_tensor_tensor(out=part[:, 0, :], in0=part[:, 0, :], scalar=float(Q),
                                                              in1=rf[:, :], op0=ALU.mult, op1=ALU.add))
                    ch.need(t)
                    t = ch.did(nc.vector.scalar_tensor_tensor(out=part[:, 0, :], in0=part[:, 0, :], scalar=float(ST),
                                                              in1=part[:, 2, :], op0=ALU.mult, op1=ALU.add))
                    dve.wait_ge(rec_free, s + 1)
                    ch.need(t)
                    ch.did(nc.vector.scalar_tensor_tensor(out=slot_i[:, u, :], in0=part[:, 1, :], scalar=float(TPB),
                                                          in1=part[:, 0, :], op0=ALU.mult, op1=ALU.add))
                    ch.did(nc.vector.tensor_scalar(record[:, u, :, A0:A0 + D],
                                                   edge_attr[:, bass.ds(s * (SC * D), SC * D)].rearrange("p (t d) -> p t d", d=D),
                                                   float(KS - 1), None, ALU.mult))
                    for word, of in ((COL, col_f), (ROW, row), (CLO, col_lo), (CHI, col_hi)):
                        last = nc.vector.tensor_scalar(record[:, u, :, word], of[:, e], 1.0, None, ALU.mult)
                    last.then_inc(rec_ready, 1)
            ch.close(start, SN // 2, per)

        @block.gpsimd
        def _(pool):
            with pool.Fori(0, SN // 2) as it:
                for u in range(2):
                    hold(pool, rec_ready, it * 2 + u + 1, held["pool"])
                    for j in range(SC):
                        pool.indirect_dma_start(slots, bass.IndirectOffsetOnAxis(ap=slot_i[:, u, j:j + 1], axis=0),
                                                record[:, u, j, :], None).then_inc(sent[u], 16)

        @block.sync
        def _(sp):
            with sp.Fori(0, SN // 2) as it:
                for u in range(2):
                    hold(sp, sent[u], (it + 1) * (16 * SC), held["sp"])
                    sp.sem_inc(rec_free, 1)

def hats(ch, at, shape, hat_consts, up, down, hat, valid):
    up_c, down_c, up_floor, down_floor = [c[:, :, :].unsqueeze(1).to_broadcast(shape) for c in hat_consts]
    wide = at.unsqueeze(3).to_broadcast(shape)
    v = ch.eng
    a = ch.did(v.tensor_tensor(up[:, :, :, :], wide, up_c, ALU.subtract))
    b = ch.did(v.tensor_tensor(down[:, :, :, :], down_c, wide, ALU.subtract))
    ch.need(a)
    ch.did(v.tensor_tensor(up[:, :, :, :], up[:, :, :, :], up_floor, ALU.max))
    ch.need(b)
    b = ch.did(v.tensor_tensor(down[:, :, :, :], down[:, :, :, :], down_floor, ALU.max))
    ch.need(b)
    a = ch.did(v.tensor_tensor(hat[:, :, :, :], up[:, :, :, :], down[:, :, :, :], ALU.min))
    ch.need(a)
    return ch.did(v.tensor_tensor(hat[:, :, 0, :], hat[:, :, 0, :], valid.unsqueeze(2).to_broadcast([P, TPB, KS]), ALU.mult))


HATS = 6


def first_layer(nc, sb, ps, sem, held, g):
    rec, slots, blocks = g["rec"], g["slots"], g["blocks"]
    PIECES = 5
    with ExitStack() as c:
        up, down = sb("up1", [P, TPB, D, KS], F32, c), sb("down1", [P, TPB, D, KS], F32, c)
        hat = sb("hat1", [P, TPB, D, KS], F32, c)
        hat01 = sb("hat01_1", [P, 2, TPB, KS * KS], F32, c)
        hat2 = sb("hat2_1", [P, 2, TPB, P // Q, KS], F32, c)
        sums = sb("sums", [KS * KS, P // Q, TPB, KS], F32, c)
        sum_ps = ps("sum_ps", [P, 2, 512], F32, c)
        row_ps = ps("row_ps", [P, 512], F32, c)
        rec_in, small_in, const_done, w_in = sem("rec_in"), sem("small_in"), sem("const_done"), sem("w_in")
        hats_ready, sum_ready, sums_copied, row_ready, dve_c = [sem(n) for n in (
            "hats_ready", "sum_ready", "sums_copied", "row_ready", "dve_c")]
        dve_ov = sem("dve_ov")
        block = c.enter_context(nc.Block())

        @block.sync
        def _(sp):
            s = slots.rearrange("(p t) c -> p t c", p=P)
            sp.dma_start(g["wt1"][:, :], g["w1"].rearrange("(a b) i f -> a (b i f)", b=KS)).then_inc(w_in, 16)
            step = ST // PIECES
            for i in range(PIECES):
                sp.dma_start(rec[:, i * step:(i + 1) * step, :], s[:, i * step:(i + 1) * step, :]).then_inc(rec_in, 16)
            for q in range(P // Q):
                sp.dma_start(g["ovn"][q * Q:(q + 1) * Q, :],
                             s[q * Q, ST // 2:ST, ROW].rearrange("(b j) -> j b", j=TPB),
                             allow_slow_non_contiguous=True).then_inc(small_in, 16)
            sp.dma_start(g["wt3"][:, :], g["w3"]).then_inc(small_in, 16)
            sp.dma_start(g["wt4"][:, :], g["w4"]).then_inc(small_in, 16)
            sp.dma_start(g["bt3"][:, :], g["b3"].unsqueeze(1)).then_inc(small_in, 16)
            for to, of, n in (("bt1", "b1", FH), ("bt2", "b2", FH), ("btc", "bc", FIN), ("bt4", "b4", D)):
                sp.dma_start(g[to][:, :], g[of].unsqueeze(0).to_broadcast([P, n])).then_inc(small_in, 16)
            sp.wait_ge(const_done, 1)
            full = N // P
            sp.dma_start(g["x_nodes"][:, 0:full, :], g["x"][0:full * P, :].rearrange("(t p) f -> p t f", p=P)).then_inc(small_in, 16)
            sp.dma_start(g["x_nodes"][0:N - full * P, full, :], g["x"][full * P:N, :]).then_inc(small_in, 16)
            sp.wait_ge(small_in, 16 * 13)

        @block.vector
        def _(dve):
            nc.vector.memset(rec[:, ST:ST + AHEAD, :], 0.0)
            nc.vector.memset(g["x_nodes"][:, :, :], 0.0).then_inc(const_done, 1)
            nc.vector.memset(blocks[:, :, :], 0.0).then_inc(const_done, 1)
            ch = Chain(nc.vector, dve_c)
            t = ch.did(nc.vector.tensor_scalar(g["inv_degree"][:, :], g["deg"][:, :], 1.0, None, ALU.max))
            ch.need(t)
            ch.did(nc.vector.reciprocal(g["inv_degree"][:, :], g["inv_degree"][:, :]))
            nc.vector.memset(g["of_block"][:, :], 0.0)
            for j in range(KS):
                nc.vector.memset(g["up_c"][:, :, j], float(j - 1))
                nc.vector.memset(g["down_c"][:, :, j], float(j + 1))
                nc.vector.memset(g["up_floor"][:, :, j], BIG if j == 0 else -BIG if j == 1 else 0.0)
                t = ch.did(nc.vector.memset(g["down_floor"][:, :, j], BIG if j == KS - 1 else -BIG if j == KS - 2 else 0.0))
            ch.need(t)
            for q in range(P // Q):
                t = ch.did(nc.vector.memset(g["of_block"][q * Q:(q + 1) * Q, q:q + 1], 1.0))
            dve.wait_ge(rec_in, 16 * PIECES)
            ch.need(t)
            start, per = ch.n, 2 * HATS
            used = used_pairs(dve, g["pairs"])
            with dve.Fori(0, BT // 2) as it, dve.If(it < used):
                ch.turn(start, it, per)
                for u in range(2):
                    c = it * 2 + u
                    e = bass.ds(c * TPB, TPB)
                    t = hats(ch, rec[:, e, A0:A0 + D], [P, TPB, D, KS], g["hat_consts"], up, down, hat, rec[:, e, VALID])
                    dve.wait_ge(sum_ready, c + 1)
                    nc.vector.tensor_tensor(hat2[:, u], hat[:, :, 2, :].unsqueeze(2).to_broadcast([P, TPB, P // Q, KS]),
                                            g["of_block"][:, :].unsqueeze(1).unsqueeze(3).to_broadcast([P, TPB, P // Q, KS]),
                                            ALU.mult)
                    ch.need(t)
                    nc.vector.tensor_tensor(hat01[:, u].rearrange("p t (a b) -> p t a b", a=KS),
                                            hat[:, :, 0, :].unsqueeze(3).to_broadcast([P, TPB, KS, KS]),
                                            hat[:, :, 1, :].unsqueeze(2).to_broadcast([P, TPB, KS, KS]),
                                            ALU.mult).then_inc(hats_ready, 1)
            ch = Chain(nc.vector, dve_ov)
            dve.wait_ge(small_in, 16 * 13)
            t = ch.did(nc.vector.tensor_copy(g["ovn_i"][:, :], g["ovn"][:, :]))
            ch.need(t)
            t = ch.did(nc.vector.tensor_scalar(g["ov_i"][:, :], g["ovn_i"][:, :], P - 1, None, ALU.bitwise_and))
            ch.need(t)
            t = ch.did(nc.vector.tensor_copy(g["ov_lo"][:, :], g["ov_i"][:, :]))
            ch.need(t)
            t = ch.did(nc.vector.tensor_scalar(g["ov_i"][:, :], g["ovn_i"][:, :], 7, None, ALU.arith_shift_right))
            ch.need(t)
            ch.did(nc.vector.tensor_copy(g["ov_hi"][:, :], g["ov_i"][:, :]))

        @block.tensor
        def _(pe):
            pe.sem_inc(sum_ready, 2)
            pe.wait_ge(w_in, 16)
            used = used_pairs(pe, g["pairs"])
            with pe.Fori(0, BT // 2) as it, pe.If(it < used):
                for u in range(2):
                    c = it * 2 + u
                    hold(pe, hats_ready, c + 1, held["pe"])
                    for j in range(TPB):
                        h, jj = divmod(j, TPB // 2)
                        last = nc.tensor.matmul(sum_ps[0:KS * KS, h, jj * 20:(jj + 1) * 20], hat01[:, u, j, :],
                                                hat2[:, u, j].rearrange("p q k -> p (q k)"), start=True, stop=True)
                    last.then_inc(sum_ready, 1)
                    hold(pe, sums_copied, c * 3 + 2, held["pe"])
                    for k in range(KS):
                        last = nc.tensor.matmul(row_ps[:, 0:FH], sums[:, :, :, k].rearrange("p q t -> p (q t)"),
                                                g["wt1"][:, k * FH:(k + 1) * FH], start=(k == 0), stop=(k == KS - 1))
                    last.then_inc(row_ready, 1)

        @block.scalar
        def _(act):
            act.wait_ge(const_done, 2)
            used = used_pairs(act, g["pairs"])
            with act.Fori(0, BT // 2) as it, act.If(it < used):
                for u in range(2):
                    c = it * 2 + u
                    act.wait_ge(sum_ready, c + 3)
                    for h in range(2):
                        nc.scalar.copy(sums[:, :, h * (TPB // 2):(h + 1) * (TPB // 2), :].rearrange("p q t k -> p t q k"),
                                       sum_ps[0:KS * KS, h, 0:320].rearrange("p (t q k) -> p t q k", q=P // Q, k=KS)).then_inc(sums_copied, 1)
                    hold(act, row_ready, c + 1, held["act"])
                    nc.scalar.copy(blocks[:, bass.ds(c, 1), :].rearrange("p t f -> p (t f)"), row_ps[:, 0:FH]).then_inc(sums_copied, 1)


def gather_overflow(nc, sb, ps, sem, held, iota, blocks, pairs, ov_lo, ov_hi, inv_degree, bias, F, hid, name, x_nodes=None, out=None):
    with ExitStack() as c:
        hot = sb("ov_hot_" + name, [P, NT, P], F32, c)
        mask = sb("ov_mask_" + name, [P, NT, NT], F32, c)
        spread = sb("ov_spread_" + name, [P, 3, NT, F], F32, c)
        node = sb("node_" + name, [P, NT, F], F32, c)
        pos = sb("node_pos_" + name, [P, NT, F], F32, c)
        neg = sb("node_neg_" + name, [P, NT, F], F32, c)
        stat = sb("stat_" + name, [P, 3, NT], F32, c)
        eps = sb("eps_" + name, [P, 1], F32, c)
        add_ps = ps("add_ps_" + name, [P, 4 * 512], F32, c)
        s_spread, s_added, s_spread_last, s_added_all, s_dve, s_neg, s_exp, s_out = [sem(n + name) for n in (
            "spread_ready_", "added_", "spread_last_", "added_all_", "dve_g_", "neg_ready_", "exp_ready_", "out_stored_")]
        per_bank = 512 // F
        steps = []
        banks = [(h, min(h + per_bank, NT)) for h in range(0, NT, per_bank)]
        block = c.enter_context(nc.Block())

        @block.vector
        def _(dve):
            ch = Chain(nc.vector, s_dve)
            nc.vector.memset(eps[:, :], 1e-5)
            ch.did(nc.vector.tensor_tensor(hot[:, :, :], iota[:, :].unsqueeze(1).to_broadcast([P, NT, P]),
                                           ov_lo[:, :].unsqueeze(2).to_broadcast([P, NT, P]), ALU.is_equal))
            t = ch.did(nc.vector.tensor_tensor(mask[:, :, :], iota[:, 0:NT].unsqueeze(1).to_broadcast([P, NT, NT]),
                                               ov_hi[:, :].unsqueeze(2).to_broadcast([P, NT, NT]), ALU.is_equal))
            ch.need(t)
            def spread_tile(i, o):
                last = i == NT - 1
                if i >= 2 and not last:
                    dve.wait_ge(s_added, i - 1)
                nc.vector.tensor_tensor(spread[:, 2 if last else i % 2], blocks[:, NT + o, 0:F].unsqueeze(1).to_broadcast([P, NT, F]),
                                        mask[:, o, :].unsqueeze(2).to_broadcast([P, NT, F]), ALU.mult).then_inc(
                                            s_spread_last if last else s_spread, 1)

            over_tiles(dve, pairs, spread_tile)
            dve.wait_ge(s_added_all, 1)
            t = ch.did(nc.vector.tensor_tensor(node[:, :, :], blocks[:, 0:NT, 0:F],
                                               add_ps[:, 0:NT * F].rearrange("p (t f) -> p t f", f=F), ALU.add))
            ch.need(t)
            t = ch.did(nc.vector.tensor_tensor(node[:, :, :], node[:, :, :], inv_degree[:, :].unsqueeze(2).to_broadcast([P, NT, F]), ALU.mult))
            ch.need(t)
            t = ch.did(nc.vector.tensor_tensor(node[:, :, :], node[:, :, :], bias[:, :].unsqueeze(1).to_broadcast([P, NT, F]), ALU.add))
            ch.need(t)
            if out is None:
                nc.vector.tensor_scalar(neg[:, :, :], node[:, :, :], 0.0, None, ALU.min).then_inc(s_neg, 1)
                t = ch.did(nc.vector.tensor_scalar(pos[:, :, :], node[:, :, :], 0.0, None, ALU.max))
                dve.wait_ge(s_exp, 1)
                ch.need(t)
                ch.did(nc.vector.scalar_tensor_tensor(out=hid[:, :, :], in0=neg[:, :, :], scalar=-1.0, in1=pos[:, :, :],
                                                      op0=ALU.add, op1=ALU.add))
                return
            t = ch.did(nc.vector.tensor_tensor(node[:, :, :], node[:, :, :], x_nodes[:, :, :], ALU.add))
            ch.need(t)
            t = ch.did(nc.vector.tensor_reduce(stat[:, 0, :], node[:, :, :], AX.X, ALU.add))
            ch.need(t)
            t = ch.did(nc.vector.tensor_scalar(stat[:, 0, :], stat[:, 0, :], 1.0 / F, None, ALU.mult))
            ch.need(t)
            t = ch.did(nc.vector.tensor_tensor(node[:, :, :], node[:, :, :], stat[:, 0, :].unsqueeze(2).to_broadcast([P, NT, F]), ALU.subtract))
            ch.need(t)
            t = ch.did(nc.vector.tensor_tensor(pos[:, :, :], node[:, :, :], node[:, :, :], ALU.mult))
            ch.need(t)
            t = ch.did(nc.vector.tensor_reduce(stat[:, 1, :], pos[:, :, :], AX.X, ALU.add))
            ch.need(t)
            nc.vector.tensor_scalar(stat[:, 1, :], stat[:, 1, :], 1.0 / F, 1e-5, ALU.mult, ALU.add).then_inc(s_neg, 1)
            dve.wait_ge(s_exp, 1)
            t = ch.did(nc.vector.reciprocal(stat[:, 2, :], stat[:, 2, :]))
            ch.need(t)
            ch.did(nc.vector.tensor_tensor(neg[:, :, :], node[:, :, :], stat[:, 2, :].unsqueeze(2).to_broadcast([P, NT, F]), ALU.mult))
            steps.append(ch.now())

        @block.tensor
        def _(pe):
            def add_tile(i, o):
                final = i == NT - 1
                pe.wait_ge(s_spread_last, 1) if final else pe.wait_ge(s_spread, i + 1)
                for b0, b1 in banks:
                    last = nc.tensor.matmul(add_ps[:, b0 * F:b1 * F], hot[:, o, :],
                                            spread[:, 2 if final else i % 2, b0:b1, :].rearrange("p t f -> p (t f)"),
                                            start=(i == 0), stop=(i == NT - 1))
                last.then_inc(s_added_all if final else s_added, 1)

            over_tiles(pe, pairs, add_tile)

        @block.scalar
        def _(act):
            act.wait_ge(s_neg, 1)
            if out is None:
                nc.scalar.activation(neg[:, :, :], neg[:, :, :], ACT.Exp).then_inc(s_exp, 1)
            else:
                nc.scalar.activation(stat[:, 2, :], stat[:, 1, :], ACT.Sqrt).then_inc(s_exp, 1)

        if out is not None:
            @block.sync
            def _(sp):
                sp.wait_ge(s_dve, steps[0])
                full = N // P
                sp.dma_start(out[0:full * P, :].rearrange("(t p) f -> p t f", p=P), neg[:, 0:full, :]).then_inc(s_out, 16)
                sp.dma_start(out[full * P:N, :], neg[0:N - full * P, full, :]).then_inc(s_out, 16)
                sp.wait_ge(s_out, 32)


def over_tiles(eng, pairs, step):
    used = used_pairs(eng, pairs)
    step(0, 0)
    for o in range(2, NT, 3):
        with eng.If(NT + o < used * 2):
            for each in range(o, min(o + 3, NT)):
                step(each - 1, each)
    step(NT - 1, 1)


def to_table(nc, sem, hid, x_nodes, table):
    stored = sem("table_stored")
    t = table.rearrange("(t p) f -> p t f", p=P)
    with nc.Block() as block:
        @block.sync
        def _(sp):
            sp.dma_start(t[:, :, 0:FH], hid[:, :, :]).then_inc(stored, 16)
            sp.dma_start(t[:, :, FH:HX], x_nodes[:, :, :]).then_inc(stored, 16)
            sp.wait_ge(stored, 32)


def conv(nc, sb, ps, sem, held, name, F, rec, moved, hat_consts, of_block, ident, pairs, blocks, weights, table, x_slots):
    NQ = P // Q
    UT = 1024 // (NQ * F)
    NU = TPB // UT
    R = 2 if table is not None else 4
    with ExitStack() as c:
        up, down = sb("up" + name, [P, TPB, D, KS], F32, c), sb("down" + name, [P, TPB, D, KS], F32, c)
        wt = sb("wt" + name, [K, F * F], F32, c)
        hat01 = sb("hat01" + name, [P, TPB, KS * KS], F32, c)
        basis = sb("basis" + name, [P, R, UT, K], F32, c)
        apart = sb("apart" + name, [P, R, UT, NQ, F], F32, c)
        wide = HX if table is not None else F
        feat = sb("feat" + name, [P, 2, TPB, wide], F32, c)
        agg = sb("agg" + name, [K, 2 * TPB, NQ, F], F32, c)
        rows_t = sb("rows_t" + name, [F, 2, NQ, TPB], F32, c)
        agg_ps = ps("agg_ps" + name, [P, 2, 1024], F32, c)
        rows_ps = ps("rows_ps" + name, [P, 512], F32, c)
        turned_ps = ps("turned_ps" + name, [P, 512], F32, c)
        unit_ready, unit_done, unit_copied, rows_ready, rows_copied, turned, weights_in, s_dve = [sem(n + name) for n in (
            "unit_ready_", "unit_done_", "unit_copied_", "rows_ready_", "rows_copied_", "turned_", "weights_in_", "dve_h_")]
        came = [sem("came0_" + name), sem("came1_" + name)]
        if table is not None:
            index = sb("index", [P, 2, TPB], I32, c)
            x_part = sb("x_part", [P, TPB, FIN], F32, c)
            x_ready, x_free, x_stored, index_ready = [sem(n) for n in ("x_ready", "x_free", "x_stored", "index_ready")]
        block = c.enter_context(nc.Block())

        @block.vector
        def _(dve):
            ch = Chain(nc.vector, s_dve)
            dve.sem_inc(unit_ready, 2 * NU)
            used = used_pairs(dve, pairs)
            ch.did(nc.vector.memset(up[:, :, :, :], 0.0))
            start, per = ch.n, 2 * (HATS + 2)
            with dve.Fori(0, BT // 2) as it, dve.If(it < used):
                ch.turn(start, it, per)
                for u in range(2):
                    c = it * 2 + u
                    e = bass.ds(c * TPB, TPB)
                    at = rec[:, e, A0:A0 + D] if moved is None else moved[:, e, :]
                    ch.need((s_dve, ch.now()))
                    t = hats(ch, at, [P, TPB, D, KS], hat_consts, up, down, up, rec[:, e, VALID])
                    hat = up
                    ch.need(t)
                    t = ch.did(nc.vector.tensor_tensor(hat01[:, :, :].rearrange("p t (a b) -> p t a b", a=KS),
                                                       hat[:, :, 0, :].unsqueeze(3).to_broadcast([P, TPB, KS, KS]),
                                                       hat[:, :, 1, :].unsqueeze(2).to_broadcast([P, TPB, KS, KS]),
                                                       ALU.mult))
                    ch.need(t)
                    dve.wait_ge(came[u], (it + 1) * (16 * (TPB if table is not None else 1)))
                    for i in range(NU):
                        ts = slice(i * UT, (i + 1) * UT)
                        dve.wait_ge(unit_done, c * NU + i + 1)
                        made = nc.vector.tensor_tensor(basis[:, i % R].rearrange("p t (a b) -> p t a b", b=KS),
                                                       hat01[:, ts, :].unsqueeze(3).to_broadcast([P, UT, KS * KS, KS]),
                                                       hat[:, ts, 2, :].unsqueeze(2).to_broadcast([P, UT, KS * KS, KS]),
                                                       ALU.mult)
                        if i == NU - 1:
                            ch.did(made)
                        nc.vector.tensor_tensor(apart[:, i % R], feat[:, u, ts, 0:F].unsqueeze(2).to_broadcast([P, UT, NQ, F]),
                                                of_block[:, :].unsqueeze(1).unsqueeze(3).to_broadcast([P, UT, NQ, F]),
                                                ALU.mult).then_inc(unit_ready, 1)
            ch.close(start, BT // 2, per)

        @block.scalar
        def _(act):
            act.dma_start(wt[:, :], weights.rearrange("k i o -> k (i o)")).then_inc(weights_in, 16)
            act.sem_inc(unit_copied, 2)
            if table is not None:
                act.sem_inc(x_ready, 2)
            used = used_pairs(act, pairs)
            with act.Fori(0, BT // 2) as it, act.If(it < used):
                for u in range(2):
                    c = it * 2 + u
                    if table is not None:
                        act.wait_ge(came[u], (it + 1) * (16 * TPB))
                        hold(act, x_free, c + 1, held["act"])
                        nc.scalar.copy(x_part[:, :, :], feat[:, u, :, FH:HX]).then_inc(x_ready, 1)
                    for i in range(NU):
                        act.wait_ge(unit_done, c * NU + i + R + 1)
                        nc.scalar.copy(agg[:, u * TPB + i * UT:u * TPB + (i + 1) * UT].rearrange("p t q f -> p (t q f)"),
                                       agg_ps[:K, i % 2, :]).then_inc(unit_copied, 1)
                act.wait_ge(rows_ready, it + 1)
                nc.scalar.copy(rows_t[:, :, :, :].rearrange("p u q t -> p u t q"),
                               rows_ps[:F, 0:2 * P].rearrange("p (u t q) -> p u t q", u=2, q=NQ)).then_inc(rows_copied, 1)
                hold(act, turned, it + 1, held["act"])
                nc.scalar.copy(blocks[:, bass.ds(it * 2, 2), 0:F], turned_ps[:, 0:2 * F].rearrange("p (t f) -> p t f", t=2))

        @block.tensor
        def _(pe):
            pe.sem_inc(unit_done, R)
            pe.wait_ge(weights_in, 16)
            used = used_pairs(pe, pairs)
            with pe.Fori(0, BT // 2) as it, pe.If(it < used):
                for u in range(2):
                    for i in range(NU):
                        g = (it * 2 + u) * NU + i
                        hold(pe, unit_ready, g + 2 * NU + 1, held["pe"])
                        hold(pe, unit_copied, g + 1, held["pe"])
                        for j in range(UT):
                            last = nc.tensor.matmul(agg_ps[:K, i % 2, j * NQ * F:(j + 1) * NQ * F], basis[:, i % R, j, :],
                                                    apart[:, i % R, j].rearrange("p q f -> p (q f)"), start=True, stop=True)
                        last.then_inc(unit_done, 1)
                hold(pe, unit_copied, it * (2 * NU) + 2 * NU + 2, held["pe"])
                flat = agg[:, :, :, :].rearrange("p t q f -> p (t q) f")
                for f in range(F):
                    last = nc.tensor.matmul(rows_ps[:F, 0:2 * P], wt[:, f * F:(f + 1) * F], flat[:, :, f],
                                            start=(f == 0), stop=(f == F - 1))
                last.then_inc(rows_ready, 1)
                hold(pe, rows_copied, it + 1, held["pe"])
                for u in range(2):
                    last = nc.tensor.transpose(turned_ps[:, u * F:(u + 1) * F], rows_t[:, u].rearrange("p q t -> p (q t)"),
                                               ident[:F, :F])
                last.then_inc(turned, 1)

        if table is not None:
            @block.gpsimd
            def _(pool):
                used = used_pairs(pool, pairs)
                with pool.Fori(0, BT // 2) as it, pool.If(it < used):
                    for u in range(2):
                        c = it * 2 + u
                        hold(pool, unit_ready, c * NU + NU, held["pool"])
                        hold(pool, x_ready, c + 1, held["pool"])
                        nc.gpsimd.tensor_copy(index[:, u, :], rec[:, bass.ds(c * TPB, TPB), COL]).then_inc(index_ready, 1)
                        hold(pool, index_ready, c + 1, held["pool"])
                        for j in range(TPB):
                            pool.indirect_dma_start(feat[:, u, j, :], None, table,
                                                    bass.IndirectOffsetOnAxis(ap=index[:, u, j:j + 1], axis=0)).then_inc(came[u], 16)

            @block.sync
            def _(sp):
                sp.sem_inc(x_free, 1)
                used = used_pairs(sp, pairs)
                with sp.Fori(0, BT // 2) as it, sp.If(it < used):
                    for u in range(2):
                        c = it * 2 + u
                        hold(sp, x_ready, c + 3, held["sp"])
                        sp.dma_start(x_slots[:, bass.ds(c * (TPB * FIN), TPB * FIN)],
                                     x_part[:, :, :].rearrange("p t f -> p (t f)")).then_inc(x_stored, 16)
                        hold(sp, x_stored, c * 16 + 16, held["sp"])
                        sp.sem_inc(x_free, 1)
        else:
            @block.sync
            def _(sp):
                used = used_pairs(sp, pairs)
                with sp.Fori(0, BT // 2) as it, sp.If(it < used):
                    for u in range(2):
                        c = it * 2 + u
                        hold(sp, unit_ready, c * NU + NU, held["sp"])
                        sp.dma_start(feat[:, u].rearrange("p t f -> p (t f)"),
                                     x_slots[:, bass.ds(c * (TPB * FIN), TPB * FIN)]).then_inc(came[u], 16)


def used_pairs(eng, pairs):
    return eng.value_load(pairs[0:1, 0:1], min_val=1, max_val=BT // 2)


def t_node(nc, sb, ps, sem, held, hid, wt3, bt3, wt4, bt4, ident, ovn_i, t_nodes, t_blocks, rec, moved, iota, npid, one, pairs):
    with ExitStack() as cc:
        t_sb = sb("t_sb", [P, BT, D], F32, cc)
        with ExitStack() as c:
            hid_t = sb("hid_t", [FH, NT * P], F32, c)
            pos, neg, act3 = [sb(n, [FH, NT * P], F32, c) for n in ("t_pos", "t_neg", "act3")]
            tr_ps = ps("tr_ps", [P, 2, 512], F32, c)
            w3_ps = ps("w3_ps", [P, 2, 512], F32, c)
            w4_ps = ps("w4_ps", [P, 512], F32, c)
            s_tr, s_trc, s_w3, s_neg, s_exp, s_act3, s_w4, s_dve, s_tsb, s_st, s_st2, s_ov = [sem("t_" + n) for n in (
                "transposed", "transposed_copied", "w3_ready", "neg_ready", "exp_ready", "act3_ready", "w4_ready", "dve", "sb", "stored", "stored2", "overflow_in")]
            GR = [(i, min(i + 4, NT)) for i in range(0, NT, 4)]
            block = c.enter_context(nc.Block())

            @block.tensor
            def _(pe):
                for i, (a, b) in enumerate(GR):
                    if i >= 2:
                        pe.wait_ge(s_trc, i - 1)
                    for n in range(a, b):
                        last = nc.tensor.transpose(tr_ps[0:FH, i % 2, (n - a) * P:(n - a + 1) * P], hid[:, n, :], ident[:, :])
                    last.then_inc(s_tr, 1)
                for i, (a, b) in enumerate(GR):
                    pe.wait_ge(s_trc, i + 1)
                    if i >= 2:
                        pe.wait_ge(s_neg, i - 1)
                    nc.tensor.matmul(w3_ps[0:FH, i % 2, 0:(b - a) * P], wt3[:, :], hid_t[:, a * P:b * P],
                                     start=True, stop=True).then_inc(s_w3, 1)
                pe.wait_ge(s_act3, len(GR))
                for n in range(NT):
                    last = nc.tensor.matmul(w4_ps[:, n * D:(n + 1) * D], act3[:, n * P:(n + 1) * P], wt4[:, :], start=True, stop=True)
                last.then_inc(s_w4, 1)

            @block.scalar
            def _(act):
                for i, (a, b) in enumerate(GR):
                    act.wait_ge(s_tr, i + 1)
                    nc.scalar.copy(hid_t[:, a * P:b * P], tr_ps[0:FH, i % 2, 0:(b - a) * P]).then_inc(s_trc, 1)
                for i, (a, b) in enumerate(GR):
                    act.wait_ge(s_neg, i + 1)
                    nc.scalar.activation(neg[:, a * P:b * P], neg[:, a * P:b * P], ACT.Exp).then_inc(s_exp, 1)

            @block.vector
            def _(dve):
                for i, (a, b) in enumerate(GR):
                    dve.wait_ge(s_w3, i + 1)
                    y = w3_ps[0:FH, i % 2, 0:(b - a) * P]
                    nc.vector.tensor_scalar(pos[:, a * P:b * P], y, bt3[:, :], 0.0, ALU.add, ALU.max)
                    nc.vector.tensor_scalar(neg[:, a * P:b * P], y, bt3[:, :], 0.0, ALU.add, ALU.min).then_inc(s_neg, 1)
                for i, (a, b) in enumerate(GR):
                    dve.wait_ge(s_exp, i + 1)
                    nc.vector.scalar_tensor_tensor(out=act3[:, a * P:b * P], in0=neg[:, a * P:b * P], scalar=-1.0,
                                                   in1=pos[:, a * P:b * P], op0=ALU.add, op1=ALU.add).then_inc(s_act3, 1)
                dve.wait_ge(s_w4, 1)
                nc.vector.tensor_tensor(t_sb[:, 0:NT, :], w4_ps[:, 0:NT * D].rearrange("p (t d) -> p t d", d=D),
                                        bt4[:, :].unsqueeze(1).to_broadcast([P, NT, D]), ALU.add).then_inc(s_tsb, 1)

            @block.sync
            def _(sp):
                sp.wait_ge(s_tsb, 1)
                sp.dma_start(t_nodes.rearrange("(t p) d -> p t d", p=P), t_sb[:, 0:NT, :]).then_inc(s_st, 16)
                sp.wait_ge(s_ov, 16 * NT)
                sp.dma_start(t_blocks, t_sb[:, :, :].rearrange("p t d -> p (t d)")).then_inc(s_st2, 16)
                sp.wait_ge(s_st2, 16)

            @block.gpsimd
            def _(pool):
                pool.wait_ge(s_st, 16)
                for o in range(NT):
                    pool.indirect_dma_start(t_sb[:, NT + o, :], None, t_nodes,
                                            bass.IndirectOffsetOnAxis(ap=ovn_i[:, o:o + 1], axis=0)).then_inc(s_ov, 16)
                pool.wait_ge(s_ov, 16 * NT)

        with ExitStack() as c:
            C = AHEAD
            G = 2 * TPB // C
            t_quad = sb("t_quad", [P // Q, ST * D], F32, c)
            expand = sb("expand", [P // Q, P], F32, c)
            ident_b = sb("ident_b", [P, P], BF16, c)
            t_part = sb("t_part", [P, 3, NT * D], BF16, c)
            t_rest = sb("t_rest", [P, 2, NT * D], F32, c)
            low = sb("low", [P, 2, C], BF16, c)
            hi_mask = sb("hi_mask3", [P, 2, C, NT], F32, c)
            away = sb("away3", [P, 2, C, P], BF16, c)
            hot = sb("hot3", [P, 2, C, P], BF16, c)
            masked = sb("masked3", [P, 2, C, NT, D], F32, c)
            low_ready, bc_ready, hot_ready, got_ready, masked_ready, s_act, s_dve, s_pool, s_quad, s_red, s_part = [sem("e_" + n) for n in (
                "low_ready", "bc_ready", "hot_ready", "got_ready", "masked_ready", "act", "dve", "pool", "quad_in", "reduced", "part")]
            with ExitStack() as pc:
                lo_bc = ps("lo_bc3", [P, 2, C, P], BF16, pc)
                got = ps("got", [P, 2, C, P], F32, pc)
                block = pc.enter_context(nc.Block())

                @block.sync
                def _(sp):
                    for q in range(P // Q):
                        sp.dma_start(t_quad[q:q + 1, :].rearrange("o (b j d) -> o b j d", b=BT, d=D),
                                     t_blocks[q * Q:(q + 1) * Q, :].rearrange("j (b d) -> b j d", d=D).unsqueeze(0)).then_inc(s_quad, 16)
                    sp.wait_ge(s_quad, 64)

                @block.gpsimd
                def _(pool):
                    ch = Chain(nc.gpsimd, s_pool)
                    t = ch.did(nc.gpsimd.memset(expand[:, :], 1.0))
                    ch.need(t)
                    t = ch.did(nc.gpsimd.affine_select(out=expand[:, :], in_=expand[:, :], compare_op=ALU.is_ge, fill=0.0,
                                                       base=0, pattern=[[1, P]], channel_multiplier=-Q))
                    ch.need(t)
                    ch.did(nc.gpsimd.affine_select(out=expand[:, :], in_=expand[:, :], compare_op=ALU.is_ge, fill=0.0,
                                                   base=Q - 1, pattern=[[-1, P]], channel_multiplier=Q))
                    used = used_pairs(pool, pairs)
                    nc.gpsimd.tensor_copy(low[:, 0, :], rec[:, 0:C, CLO]).then_inc(low_ready, 1)
                    with pool.Fori(0, BT // 2) as it, pool.If(it < used):
                        for i in range(1, G + 1):
                            g = it * G + i
                            hold(pool, bc_ready, g + 1, held["pool"])
                            nc.gpsimd.tensor_copy(low[:, i % 2, :], rec[:, bass.ds(g * C, C), CLO]).then_inc(low_ready, 1)

                @block.tensor
                def _(pe):
                    pe.sem_inc(bc_ready, 2)
                    pe.wait_ge(s_part, 5)

                    def turn_low(g, u):
                        hold(pe, low_ready, g + 1, held["pe"])
                        hold(pe, hot_ready, g + 1, held["pe"])
                        for j in range(C):
                            last = nc.tensor.transpose(lo_bc[:, u, j, :], low[:, u, j:j + 1].to_broadcast([P, P]), ident_b[:, :])
                        last.then_inc(bc_ready, 1)

                    def fetch(g, u):
                        hold(pe, hot_ready, g + 3, held["pe"])
                        hold(pe, masked_ready, g + 1, held["pe"])
                        for j in range(C):
                            for part in range(3):
                                last = nc.tensor.matmul(got[:, u, j, 0:NT * D], hot[:, u, j, :], t_part[:, part, :],
                                                        start=(part == 0), stop=(part == 2))
                        last.then_inc(got_ready, 1)

                    used = used_pairs(pe, pairs)
                    turn_low(0, 0)
                    with pe.Fori(0, BT // 2) as it, pe.If(it < used):
                        for i in range(G):
                            turn_low(it * G + i + 1, (i + 1) % 2)
                            fetch(it * G + i, i % 2)

                @block.scalar
                def _(act):
                    act.sem_inc(hot_ready, 2)
                    ch = Chain(nc.scalar, s_act)
                    used = used_pairs(act, pairs)
                    with act.Fori(0, BT // 2) as it, act.If(it < used):
                        ch.turn(0, it, G)
                        for i in range(G):
                            g, u = it * G + i, i % 2
                            act.wait_ge(bc_ready, g + 3)
                            t = ch.did(nc.scalar.activation(away[:, u], lo_bc[:, u], ACT.Abs, bias=npid[:, :]))
                            act.wait_ge(got_ready, g + 1)
                            ch.need(t)
                            nc.scalar.activation(hot[:, u], away[:, u], ACT.Relu, scale=-1.0, bias=one[:, :]).then_inc(hot_ready, 1)

                @block.vector
                def _(dve):
                    dve.sem_inc(masked_ready, 2)
                    dve.sem_inc(got_ready, 2)
                    ch = Chain(nc.vector, s_part)
                    t_flat = t_sb[:, 0:NT, :].rearrange("p t d -> p (t d)")
                    t = ch.did(nc.vector.tensor_copy(t_part[:, 0, :], t_flat))
                    ch.need(t)
                    t = ch.did(nc.vector.tensor_tensor(t_rest[:, 0, :], t_flat, t_part[:, 0, :], ALU.subtract))
                    ch.need(t)
                    t = ch.did(nc.vector.tensor_copy(t_part[:, 1, :], t_rest[:, 0, :]))
                    ch.need(t)
                    nc.vector.memset(moved[:, :, :], 0.0)
                    nc.vector.tensor_copy(ident_b[:, :], ident[:, :])
                    t = ch.did(nc.vector.tensor_tensor(t_rest[:, 1, :], t_rest[:, 0, :], t_part[:, 1, :], ALU.subtract))
                    ch.need(t)
                    t = ch.did(nc.vector.tensor_copy(t_part[:, 2, :], t_rest[:, 1, :]))
                    ch.need(t)
                    ch = Chain(nc.vector, s_dve)
                    used = used_pairs(dve, pairs)
                    with dve.Fori(0, BT // 2) as it, dve.If(it < used):
                        ch.turn(0, it, G)
                        for i in range(G):
                            g, u = it * G + i, i % 2
                            t = ch.did(nc.vector.tensor_tensor(hi_mask[:, u], iota[:, 0:NT].unsqueeze(1).to_broadcast([P, C, NT]),
                                                               rec[:, bass.ds(g * C, C), CHI].unsqueeze(2).to_broadcast([P, C, NT]),
                                                               ALU.is_equal))
                            ch.need(t)
                            dve.wait_ge(got_ready, g + 3)
                            nc.vector.tensor_tensor(masked[:, u], got[:, u, :, 0:NT * D].rearrange("p c (h d) -> p c h d", d=D),
                                                    hi_mask[:, u].unsqueeze(3).to_broadcast([P, C, NT, D]), ALU.mult).then_inc(masked_ready, 1)
                            dve.wait_ge(masked_ready, g + 3)
                            nc.vector.tensor_reduce(moved[:, bass.ds(g * C, C), :], masked[:, u].rearrange("p c h d -> p c d h"), AX.X, ALU.add)

            with ExitStack() as pc:
                row_t = ps("row_t", [P, 8, 512], F32, pc)
                s_row, s_new, s_ch = sem("row_t_ready"), sem("new_ready"), sem("dve_n")
                CW = 480
                block = pc.enter_context(nc.Block())
                CH = ST * D // CW

                @block.tensor
                def _(pe):
                    for i in range(CH):
                        if i >= 8:
                            pe.wait_ge(s_new, i - 7)
                        nc.tensor.matmul(row_t[:, i % 8, 0:CW], expand[:, :], t_quad[:, i * CW:(i + 1) * CW], start=True, stop=True).then_inc(s_row, 1)

                @block.vector
                def _(dve):
                    ch = Chain(nc.vector, s_ch)
                    t = ch.did(nc.vector.scalar_tensor_tensor(out=moved[:, :, :], in0=rec[:, 0:ST, A0:A0 + D], scalar=1.0 / (KS - 1),
                                                              in1=moved[:, :, :], op0=ALU.mult, op1=ALU.add))
                    ch.need(t)
                    flat = moved[:, :, :].rearrange("p t d -> p (t d)")
                    for i in range(CH):
                        dve.wait_ge(s_row, i + 1)
                        nc.vector.tensor_tensor(flat[:, i * CW:(i + 1) * CW], flat[:, i * CW:(i + 1) * CW], row_t[:, i % 8, 0:CW],
                                                ALU.subtract).then_inc(s_new, 1)
                    dve.wait_ge(s_new, CH)
                    t = ch.did(nc.vector.tensor_scalar(flat, flat, 0.0, 1.0, ALU.max, ALU.min))
                    ch.need(t)
                    ch.did(nc.vector.tensor_scalar(flat, flat, float(KS - 1), None, ALU.mult))


_INS = ["x", "src", "dst", "edge_attr_3"] + ["L0_gnn_" + n for n in (
    "stn1_w", "stn1_b", "stn2_w", "stn2_b", "stn3_w", "stn3_b", "stn4_w", "stn4_b", "conv_w", "conv_b")]


def kernel(**inputs):
    import numpy as np
    import concourse.bacc as bacc
    from concourse.bass_utils import run_bass_kernel_spmd

    nc = bacc.Bacc("TRN2", target_bir_lowering=False, num_devices=1)
    arrays, args = {}, []
    for name in _INS:
        a = np.ascontiguousarray(inputs[name])
        arrays[f"in_{name}"] = a
        args.append(nc.dram_tensor(f"in_{name}", a.shape, mybir.dt.from_np(a.dtype), kind="ExternalInput").ap())
    args.append(nc.dram_tensor("out", (N, FIN), F32, kind="ExternalOutput").ap())
    spline_net(nc, *args)
    r = run_bass_kernel_spmd(nc, [arrays], core_ids=[0])
    return r.results[0]["out"]
```

```python
import concourse.bass as bass
from concourse import mybir
from contextlib import ExitStack

F32 = mybir.dt.float32
BF16 = mybir.dt.bfloat16
I32 = mybir.dt.int32
ALU = mybir.AluOpType
ACT = mybir.ActivationFunctionType
AX = mybir.AxisListType

P = 128
N, FIN, FH = 3125, 32, 64
E, D = 100000, 3
KS = 5
K = KS ** D
NT = -(-N // P)
EP, ET = 125, E // 125
Q = 32
OV0 = NT * P
BT = 2 * NT
assert -(-E // Q) <= NT * P
TPB = P // (P // Q)
ST = BT * TPB
W = 8
A0, VALID, COL, ROW, CLO, CHI = 0, 3, 4, 5, 6, 7
HX = FH + FIN
BIG = 3.0e38
AHEAD = 2 * 2 * TPB


class Chain:

    def __init__(self, eng, sem):
        self.eng, self.sem, self.base, self.n = eng, sem, 0, 0

    def did(self, ins):
        ins.then_inc(self.sem, 1)
        self.n += 1
        return self.sem, self.base + self.n

    def need(self, ticket):
        self.eng.wait_ge(*ticket)

    def turn(self, start, it, per):
        self.base, self.n = start + it * per, 0

    def close(self, start, turns, per):
        assert self.n == per, (self.n, per)
        self.base, self.n = start + turns * per, 0

    def now(self):
        return self.base + self.n


def hold(eng, sem, value, held):
    eng.wait_ge(sem, value)
    eng.sem_inc(held, 1)


def spline_net(nc, x, src, dst, attr, w1, b1, w2, b2, w3, b3, w4, b4, wc, bc, out):
    with ExitStack() as ctx:
        def sb(name, shape, dt=F32, c=ctx):
            return c.enter_context(nc.sbuf_tensor(name, shape, dt))

        def ps(name, shape, dt=F32, c=ctx):
            return c.enter_context(nc.psum_tensor(name, shape, dt))

        def sem(name):
            return ctx.enter_context(nc.semaphore(name))

        slots = nc.dram_tensor("slots", (P * ST, W), F32, kind="Internal").ap()
        held = {e: sem(f"held_{e}") for e in ("pe", "act", "dve", "pool", "sp")}

        iota = sb("iota", [P, P])
        pid = sb("pid", [P, 1])
        npid = sb("npid", [P, 1])
        one = sb("one", [P, 1])
        ident = sb("ident", [P, P])
        deg = sb("deg", [P, NT])
        pairs = sb("pairs", [P, 1], I32)

        with ExitStack() as ab:
            place_edges(nc, ab, sb, ps, sem, held, src, dst, attr, slots, iota, pid, npid, one, ident, deg, pairs)

        rec = sb("rec", [P, ST + AHEAD, W])
        blocks = sb("blocks", [P, BT, FH])
        hid = sb("hid", [P, NT, FH])
        x_nodes = sb("x_nodes", [P, NT, FIN])
        wt3, wt4 = sb("wt3", [FH, FH]), sb("wt4", [FH, D])
        bt1, bt2, btc, bt4 = sb("bt1", [P, FH]), sb("bt2", [P, FH]), sb("btc", [P, FIN]), sb("bt4", [P, D])
        bt3 = sb("bt3", [FH, 1])
        ovn, ov_lo, ov_hi = sb("ovn", [P, NT]), sb("ov_lo", [P, NT]), sb("ov_hi", [P, NT])
        ovn_i, ov_i = sb("ovn_i", [P, NT], I32), sb("ov_i", [P, NT], I32)
        inv_degree = sb("inv_degree", [P, NT])
        of_block = sb("of_block", [P, P // Q])
        up_c, down_c, up_floor, down_floor = [sb(n, [P, D, KS]) for n in ("up_c", "down_c", "up_floor", "down_floor")]
        table = nc.dram_tensor("table", (NT * P, HX), F32, kind="Internal").ap()
        x_slots = nc.dram_tensor("x_slots", (P, ST * FIN), F32, kind="Internal").ap()
        t_nodes = nc.dram_tensor("t_nodes", (NT * P, D), F32, kind="Internal").ap()
        t_blocks = nc.dram_tensor("t_blocks", (P, BT * D), F32, kind="Internal").ap()

        hat_consts = (up_c, down_c, up_floor, down_floor)
        first_layer(nc, sb, ps, sem, held, locals())
        gather_overflow(nc, sb, ps, sem, held, iota, blocks, pairs, ov_lo, ov_hi, inv_degree, bt1, FH, hid, "one")
        to_table(nc, sem, hid, x_nodes, table)
        conv(nc, sb, ps, sem, held, rec, hat_consts, of_block, ident, pairs, blocks, w2, table, x_slots)
        gather_overflow(nc, sb, ps, sem, held, iota, blocks, pairs, ov_lo, ov_hi, inv_degree, bt2, FH, hid, "two")
        with ExitStack() as c3:
            t_row = sb("t_row", [P, ST + 2 * TPB, D], F32, c3)
            t_sb = sb("t_sb", [P, BT, D], F32, c3)
            t_node(nc, sb, ps, sem, hid, wt3, bt3, wt4, bt4, ident, t_sb, t_nodes)
            last_conv(nc, sb, ps, sem, held, rec, ovn_i, t_sb, t_nodes, t_blocks, t_row, hat_consts, of_block, ident, iota, npid, one, pairs,
                      blocks, wc, x_slots)
        gather_overflow(nc, sb, ps, sem, held, iota, blocks, pairs, ov_lo, ov_hi, inv_degree, btc, FIN, None, "three",
                        x_nodes, out)




def place_edges(nc, ab, sb, ps, sem, held, src, dst, attr, slots, iota, pid, npid, one, ident, deg, pairs):
    G = 20
    GN = ET // G
    GD = 17
    TAIL = (G - GD) * P + G * NT
    C = 8
    SC = 16
    SN, CN = ET // SC, SC // C
    BC = 2 * CN

    iota_i = sb("iota_i", [P, P], I32, ab)
    pid_i = sb("pid_i", [P, 1], I32, ab)
    lower = sb("lower", [P, P], F32, ab)
    upper = sb("upper", [P, P], F32, ab)
    ones = sb("ones", [P, P], F32, ab)
    zeros = sb("zeros", [P, ST], F32, ab)
    src_i = sb("src_i", [EP, ET], I32, ab)
    dst_i = sb("dst_i", [EP, ET], I32, ab)
    tmp_i = sb("tmp_i", [EP, ET], I32, ab)
    edge_attr = sb("edge_attr", [EP, ET * D], F32, ab)
    row = sb("row", [EP, ET + G], F32, ab)
    row_lo = sb("row_lo", [EP, ET + G], F32, ab)
    row_hi = sb("row_hi", [EP, ET + G], F32, ab)
    hot = sb("hot", [EP, 2, G * (P + NT)], BF16, ab)
    diff = sb("diff", [EP, 2, TAIL], BF16, ab)
    diff_abs = sb("diff_abs", [EP, 2, TAIL], BF16, ab)
    before = sb("before", [P, ET + 1, NT], F32, ab)
    onescan = sb("onescan", [P, ET], F32, ab)
    over_i = sb("over_i", [P, NT], I32, ab)
    over = sb("over", [P, NT], F32, ab)
    over_at = sb("over_at", [P, NT], F32, ab)
    hi_sum = sb("hi_sum", [P, NT], F32, ab)

    src_in, dst_in, attr_in, cleared = sem("src_in"), sem("dst_in"), sem("attr_in"), sem("cleared")
    zero_ready, const_ready, hot_ready, hist_ready = sem("zero_ready"), sem("const_ready"), sem("hot_ready"), sem("hist_ready")
    hist_free, dve_a, pool_a, over_ready, pre_ready = sem("hist_free"), sem("dve_a"), sem("pool_a"), sem("over_ready"), sem("pre_ready")

    rows_ready, diff_ready, tail_ready, act_a = sem("rows_ready"), sem("diff_ready"), sem("tail_ready"), sem("act_a")

    with ExitStack() as pa:
        hist = ps("hist", [P, 2, 512], F32, pa)
        over_ps = ps("over_ps", [P, 512], F32, pa)
        block = pa.enter_context(nc.Block())

        @block.sync
        def _(sp):
            sp.dma_start(src_i[:, :], src.rearrange("(p t) -> p t", p=EP)).then_inc(src_in, 16)
            sp.dma_start(dst_i[:, :], dst.rearrange("(p t) -> p t", p=EP)).then_inc(dst_in, 16)
            sp.dma_start(edge_attr[:, :], attr.rearrange("(p t) d -> p (t d)", p=EP)).then_inc(attr_in, 16)
            sp.wait_ge(zero_ready, 1)
            sp.dma_start(slots.rearrange("(p w t) c -> p w (t c)", p=P, w=W),
                         zeros[:, :].unsqueeze(1).to_broadcast([P, W, ST])).then_inc(cleared, 16)
            sp.wait_ge(cleared, 16)

        @block.gpsimd
        def _(pool):
            ch = Chain(pool, pool_a)
            pool.iota(iota_i[:, :], [[1, P]], base=0, channel_multiplier=0)
            pool.iota(pid_i[:, :], [[0, 1]], base=0, channel_multiplier=1)
            nc.gpsimd.memset(ones[:, :], 1.0)
            t = ch.did(nc.gpsimd.memset(ident[:, :], 0.0))
            ch.need(t)
            ch.did(nc.gpsimd.affine_select(out=ident[:, :], in_=ident[:, :], compare_op=ALU.not_equal, fill=1.0,
                                           base=0, pattern=[[-1, P]], channel_multiplier=1))
            ch.did(nc.gpsimd.affine_select(out=lower[:, :], in_=ones[:, :], compare_op=ALU.is_gt, fill=0.0,
                                           base=0, pattern=[[-1, P]], channel_multiplier=1))
            t = ch.did(nc.gpsimd.affine_select(out=upper[:, :], in_=ones[:, :], compare_op=ALU.is_gt, fill=0.0,
                                               base=0, pattern=[[1, P]], channel_multiplier=-1))
            ch.need(t)
            nc.gpsimd.memset(one[:, :], 1.0).then_inc(const_ready, 1)
            pool.wait_ge(rows_ready, 1)

            def subtract(g, u):
                hold(pool, tail_ready, g + 1, held["pool"])
                nc.gpsimd.tensor_tensor(diff[:, u, 0:(G - GD) * P].rearrange("p (t n) -> p t n", n=P),
                                        iota[:EP, :].unsqueeze(1).to_broadcast([EP, G - GD, P]),
                                        row_lo[:, bass.ds(g * G + GD, G - GD)].unsqueeze(2).to_broadcast([EP, G - GD, P]),
                                        ALU.subtract).then_inc(diff_ready, 1)
                nc.gpsimd.tensor_tensor(diff[:, u, (G - GD) * P:TAIL].rearrange("p (t n) -> p t n", n=NT),
                                        iota[:EP, 0:NT].unsqueeze(1).to_broadcast([EP, G, NT]),
                                        row_hi[:, bass.ds(g * G, G)].unsqueeze(2).to_broadcast([EP, G, NT]),
                                        ALU.subtract).then_inc(diff_ready, 1)

            subtract(0, 0)
            with pool.Fori(0, GN // 2) as it:
                for u in range(2):
                    subtract(it * 2 + u + 1, 1 - u)

        @block.vector
        def _(dve):
            ch = Chain(dve, dve_a)
            nc.vector.memset(zeros[:, :], 0.0).then_inc(zero_ready, 1)
            nc.vector.memset(onescan[:, :], 1.0)
            for of in (row, row_lo, row_hi):
                nc.vector.memset(of[:, ET:ET + G], 0.0)
            nc.vector.memset(before[:, 0, :], 0.0)
            dve.wait_ge(src_in, 16)
            t = ch.did(nc.vector.tensor_scalar(tmp_i[:, :], src_i[:, :], P - 1, None, ALU.bitwise_and))
            nc.vector.tensor_copy(row[:, 0:ET], src_i[:, :])
            ch.need(t)
            t = ch.did(nc.vector.tensor_copy(row_lo[:, 0:ET], tmp_i[:, :]))
            ch.need(t)
            t = ch.did(nc.vector.tensor_scalar(tmp_i[:, :], src_i[:, :], 7, None, ALU.arith_shift_right))
            ch.need(t)
            ch.did(nc.vector.tensor_copy(row_hi[:, 0:ET], tmp_i[:, :]))
            dve.wait_ge(const_ready, 1)
            ch.did(nc.vector.tensor_copy(iota[:, :], iota_i[:, :]))
            t = ch.did(nc.vector.tensor_copy(pid[:, :], pid_i[:, :]))
            ch.need(t)
            t = ch.did(nc.vector.tensor_scalar(npid[:, :], pid[:, :], -1.0, None, ALU.mult))
            ch.need(t)
            dve.sem_inc(rows_ready, 1)
            with dve.Fori(0, GN // 2) as it:
                for u in range(2):
                    g = it * 2 + u
                    dve.wait_ge(hist_ready, g + 1)
                    nc.vector.tensor_tensor(hot[:, u, 0:GD * P].rearrange("p (t n) -> p t n", n=P),
                                            iota[:EP, :].unsqueeze(1).to_broadcast([EP, GD, P]),
                                            row_lo[:, bass.ds(g * G, GD)].unsqueeze(2).to_broadcast([EP, GD, P]),
                                            ALU.is_equal).then_inc(hot_ready, 1)
            dve.wait_ge(hist_free, GN + 2)
            for h in range(NT):
                last = ch.did(nc.vector.tensor_tensor_scan(before[:, 1:ET + 1, h], onescan[:, :], before[:, 1:ET + 1, h],
                                                           0.0, ALU.mult, ALU.add))
            ch.need(last)
            t = ch.did(nc.vector.tensor_copy(deg[:, :], before[:, ET, :]))
            ch.need(t)
            t = ch.did(nc.vector.tensor_scalar(over[:, :], deg[:, :], -1.0, 0.0, ALU.add, ALU.max))
            ch.need(t)
            t = ch.did(nc.vector.tensor_copy(over_i[:, :], over[:, :]))
            ch.need(t)
            t = ch.did(nc.vector.tensor_scalar(over_i[:, :], over_i[:, :], 5, None, ALU.arith_shift_right))
            ch.need(t)
            nc.vector.tensor_copy(over[:, :], over_i[:, :]).then_inc(over_ready, 1)
            dve.wait_ge(pre_ready, 1)
            t = ch.did(nc.vector.tensor_tensor_scan(hi_sum[:, :], onescan[:, 0:NT], over_ps[:, NT:2 * NT],
                                                    0.0, ALU.mult, ALU.add))
            ch.need(t)
            t = ch.did(nc.vector.tensor_scalar(pairs[:, :], hi_sum[:, NT - 1:NT], float(OV0 + 2 * P - 1), None, ALU.add))
            ch.need(t)
            ch.did(nc.vector.tensor_scalar(pairs[:, :], pairs[:, :], 8, None, ALU.arith_shift_right))
            t = ch.did(nc.vector.tensor_tensor(over_at[:, :], hi_sum[:, :], over_ps[:, NT:2 * NT], ALU.subtract))
            ch.need(t)
            t = ch.did(nc.vector.scalar_tensor_tensor(out=over_at[:, :], in0=over_at[:, :], scalar=float(OV0 - 1),
                                                      in1=over_ps[:, 0:NT], op0=ALU.add, op1=ALU.add))
            ch.need(t)

        @block.tensor
        def _(pe):
            pe.sem_inc(hist_ready, 2)
            with pe.Fori(0, GN // 2) as it:
                for u in range(2):
                    g = it * 2 + u
                    hold(pe, hot_ready, g + 1, held["pe"])
                    hold(pe, tail_ready, g + 3, held["pe"])
                    hold(pe, hist_free, g + 1, held["pe"])
                    for j in range(G):
                        last = nc.tensor.matmul(hist[:, u, j * NT:(j + 1) * NT], hot[:, u, j * P:(j + 1) * P],
                                                hot[:, u, G * P + j * NT:G * P + (j + 1) * NT],
                                                start=True, stop=True)
                    last.then_inc(hist_ready, 1)
            pe.wait_ge(over_ready, 1)
            nc.tensor.matmul(over_ps[:, 0:NT], upper[:, :], over[:, :], start=True, stop=True)
            nc.tensor.matmul(over_ps[:, NT:2 * NT], ones[:, :], over[:, :], start=True, stop=True).then_inc(pre_ready, 1)

        @block.scalar
        def _(act):
            act.sem_inc(hist_free, 2)
            act.sem_inc(tail_ready, 2)
            ch = Chain(act, act_a)
            act.wait_ge(const_ready, 1)

            def one_hot(g, u):
                hold(act, diff_ready, g * 2 + 2, held["act"])
                t = ch.did(nc.scalar.activation(diff_abs[:, u], diff[:, u], ACT.Abs))
                hold(act, hist_ready, g + 1, held["act"])
                ch.need(t)
                nc.scalar.activation(hot[:, u, GD * P:], diff_abs[:, u], ACT.Relu, scale=-1.0,
                                     bias=one[:EP, :]).then_inc(tail_ready, 1)

            one_hot(0, 0)
            with act.Fori(0, GN // 2) as it:
                ch.turn(1, it, 2)
                for u in range(2):
                    g = it * 2 + u
                    one_hot(g + 1, 1 - u)
                    hold(act, hist_ready, g + 3, held["act"])
                    nc.scalar.copy(before[:, bass.ds(g * G + 1, G), :].rearrange("p t h -> p (t h)"),
                                   hist[:, u, 0:G * NT]).then_inc(hist_free, 1)

    record = sb("record", [EP, 2, SC, W], F32, ab)
    slot_i = sb("slot_i", [EP, 2, SC], I32, ab)
    col_row = sb("col_row", [EP, 2, C], F32, ab)
    col_lo_b = sb("col_lo_b", [EP, 2, C], BF16, ab)
    ident_ab = sb("ident_ab", [P, P], BF16, ab)
    places = sb("places", [P, 2, C, 2, NT], F32, ab)
    col_f = sb("col_f", [EP, ET], F32, ab)
    col_lo = sb("col_lo", [EP, ET], F32, ab)
    col_hi = sb("col_hi", [EP, ET], F32, ab)
    hot_t = sb("hot_t", [P, 2, C, P], F32, ab)
    away = sb("away", [P, 2, C, P], BF16, ab)
    junk = sb("junk", [EP, C, P], BF16, ab)
    hi_mask = sb("hi_mask", [EP, C, NT], F32, ab)
    masked = sb("masked", [EP, C, 2, NT], F32, ab)
    within = sb("within", [EP, SC], F32, ab)
    found = sb("found", [EP, SC, 2], F32, ab)
    rank = sb("rank", [EP, SC], F32, ab)
    rank_i = sb("rank_i", [EP, SC], I32, ab)
    q_i = sb("q_i", [EP, SC], I32, ab)
    r_i = sb("r_i", [EP, SC], I32, ab)
    qf = sb("qf", [EP, SC], F32, ab)
    rf = sb("rf", [EP, SC], F32, ab)
    far = sb("far", [EP, SC], F32, ab)
    blk_i = sb("blk_i", [EP, SC], I32, ab)
    part_i = sb("part_i", [EP, 3, SC], I32, ab)
    part = sb("part", [EP, 3, SC], F32, ab)

    cols_ready, bc_ready, hot_t_ready, found_ready, lookup_free = [sem(n) for n in (
        "cols_ready", "bc_ready", "hot_t_ready", "found_ready", "lookup_free")]
    dve_const, dve_b, act_b, rec_ready, bc_free, rec_free = sem("dve_const"), sem("dve_b"), sem("act_b"), sem("rec_ready"), sem("bc_free"), sem("rec_free")
    sent = [sem("sent0"), sem("sent1")]
    with ExitStack() as pb:
        row_bc = ps("row_bc", [P, 2, C, P], F32, pb)
        lo_bc = ps("lo_bc", [P, 2, C, P], BF16, pb)
        lookup = ps("lookup", [P, 2, 512], F32, pb)
        block = pb.enter_context(nc.Block())

        @block.scalar
        def _(act):
            ch = Chain(act, act_b)
            act.wait_ge(dve_const, 2)

            def take_cols(c, u):
                nc.scalar.copy(col_row[:, u, :], row[:, bass.ds(c * C, C)])
                nc.scalar.copy(col_lo_b[:, u, :], row_lo[:, bass.ds(c * C, C)]).then_inc(cols_ready, 1)

            take_cols(0, 0)
            with act.Fori(0, ET // C // BC) as it:
                ch.turn(0, it, BC)
                for i in range(BC):
                    c, u = it * BC + i, i % 2
                    hold(act, bc_ready, c + 2, held["act"])
                    hold(act, bc_free, c + 2, held["act"])
                    take_cols(c + 1, 1 - u)
                    hold(act, found_ready, c + 1, held["act"])
                    nc.scalar.copy(places[:, u, :, 0, :], before[:, bass.ds(c * C, C), :])
                    act.wait_ge(bc_ready, c + 3)
                    t = ch.did(nc.scalar.activation(away[:, u, :, 0:EP], lo_bc[:, u, :, 0:EP], ACT.Abs, bias=npid[:, :]))
                    ch.need(t)
                    nc.scalar.activation(hot_t[:, u, :, 0:EP], away[:, u, :, 0:EP], ACT.Relu, scale=-1.0,
                                         bias=one[:, :]).then_inc(hot_t_ready, 1)

        @block.tensor
        def _(pe):
            pe.sem_inc(bc_ready, 2)
            pe.sem_inc(found_ready, 2)

            def turn(c, u):
                hold(pe, cols_ready, c + 1, held["pe"])
                hold(pe, bc_free, c + 1, held["pe"])
                for j in range(C):
                    nc.tensor.transpose(row_bc[:, u, j, 0:EP], col_row[:, u, j:j + 1].to_broadcast([EP, P]), ident[:EP, :EP])
                for j in range(C):
                    last = nc.tensor.transpose(lo_bc[:, u, j, 0:EP], col_lo_b[:, u, j:j + 1].to_broadcast([EP, P]), ident_ab[:EP, :EP])
                last.then_inc(bc_ready, 1)

            turn(0, 0)
            with pe.Fori(0, ET // C // BC) as it:
                for i in range(BC):
                    c, u = it * BC + i, i % 2
                    turn(c + 1, 1 - u)
                    hold(pe, hot_t_ready, c + 1, held["pe"])
                    hold(pe, lookup_free, c + 1, held["pe"])
                    for j in range(C):
                        last = nc.tensor.matmul(lookup[:EP, u, j * 2 * NT:(j + 1) * 2 * NT], hot_t[:, u, j, 0:EP],
                                                places[:, u, j].rearrange("p w h -> p (w h)"), start=True, stop=True)
                    last.then_inc(found_ready, 1)

        @block.vector
        def _(dve):
            ch = Chain(dve, dve_b)
            dve.sem_inc(bc_free, 2)
            dve.sem_inc(lookup_free, 2)
            dve.sem_inc(rec_free, 2)
            nc.vector.tensor_copy(ident_ab[:, :], ident[:, :]).then_inc(dve_const, 1)
            nc.vector.tensor_copy(places[:, :, :, 1, :].rearrange("p u c h -> p (u c) h"),
                                  over_at[:, :].unsqueeze(1).to_broadcast([P, 2 * C, NT])).then_inc(dve_const, 1)
            dve.wait_ge(dst_in, 16)
            dve.wait_ge(attr_in, 16)
            t = ch.did(nc.vector.tensor_scalar(tmp_i[:, :], dst_i[:, :], P - 1, None, ALU.bitwise_and))
            nc.vector.tensor_copy(col_f[:, :], dst_i[:, :])
            nc.vector.memset(record[:, :, :, VALID], 1.0)
            ch.need(t)
            t = ch.did(nc.vector.tensor_copy(col_lo[:, :], tmp_i[:, :]))
            ch.need(t)
            t = ch.did(nc.vector.tensor_scalar(tmp_i[:, :], dst_i[:, :], 7, None, ALU.arith_shift_right))
            ch.need(t)
            t = ch.did(nc.vector.tensor_copy(col_hi[:, :], tmp_i[:, :]))
            ch.need(t)
            start = ch.n
            per = 2 * (CN * 2 + 18)
            with dve.Fori(0, SN // 2) as it:
                ch.turn(start, it, per)
                for u in range(2):
                    s = it * 2 + u
                    for cc in range(CN):
                        c, v = s * CN + cc, (u * CN + cc) % 2
                        js = slice(cc * C, (cc + 1) * C)
                        ch.did(nc.vector.tensor_tensor(hi_mask[:, :, :], iota[:EP, 0:NT].unsqueeze(1).to_broadcast([EP, C, NT]),
                                                       row_hi[:, bass.ds(c * C, C)].unsqueeze(2).to_broadcast([EP, C, NT]),
                                                       ALU.is_equal))
                        dve.wait_ge(bc_ready, c + 3)
                        for j in range(C):
                            last = nc.vector.scalar_tensor_tensor(
                                out=junk[:, j, 0:EP], in0=row_bc[:EP, v, j, 0:EP], scalar=col_row[:, v, j:j + 1],
                                in1=lower[:EP, 0:EP], op0=ALU.is_equal, op1=ALU.mult,
                                accum_out=within[:, cc * C + j:cc * C + j + 1])
                        hm = bc_free, c + 3
                        last.then_inc(bc_free, 1)
                        dve.wait_ge(found_ready, c + 3)
                        ch.need(hm)
                        nc.vector.tensor_tensor(
                            masked[:, :, :, :], lookup[:EP, v, 0:C * 2 * NT].rearrange("p (c w h) -> p c w h", c=C, w=2),
                            hi_mask[:, :, :].unsqueeze(2).to_broadcast([EP, C, 2, NT]), ALU.mult).then_inc(lookup_free, 1)
                        ch.need((lookup_free, c + 3))
                        t = ch.did(nc.vector.tensor_reduce(found[:, js, :], masked[:, :, :, :], AX.X, ALU.add))
                    e = bass.ds(s * SC, SC)
                    ch.need(t)
                    t = ch.did(nc.vector.tensor_tensor(rank[:, :], found[:, :, 0], within[:, :], ALU.add))
                    ch.need(t)
                    t = ch.did(nc.vector.tensor_copy(rank_i[:, :], rank[:, :]))
                    ch.need(t)
                    tq = ch.did(nc.vector.tensor_scalar(q_i[:, :], rank_i[:, :], 5, None, ALU.arith_shift_right))
                    tr = ch.did(nc.vector.tensor_scalar(r_i[:, :], rank_i[:, :], Q - 1, None, ALU.bitwise_and))
                    ch.need(tq)
                    tq = ch.did(nc.vector.tensor_copy(qf[:, :], q_i[:, :]))
                    ch.need(tr)
                    ch.did(nc.vector.tensor_copy(rf[:, :], r_i[:, :]))
                    ch.need(tq)
                    t = ch.did(nc.vector.tensor_tensor(far[:, :], found[:, :, 1], qf[:, :], ALU.add))
                    ch.need(t)
                    t = ch.did(nc.vector.tensor_tensor(far[:, :], far[:, :], row[:, e], ALU.subtract))
                    ch.need(t)
                    t = ch.did(nc.vector.scalar_tensor_tensor(out=far[:, :], in0=qf[:, :], scalar=1.0, in1=far[:, :],
                                                              op0=ALU.min, op1=ALU.mult))
                    ch.need(t)
                    t = ch.did(nc.vector.tensor_tensor(blk_i[:, :], far[:, :], row[:, e], ALU.add))
                    ch.need(t)
                    ch.did(nc.vector.tensor_scalar(part_i[:, 0, :], blk_i[:, :], 5, 3, ALU.arith_shift_right, ALU.bitwise_and))
                    ch.did(nc.vector.tensor_scalar(part_i[:, 1, :], blk_i[:, :], 7, None, ALU.arith_shift_right))
                    t = ch.did(nc.vector.tensor_scalar(part_i[:, 2, :], blk_i[:, :], 31, None, ALU.bitwise_and))
                    ch.need(t)
                    t = ch.did(nc.vector.tensor_copy(part[:, :, :], part_i[:, :, :]))
                    ch.need(t)
                    t = ch.did(nc.vector.scalar_tensor_tensor(out=part[:, 0, :], in0=part[:, 0, :], scalar=float(Q),
                                                              in1=rf[:, :], op0=ALU.mult, op1=ALU.add))
                    ch.need(t)
                    t = ch.did(nc.vector.scalar_tensor_tensor(out=part[:, 0, :], in0=part[:, 0, :], scalar=float(ST),
                                                              in1=part[:, 2, :], op0=ALU.mult, op1=ALU.add))
                    dve.wait_ge(rec_free, s + 1)
                    ch.need(t)
                    ch.did(nc.vector.scalar_tensor_tensor(out=slot_i[:, u, :], in0=part[:, 1, :], scalar=float(TPB),
                                                          in1=part[:, 0, :], op0=ALU.mult, op1=ALU.add))
                    ch.did(nc.vector.tensor_scalar(record[:, u, :, A0:A0 + D],
                                                   edge_attr[:, bass.ds(s * (SC * D), SC * D)].rearrange("p (t d) -> p t d", d=D),
                                                   float(KS - 1), None, ALU.mult))
                    for word, of in ((COL, col_f), (ROW, row), (CLO, col_lo), (CHI, col_hi)):
                        last = nc.vector.tensor_scalar(record[:, u, :, word], of[:, e], 1.0, None, ALU.mult)
                    last.then_inc(rec_ready, 1)
            ch.close(start, SN // 2, per)

        @block.gpsimd
        def _(pool):
            with pool.Fori(0, SN // 2) as it:
                for u in range(2):
                    hold(pool, rec_ready, it * 2 + u + 1, held["pool"])
                    for j in range(SC):
                        pool.indirect_dma_start(slots, bass.IndirectOffsetOnAxis(ap=slot_i[:, u, j:j + 1], axis=0),
                                                record[:, u, j, :], None).then_inc(sent[u], 16)

        @block.sync
        def _(sp):
            with sp.Fori(0, SN // 2) as it:
                for u in range(2):
                    hold(sp, sent[u], (it + 1) * (16 * SC), held["sp"])
                    sp.sem_inc(rec_free, 1)

def hats(ch, at, shape, hat_consts, up, down, hat, valid):
    up_c, down_c, up_floor, down_floor = [c[:, :, :].unsqueeze(1).to_broadcast(shape) for c in hat_consts]
    wide = at.unsqueeze(3).to_broadcast(shape)
    v = ch.eng
    a = ch.did(v.tensor_tensor(up[:, :, :, :], wide, up_c, ALU.subtract))
    b = ch.did(v.tensor_tensor(down[:, :, :, :], down_c, wide, ALU.subtract))
    ch.need(a)
    ch.did(v.tensor_tensor(up[:, :, :, :], up[:, :, :, :], up_floor, ALU.max))
    ch.need(b)
    b = ch.did(v.tensor_tensor(down[:, :, :, :], down[:, :, :, :], down_floor, ALU.max))
    ch.need(b)
    a = ch.did(v.tensor_tensor(hat[:, :, :, :], up[:, :, :, :], down[:, :, :, :], ALU.min))
    ch.need(a)
    return ch.did(v.tensor_tensor(hat[:, :, 0, :], hat[:, :, 0, :], valid.unsqueeze(2).to_broadcast([P, shape[1], KS]), ALU.mult))


HATS = 6


def first_layer(nc, sb, ps, sem, held, g):
    rec, slots, blocks = g["rec"], g["slots"], g["blocks"]
    with ExitStack() as c:
        up, down = sb("up1", [P, 2 * TPB, D, KS], F32, c), sb("down1", [P, 2 * TPB, D, KS], F32, c)
        hat = sb("hat1", [P, 2 * TPB, D, KS], F32, c)
        hat01 = sb("hat01_1", [P, 2, TPB, KS * KS], F32, c)
        hat2 = sb("hat2_1", [P, 2, TPB, P // Q, KS], F32, c)
        sums = sb("sums", [KS * KS, 2, P // Q, TPB, KS], F32, c)
        wt1 = sb("wt1", [KS * KS, KS * FH], F32, c)
        sum_ps = ps("sum_ps", [P, 2, 2, 512], F32, c)
        row_ps = ps("row_ps", [P, 2, 512], F32, c)
        rec_in, small_in, const_done, w_in = sem("rec_in"), sem("small_in"), sem("const_done"), sem("w_in")
        hats_ready, block_ready, hat_ready, hat2_ready, sum_ready, sums_copied, row_ready, row_copied, dve_c = [sem(n) for n in (
            "hats_ready", "of_block_ready", "hat_ready", "hat2_ready", "sum_ready", "sums_copied", "row_ready", "row_copied", "dve_c")]
        dve_ov = sem("dve_ov")
        block = c.enter_context(nc.Block())

        @block.sync
        def _(sp):
            s = slots.rearrange("(p t) c -> p t c", p=P)
            sp.dma_start(wt1[:, :], g["w1"].rearrange("(a b) i f -> a (b i f)", b=KS)).then_inc(w_in, 16)
            with sp.Fori(0, BT // 2) as it:
                e = bass.ds(it * (2 * TPB), 2 * TPB)
                sp.dma_start(rec[:, e, :], s[:, e, :]).then_inc(rec_in, 16)
                hold(sp, rec_in, (it + 1) * 16, held["sp"])
            for q in range(P // Q):
                sp.dma_start(g["ovn"][q * Q:(q + 1) * Q, :],
                             s[q * Q, ST // 2:ST, ROW].rearrange("(b j) -> j b", j=TPB),
                             allow_slow_non_contiguous=True).then_inc(small_in, 16)
            sp.dma_start(g["wt3"][:, :], g["w3"]).then_inc(small_in, 16)
            sp.dma_start(g["wt4"][:, :], g["w4"]).then_inc(small_in, 16)
            sp.dma_start(g["bt3"][:, :], g["b3"].unsqueeze(1)).then_inc(small_in, 16)
            for to, of, n in (("bt1", "b1", FH), ("bt2", "b2", FH), ("btc", "bc", FIN), ("bt4", "b4", D)):
                sp.dma_start(g[to][:, :], g[of].unsqueeze(0).to_broadcast([P, n])).then_inc(small_in, 16)
            sp.wait_ge(const_done, 1)
            full = N // P
            sp.dma_start(g["x_nodes"][:, 0:full, :], g["x"][0:full * P, :].rearrange("(t p) f -> p t f", p=P)).then_inc(small_in, 16)
            sp.dma_start(g["x_nodes"][0:N - full * P, full, :], g["x"][full * P:N, :]).then_inc(small_in, 16)
            sp.wait_ge(small_in, 16 * 13)

        @block.vector
        def _(dve):
            nc.vector.memset(rec[:, ST:ST + AHEAD, :], 0.0)
            nc.vector.memset(g["x_nodes"][:, :, :], 0.0).then_inc(const_done, 1)
            nc.vector.memset(blocks[:, :, :], 0.0).then_inc(const_done, 1)
            ch = Chain(nc.vector, dve_c)
            t = ch.did(nc.vector.tensor_scalar(g["inv_degree"][:, :], g["deg"][:, :], 1.0, None, ALU.max))
            ch.need(t)
            ch.did(nc.vector.reciprocal(g["inv_degree"][:, :], g["inv_degree"][:, :]))
            nc.vector.memset(g["of_block"][:, :], 0.0)
            for j in range(KS):
                nc.vector.memset(g["up_c"][:, :, j], float(j - 1))
                nc.vector.memset(g["down_c"][:, :, j], float(j + 1))
                nc.vector.memset(g["up_floor"][:, :, j], BIG if j == 0 else -BIG if j == 1 else 0.0)
                t = ch.did(nc.vector.memset(g["down_floor"][:, :, j], BIG if j == KS - 1 else -BIG if j == KS - 2 else 0.0))
            ch.need(t)
            for q in range(P // Q):
                t = ch.did(nc.vector.memset(g["of_block"][q * Q:(q + 1) * Q, q:q + 1], 1.0))
            ch.need(t)
            dve.sem_inc(block_ready, 1)
            dve.sem_inc(hat_ready, 1)
            start, per = ch.n, HATS
            used = used_pairs(dve, g["pairs"])
            with dve.Fori(0, BT // 2) as it, dve.If(it < used):
                ch.turn(start, it, per)
                e = bass.ds(it * (2 * TPB), 2 * TPB)
                dve.wait_ge(rec_in, (it + 1) * 16)
                dve.wait_ge(hat2_ready, it * 2 + 1)
                t = hats(ch, rec[:, e, A0:A0 + D], [P, 2 * TPB, D, KS], g["hat_consts"], up, down, hat, rec[:, e, VALID])
                ch.need(t)
                dve.sem_inc(hat_ready, 1)
                for u in range(2):
                    c, ts = it * 2 + u, slice(u * TPB, (u + 1) * TPB)
                    dve.wait_ge(sum_ready, c + 1)
                    nc.vector.tensor_tensor(hat01[:, u].rearrange("p t (a b) -> p t a b", a=KS),
                                            hat[:, ts, 0, :].unsqueeze(3).to_broadcast([P, TPB, KS, KS]),
                                            hat[:, ts, 1, :].unsqueeze(2).to_broadcast([P, TPB, KS, KS]),
                                            ALU.mult).then_inc(hats_ready, 1)
            ch = Chain(nc.vector, dve_ov)
            dve.wait_ge(small_in, 16 * 13)
            t = ch.did(nc.vector.tensor_copy(g["ovn_i"][:, :], g["ovn"][:, :]))
            ch.need(t)
            t = ch.did(nc.vector.tensor_scalar(g["ov_i"][:, :], g["ovn_i"][:, :], P - 1, None, ALU.bitwise_and))
            ch.need(t)
            t = ch.did(nc.vector.tensor_copy(g["ov_lo"][:, :], g["ov_i"][:, :]))
            ch.need(t)
            t = ch.did(nc.vector.tensor_scalar(g["ov_i"][:, :], g["ovn_i"][:, :], 7, None, ALU.arith_shift_right))
            ch.need(t)
            ch.did(nc.vector.tensor_copy(g["ov_hi"][:, :], g["ov_i"][:, :]))

        @block.gpsimd
        def _(pool):
            pool.sem_inc(hat2_ready, 1)
            pool.wait_ge(block_ready, 1)
            used = used_pairs(pool, g["pairs"])
            with pool.Fori(0, BT // 2) as it, pool.If(it < used):
                hold(pool, hat_ready, it + 2, held["pool"])
                for u in range(2):
                    c, ts = it * 2 + u, slice(u * TPB, (u + 1) * TPB)
                    hold(pool, sum_ready, c + 1, held["pool"])
                    nc.gpsimd.tensor_tensor(hat2[:, u], hat[:, ts, 2, :].unsqueeze(2).to_broadcast([P, TPB, P // Q, KS]),
                                            g["of_block"][:, :].unsqueeze(1).unsqueeze(3).to_broadcast([P, TPB, P // Q, KS]),
                                            ALU.mult).then_inc(hat2_ready, 1)

        @block.tensor
        def _(pe):
            pe.sem_inc(sum_ready, 2)
            pe.sem_inc(row_ready, 2)
            pe.wait_ge(w_in, 16)
            used = used_pairs(pe, g["pairs"])
            with pe.Fori(0, BT // 2) as it, pe.If(it < used):
                for u in range(2):
                    c = it * 2 + u
                    hold(pe, hats_ready, c + 1, held["pe"])
                    hold(pe, hat2_ready, c + 2, held["pe"])
                    hold(pe, sums_copied, c + 1, held["pe"])
                    for j in range(TPB):
                        h, jj = divmod(j, TPB // 2)
                        last = nc.tensor.matmul(sum_ps[0:KS * KS, u, h, jj * 20:(jj + 1) * 20], hat01[:, u, j, :],
                                                hat2[:, u, j].rearrange("p q k -> p (q k)"), start=True, stop=True)
                    last.then_inc(sum_ready, 1)
                for u in range(2):
                    c = it * 2 + u
                    hold(pe, sums_copied, c + 3, held["pe"])
                    hold(pe, row_copied, c + 1, held["pe"])
                    for k in range(KS):
                        last = nc.tensor.matmul(row_ps[:, u, 0:FH], sums[:, u, :, :, k].rearrange("p q t -> p (q t)"),
                                                wt1[:, k * FH:(k + 1) * FH], start=(k == 0), stop=(k == KS - 1))
                    last.then_inc(row_ready, 1)

        @block.scalar
        def _(act):
            act.sem_inc(sums_copied, 2)
            act.sem_inc(row_copied, 2)
            act.wait_ge(const_done, 2)
            used = used_pairs(act, g["pairs"])
            with act.Fori(0, BT // 2) as it, act.If(it < used):
                for u in range(2):
                    c = it * 2 + u
                    act.wait_ge(sum_ready, c + 3)
                    hold(act, row_ready, c + 1, held["act"])
                    for h in range(2):
                        last = nc.scalar.copy(sums[:, u, :, h * (TPB // 2):(h + 1) * (TPB // 2), :].rearrange("p q t k -> p t q k"),
                                              sum_ps[0:KS * KS, u, h, 0:320].rearrange("p (t q k) -> p t q k", q=P // Q, k=KS))
                    last.then_inc(sums_copied, 1)
                for u in range(2):
                    c = it * 2 + u
                    hold(act, row_ready, c + 3, held["act"])
                    nc.scalar.copy(blocks[:, bass.ds(c, 1), :].rearrange("p t f -> p (t f)"), row_ps[:, u, 0:FH]).then_inc(row_copied, 1)


def gather_overflow(nc, sb, ps, sem, held, iota, blocks, pairs, ov_lo, ov_hi, inv_degree, bias, F, hid, name, x_nodes=None, out=None):
    with ExitStack() as c:
        hot = sb("ov_hot_" + name, [P, 3, P], F32, c)
        mask = sb("ov_mask_" + name, [P, NT, NT], F32, c)
        spread = sb("ov_spread_" + name, [P, 3, NT, F], F32, c)
        node = sb("node_" + name, [P, NT, F], F32, c)
        pos = sb("node_pos_" + name, [P, NT, F], F32, c)
        neg = sb("node_neg_" + name, [P, NT, F], F32, c)
        stat = sb("stat_" + name, [P, 3, NT], F32, c)
        eps = sb("eps_" + name, [P, 1], F32, c)
        add_ps = ps("add_ps_" + name, [P, 4 * 512], F32, c)
        s_spread, s_added, s_spread_last, s_added_all, s_dve, s_neg, s_exp, s_out = [sem(n + name) for n in (
            "spread_ready_", "added_", "spread_last_", "added_all_", "dve_g_", "neg_ready_", "exp_ready_", "out_stored_")]
        per_bank = 512 // F
        steps = []
        banks = [(h, min(h + per_bank, NT)) for h in range(0, NT, per_bank)]
        block = c.enter_context(nc.Block())

        @block.vector
        def _(dve):
            ch = Chain(nc.vector, s_dve)
            nc.vector.memset(eps[:, :], 1e-5)
            t = ch.did(nc.vector.tensor_tensor(mask[:, :, :], iota[:, 0:NT].unsqueeze(1).to_broadcast([P, NT, NT]),
                                               ov_hi[:, :].unsqueeze(2).to_broadcast([P, NT, NT]), ALU.is_equal))
            ch.need(t)
            def spread_tile(i, o):
                last = i == NT - 1
                if i >= 2 and not last:
                    dve.wait_ge(s_added, i - 1)
                nc.vector.tensor_tensor(hot[:, 2 if last else i % 2, :], iota[:, :], ov_lo[:, o:o + 1].to_broadcast([P, P]), ALU.is_equal)
                nc.vector.tensor_tensor(spread[:, 2 if last else i % 2], blocks[:, NT + o, 0:F].unsqueeze(1).to_broadcast([P, NT, F]),
                                        mask[:, o, :].unsqueeze(2).to_broadcast([P, NT, F]), ALU.mult).then_inc(
                                            s_spread_last if last else s_spread, 1)

            over_tiles(dve, pairs, spread_tile)
            dve.wait_ge(s_added_all, 1)
            t = ch.did(nc.vector.tensor_tensor(node[:, :, :], blocks[:, 0:NT, 0:F],
                                               add_ps[:, 0:NT * F].rearrange("p (t f) -> p t f", f=F), ALU.add))
            ch.need(t)
            t = ch.did(nc.vector.tensor_tensor(node[:, :, :], node[:, :, :], inv_degree[:, :].unsqueeze(2).to_broadcast([P, NT, F]), ALU.mult))
            ch.need(t)
            t = ch.did(nc.vector.tensor_tensor(node[:, :, :], node[:, :, :], bias[:, :].unsqueeze(1).to_broadcast([P, NT, F]), ALU.add))
            ch.need(t)
            if out is None:
                nc.vector.tensor_scalar(neg[:, :, :], node[:, :, :], 0.0, None, ALU.min).then_inc(s_neg, 1)
                t = ch.did(nc.vector.tensor_scalar(pos[:, :, :], node[:, :, :], 0.0, None, ALU.max))
                dve.wait_ge(s_exp, 1)
                ch.need(t)
                ch.did(nc.vector.scalar_tensor_tensor(out=hid[:, :, :], in0=neg[:, :, :], scalar=-1.0, in1=pos[:, :, :],
                                                      op0=ALU.add, op1=ALU.add))
                return
            t = ch.did(nc.vector.tensor_tensor(node[:, :, :], node[:, :, :], x_nodes[:, :, :], ALU.add))
            ch.need(t)
            t = ch.did(nc.vector.tensor_reduce(stat[:, 0, :], node[:, :, :], AX.X, ALU.add))
            ch.need(t)
            t = ch.did(nc.vector.tensor_scalar(stat[:, 0, :], stat[:, 0, :], 1.0 / F, None, ALU.mult))
            ch.need(t)
            t = ch.did(nc.vector.tensor_tensor(node[:, :, :], node[:, :, :], stat[:, 0, :].unsqueeze(2).to_broadcast([P, NT, F]), ALU.subtract))
            ch.need(t)
            t = ch.did(nc.vector.tensor_tensor(pos[:, :, :], node[:, :, :], node[:, :, :], ALU.mult))
            ch.need(t)
            t = ch.did(nc.vector.tensor_reduce(stat[:, 1, :], pos[:, :, :], AX.X, ALU.add))
            ch.need(t)
            nc.vector.tensor_scalar(stat[:, 1, :], stat[:, 1, :], 1.0 / F, 1e-5, ALU.mult, ALU.add).then_inc(s_neg, 1)
            dve.wait_ge(s_exp, 1)
            t = ch.did(nc.vector.reciprocal(stat[:, 2, :], stat[:, 2, :]))
            ch.need(t)
            ch.did(nc.vector.tensor_tensor(neg[:, :, :], node[:, :, :], stat[:, 2, :].unsqueeze(2).to_broadcast([P, NT, F]), ALU.mult))
            steps.append(ch.now())

        @block.tensor
        def _(pe):
            def add_tile(i, o):
                final = i == NT - 1
                pe.wait_ge(s_spread_last, 1) if final else pe.wait_ge(s_spread, i + 1)
                for b0, b1 in banks:
                    last = nc.tensor.matmul(add_ps[:, b0 * F:b1 * F], hot[:, 2 if final else i % 2, :],
                                            spread[:, 2 if final else i % 2, b0:b1, :].rearrange("p t f -> p (t f)"),
                                            start=(i == 0), stop=(i == NT - 1))
                last.then_inc(s_added_all if final else s_added, 1)

            over_tiles(pe, pairs, add_tile)

        @block.scalar
        def _(act):
            act.wait_ge(s_neg, 1)
            if out is None:
                nc.scalar.activation(neg[:, :, :], neg[:, :, :], ACT.Exp).then_inc(s_exp, 1)
            else:
                nc.scalar.activation(stat[:, 2, :], stat[:, 1, :], ACT.Sqrt).then_inc(s_exp, 1)

        if out is not None:
            @block.sync
            def _(sp):
                sp.wait_ge(s_dve, steps[0])
                full = N // P
                sp.dma_start(out[0:full * P, :].rearrange("(t p) f -> p t f", p=P), neg[:, 0:full, :]).then_inc(s_out, 16)
                sp.dma_start(out[full * P:N, :], neg[0:N - full * P, full, :]).then_inc(s_out, 16)
                sp.wait_ge(s_out, 32)


def over_tiles(eng, pairs, step):
    used = used_pairs(eng, pairs)
    step(0, 0)
    for o in range(2, NT, 3):
        with eng.If(NT + o < used * 2):
            for each in range(o, min(o + 3, NT)):
                step(each - 1, each)
    step(NT - 1, 1)


def to_table(nc, sem, hid, x_nodes, table):
    stored = sem("table_stored")
    t = table.rearrange("(t p) f -> p t f", p=P)
    with nc.Block() as block:
        @block.sync
        def _(sp):
            sp.dma_start(t[:, :, 0:FH], hid[:, :, :]).then_inc(stored, 16)
            sp.dma_start(t[:, :, FH:HX], x_nodes[:, :, :]).then_inc(stored, 16)
            sp.wait_ge(stored, 32)


def conv(nc, sb, ps, sem, held, rec, hat_consts, of_block, ident, pairs, blocks, weights, table, x_slots):
    name, F = "two", FH
    NQ = P // Q
    UT = 1024 // (NQ * F)
    NU = TPB // UT
    R = 2
    with ExitStack() as c:
        up, down = sb("up" + name, [P, TPB, D, KS], F32, c), sb("down" + name, [P, TPB, D, KS], F32, c)
        wt = sb("wt" + name, [K, F * F], F32, c)
        hat01 = sb("hat01" + name, [P, TPB, KS * KS], F32, c)
        basis = sb("basis" + name, [P, R, UT, K], F32, c)
        apart = sb("apart" + name, [P, R, UT, NQ, F], F32, c)
        feat = sb("feat" + name, [P, 2, TPB, HX], F32, c)
        agg = sb("agg" + name, [K, 2 * TPB, NQ, F], F32, c)
        rows_t = sb("rows_t" + name, [F, 2, NQ, TPB], F32, c)
        agg_ps = ps("agg_ps" + name, [P, 2, 1024], F32, c)
        rows_ps = ps("rows_ps" + name, [P, 512], F32, c)
        turned_ps = ps("turned_ps" + name, [P, 512], F32, c)
        unit_ready, unit_done, unit_copied, rows_ready, rows_copied, turned, weights_in, s_dve = [sem(n + name) for n in (
            "unit_ready_", "unit_done_", "unit_copied_", "rows_ready_", "rows_copied_", "turned_", "weights_in_", "dve_h_")]
        PARTS = 4
        came = [[sem(f"came{u}_{h}_{name}") for h in range(PARTS)] for u in range(2)]
        index = sb("index", [P, 2, TPB], I32, c)
        x_part = sb("x_part", [P, TPB, FIN], F32, c)
        x_ready, x_free, x_stored, index_ready = [sem(n) for n in ("x_ready", "x_free", "x_stored", "index_ready")]
        block = c.enter_context(nc.Block())

        @block.vector
        def _(dve):
            ch = Chain(nc.vector, s_dve)
            dve.sem_inc(unit_ready, 2 * NU)
            used = used_pairs(dve, pairs)
            ch.did(nc.vector.memset(up[:, :, :, :], 0.0))
            start, per = ch.n, 2 * (HATS + 2)
            with dve.Fori(0, BT // 2) as it, dve.If(it < used):
                ch.turn(start, it, per)
                for u in range(2):
                    c = it * 2 + u
                    e = bass.ds(c * TPB, TPB)
                    ch.need((s_dve, ch.now()))
                    t = hats(ch, rec[:, e, A0:A0 + D], [P, TPB, D, KS], hat_consts, up, down, up, rec[:, e, VALID])
                    hat = up
                    ch.need(t)
                    t = ch.did(nc.vector.tensor_tensor(hat01[:, :, :].rearrange("p t (a b) -> p t a b", a=KS),
                                                       hat[:, :, 0, :].unsqueeze(3).to_broadcast([P, TPB, KS, KS]),
                                                       hat[:, :, 1, :].unsqueeze(2).to_broadcast([P, TPB, KS, KS]),
                                                       ALU.mult))
                    ch.need(t)
                    for i in range(NU):
                        if i % (NU // PARTS) == 0:
                            dve.wait_ge(came[u][i // (NU // PARTS)], (it + 1) * (16 * TPB // PARTS))
                        ts = slice(i * UT, (i + 1) * UT)
                        dve.wait_ge(unit_done, c * NU + i + 1)
                        made = nc.vector.tensor_tensor(basis[:, i % R].rearrange("p t (a b) -> p t a b", b=KS),
                                                       hat01[:, ts, :].unsqueeze(3).to_broadcast([P, UT, KS * KS, KS]),
                                                       hat[:, ts, 2, :].unsqueeze(2).to_broadcast([P, UT, KS * KS, KS]),
                                                       ALU.mult)
                        if i == NU - 1:
                            ch.did(made)
                        nc.vector.tensor_tensor(apart[:, i % R], feat[:, u, ts, 0:F].unsqueeze(2).to_broadcast([P, UT, NQ, F]),
                                                of_block[:, :].unsqueeze(1).unsqueeze(3).to_broadcast([P, UT, NQ, F]),
                                                ALU.mult).then_inc(unit_ready, 1)
            ch.close(start, BT // 2, per)

        @block.scalar
        def _(act):
            act.dma_start(wt[:, :], weights.rearrange("k i o -> k (i o)")).then_inc(weights_in, 16)
            act.sem_inc(unit_copied, 2)
            act.sem_inc(x_ready, 2)
            used = used_pairs(act, pairs)
            with act.Fori(0, BT // 2) as it, act.If(it < used):
                for u in range(2):
                    c = it * 2 + u
                    for i in range(NU):
                        if i % (NU // PARTS) == 0:
                            part, ts = i // (NU // PARTS), slice(i * UT, (i + NU // PARTS) * UT)
                            if i == 0:
                                hold(act, x_free, c + 1, held["act"])
                            act.wait_ge(came[u][part], (it + 1) * (16 * TPB // PARTS))
                            taken = nc.scalar.copy(x_part[:, ts, :], feat[:, u, ts, FH:HX])
                            if part == PARTS - 1:
                                taken.then_inc(x_ready, 1)
                        act.wait_ge(unit_done, c * NU + i + R + 1)
                        nc.scalar.copy(agg[:, u * TPB + i * UT:u * TPB + (i + 1) * UT].rearrange("p t q f -> p (t q f)"),
                                       agg_ps[:K, i % 2, :]).then_inc(unit_copied, 1)
                act.wait_ge(rows_ready, it + 1)
                nc.scalar.copy(rows_t[:, :, :, :].rearrange("p u q t -> p u t q"),
                               rows_ps[:F, 0:2 * P].rearrange("p (u t q) -> p u t q", u=2, q=NQ)).then_inc(rows_copied, 1)
                hold(act, turned, it + 1, held["act"])
                nc.scalar.copy(blocks[:, bass.ds(it * 2, 2), 0:F], turned_ps[:, 0:2 * F].rearrange("p (t f) -> p t f", t=2))

        @block.tensor
        def _(pe):
            pe.sem_inc(unit_done, R)
            pe.wait_ge(weights_in, 16)
            used = used_pairs(pe, pairs)
            with pe.Fori(0, BT // 2) as it, pe.If(it < used):
                for u in range(2):
                    for i in range(NU):
                        g = (it * 2 + u) * NU + i
                        hold(pe, unit_ready, g + 2 * NU + 1, held["pe"])
                        hold(pe, unit_copied, g + 1, held["pe"])
                        for j in range(UT):
                            last = nc.tensor.matmul(agg_ps[:K, i % 2, j * NQ * F:(j + 1) * NQ * F], basis[:, i % R, j, :],
                                                    apart[:, i % R, j].rearrange("p q f -> p (q f)"), start=True, stop=True)
                        last.then_inc(unit_done, 1)
                hold(pe, unit_copied, it * (2 * NU) + 2 * NU + 2, held["pe"])
                flat = agg[:, :, :, :].rearrange("p t q f -> p (t q) f")
                for f in range(F):
                    last = nc.tensor.matmul(rows_ps[:F, 0:2 * P], wt[:, f * F:(f + 1) * F], flat[:, :, f],
                                            start=(f == 0), stop=(f == F - 1))
                last.then_inc(rows_ready, 1)
                hold(pe, rows_copied, it + 1, held["pe"])
                for u in range(2):
                    last = nc.tensor.transpose(turned_ps[:, u * F:(u + 1) * F], rows_t[:, u].rearrange("p q t -> p (q t)"),
                                               ident[:F, :F])
                last.then_inc(turned, 1)

        @block.gpsimd
        def _(pool):
            used = used_pairs(pool, pairs)
            with pool.Fori(0, BT // 2) as it, pool.If(it < used):
                for u in range(2):
                    c = it * 2 + u
                    hold(pool, unit_ready, c * NU + NU, held["pool"])
                    hold(pool, x_ready, c + 1, held["pool"])
                    nc.gpsimd.tensor_copy(index[:, u, :], rec[:, bass.ds(c * TPB, TPB), COL]).then_inc(index_ready, 1)
                    hold(pool, index_ready, c + 1, held["pool"])
                    for j in range(TPB):
                        pool.indirect_dma_start(feat[:, u, j, :], None, table,
                                                bass.IndirectOffsetOnAxis(ap=index[:, u, j:j + 1], axis=0)).then_inc(came[u][j * PARTS // TPB], 16)

        @block.sync
        def _(sp):
            sp.sem_inc(x_free, 1)
            used = used_pairs(sp, pairs)
            with sp.Fori(0, BT // 2) as it, sp.If(it < used):
                for u in range(2):
                    c = it * 2 + u
                    hold(sp, x_ready, c + 3, held["sp"])
                    sp.dma_start(x_slots[:, bass.ds(c * (TPB * FIN), TPB * FIN)],
                                 x_part[:, :, :].rearrange("p t f -> p (t f)")).then_inc(x_stored, 16)
                    hold(sp, x_stored, c * 16 + 16, held["sp"])
                    sp.sem_inc(x_free, 1)


def last_conv(nc, sb, ps, sem, held, rec, ovn_i, t_sb, t_nodes, t_blocks, t_row, hat_consts, of_block, ident, iota, npid, one, pairs,
              blocks, weights, x_slots):
    F, NQ = FIN, P // Q
    UT = 1024 // (NQ * F)
    NU = TPB // UT
    R = 4
    U = 2 * NU
    G, G_TILES = U - 2, UT
    FIRST = U - G
    PAIR = 2 * TPB
    GATHERED = PAIR - G * G_TILES
    EARLY = GATHERED - G
    with ExitStack() as c:
        up, down = sb("up3", [P, PAIR, D, KS], F32, c), sb("down3", [P, PAIR, D, KS], F32, c)
        wt = sb("wt_last", [K, F * F], F32, c)
        hat01 = sb("hat01_3", [P, PAIR, KS * KS], F32, c)
        basis = sb("basis3", [P, R, UT, K], F32, c)
        apart = sb("apart3", [P, R, UT, NQ, F], F32, c)
        feat = sb("feat3", [P, 2, TPB, F], F32, c)
        agg = sb("agg3", [K, 2 * TPB, NQ, F], F32, c)
        rows_t = sb("rows_t3", [F, 2, NQ, TPB], F32, c)
        ident_b = sb("ident_b", [P, P], BF16, c)
        low = sb("low", [P, 2, G_TILES], BF16, c)
        hi_mask = sb("hi_mask3", [P, 2, G_TILES, NT], F32, c)
        away = sb("away3", [P, 2, G_TILES, P], BF16, c)
        hot = sb("hot3", [P, 2, G_TILES, P], BF16, c)
        masked = sb("masked3", [P, 2, G_TILES, NT, D], F32, c)
        t_col = sb("t_col", [P, PAIR, D], F32, c)
        moved = sb("moved", [P, PAIR, D], F32, c)
        t_part = sb("t_part", [P, 3, NT * D], BF16, c)
        t_rest = sb("t_rest", [P, 2, NT * D], F32, c)
        expand = sb("expand", [NQ, P], F32, c)
        agg_ps = ps("agg_ps3", [P, 2, 1024], F32, c)
        t_quad = agg[0:NQ, :, :, :].rearrange("p t q f -> p (t q f)")[:, 0:ST * D]
        row_ps = agg_ps[:, :, :].rearrange("p u (h n) -> p (u h) n", h=2)
        ROW_COLS = 480
        ROW_STEPS = ST * D // ROW_COLS
        out_ps = ps("out_ps3", [P, 512], F32, c)
        rows_ps, turned_ps = out_ps[:F, 0:2 * P], out_ps[:, 2 * P:2 * P + 2 * F]
        lo_bc = ps("lo_bc3", [P, G_TILES, P], BF16, c)
        got = ps("got", [P, G_TILES, P], F32, c)
        basis_ready, apart_ready, unit_done, unit_copied, rows_ready, rows_copied, turned, weights_in = [sem(n + "_3") for n in (
            "basis_ready", "apart_ready", "unit_done", "unit_copied", "rows_ready", "rows_copied", "turned", "weights_in")]
        low_ready, bc_ready, away_ready, hot_ready, got_ready, masked_ready, s_const, s_dve = [sem(n + "_3") for n in (
            "low_ready", "bc_ready", "away_ready", "hot_ready", "got_ready", "masked_ready", "const", "dve")]
        nodes_in, blocks_out, quad_in, expand_ready, parts_ready, t_row_ready, t_row_copied = [sem(n) for n in (
            "nodes_in", "blocks_out", "quad_in", "expand_ready", "parts_ready", "t_row_ready", "t_row_copied")]
        t_index = sb("t_index", [P, GATHERED], I32, c)
        t_index_ready, t_came, t_taken = sem("t_index_ready"), sem("t_came"), sem("t_taken")
        came = [sem("came0_3"), sem("came1_3")]

        def group_tiles(pair, i):
            return bass.ds(pair * PAIR + (i if i < G else U) * G_TILES, G_TILES)

        block = c.enter_context(nc.Block())

        @block.sync
        def _(sp):
            sp.wait_ge(nodes_in, 16 * NT)
            sp.dma_start(t_blocks, t_sb[:, :, :].rearrange("p t d -> p (t d)")).then_inc(blocks_out, 16)
            sp.wait_ge(blocks_out, 16)
            for q in range(NQ):
                sp.dma_start(t_quad[q:q + 1, :].rearrange("o (b j d) -> o b j d", b=BT, d=D),
                             t_blocks[q * Q:(q + 1) * Q, :].rearrange("j (b d) -> b j d", d=D).unsqueeze(0)).then_inc(quad_in, 16)
            used = used_pairs(sp, pairs)
            with sp.Fori(0, BT // 2) as it, sp.If(it < used):
                for u in range(2):
                    c = it * 2 + u
                    hold(sp, apart_ready, c * NU + NU, held["sp"])
                    sp.dma_start(feat[:, u].rearrange("p t f -> p (t f)"),
                                 x_slots[:, bass.ds(c * (TPB * FIN), TPB * FIN)]).then_inc(came[u], 16)

        @block.gpsimd
        def _(pool):
            pool.sem_inc(apart_ready, 2 * NU)

            def take_low(pair, i):
                hold(pool, bc_ready, pair * G + i + 1, held["pool"])
                nc.gpsimd.tensor_copy(low[:, i % 2, :], rec[:, group_tiles(pair, i), CLO]).then_inc(low_ready, 1)

            def take_index(pair):
                nc.gpsimd.tensor_copy(t_index[:, :], rec[:, bass.ds(pair * PAIR + G * G_TILES, GATHERED), COL]).then_inc(t_index_ready, 1)
                hold(pool, t_index_ready, pair + 1, held["pool"])

            def gather(j):
                pool.indirect_dma_start(t_col[:, G * G_TILES + j, :], None, t_nodes,
                                        bass.IndirectOffsetOnAxis(ap=t_index[:, j:j + 1], axis=0)).then_inc(t_came, 16)

            ch = Chain(nc.gpsimd, expand_ready)
            t = ch.did(nc.gpsimd.memset(expand[:, :], 1.0))
            ch.need(t)
            t = ch.did(nc.gpsimd.affine_select(out=expand[:, :], in_=expand[:, :], compare_op=ALU.is_ge, fill=0.0,
                                               base=0, pattern=[[1, P]], channel_multiplier=-Q))
            ch.need(t)
            ch.did(nc.gpsimd.affine_select(out=expand[:, :], in_=expand[:, :], compare_op=ALU.is_ge, fill=0.0,
                                           base=Q - 1, pattern=[[-1, P]], channel_multiplier=Q))
            for g in range(G + 1):
                take_low(0, g)
                for o in range(g * NT // (G + 1), (g + 1) * NT // (G + 1)):
                    pool.indirect_dma_start(t_sb[:, NT + o, :], None, t_nodes,
                                            bass.IndirectOffsetOnAxis(ap=ovn_i[:, o:o + 1], axis=0)).then_inc(nodes_in, 16)
            take_index(0)
            for j in range(GATHERED):
                gather(j)

            def gather_early(pair):
                hold(pool, t_came, pair * (16 * GATHERED), held["pool"])
                hold(pool, t_taken, pair, held["pool"])
                take_index(pair)
                for j in range(EARLY):
                    gather(j)

            gather_early(1)
            used = used_pairs(pool, pairs)
            with pool.Fori(0, BT // 2) as it, pool.If(it < used):
                for i in range(U):
                    u, ts = i // NU, slice(i % NU * UT, (i % NU + 1) * UT)
                    if i >= FIRST:
                        take_low(it + 1, i - FIRST + 1)
                    if i % NU == 0:
                        hold(pool, came[u], (it + 1) * 16, held["pool"])
                    hold(pool, unit_done, it * U + i + 1, held["pool"])
                    nc.gpsimd.tensor_tensor(apart[:, i % R], feat[:, u, ts, 0:F].unsqueeze(2).to_broadcast([P, UT, NQ, F]),
                                            of_block[:, :].unsqueeze(1).unsqueeze(3).to_broadcast([P, UT, NQ, F]),
                                            ALU.mult).then_inc(apart_ready, 1)
                    if i >= FIRST:
                        gather(EARLY + i - FIRST)
                gather_early(it + 2)

        @block.vector
        def _(dve):
            dve.sem_inc(masked_ready, 1)
            nc.vector.tensor_copy(ident_b[:, :], ident[:, :]).then_inc(s_const, 1)
            nc.vector.memset(t_row[:, ST:ST + PAIR, :], 0.0)
            ch = Chain(nc.vector, parts_ready)
            t_flat = t_sb[:, 0:NT, :].rearrange("p t d -> p (t d)")
            t = ch.did(nc.vector.tensor_copy(t_part[:, 0, :], t_flat))
            ch.need(t)
            t = ch.did(nc.vector.tensor_tensor(t_rest[:, 0, :], t_flat, t_part[:, 0, :], ALU.subtract))
            ch.need(t)
            t = ch.did(nc.vector.tensor_copy(t_part[:, 1, :], t_rest[:, 0, :]))
            ch.need(t)
            t = ch.did(nc.vector.tensor_tensor(t_rest[:, 1, :], t_rest[:, 0, :], t_part[:, 1, :], ALU.subtract))
            ch.need(t)
            ch.did(nc.vector.tensor_copy(t_part[:, 2, :], t_rest[:, 1, :]))
            ch = Chain(nc.vector, s_dve)

            def mask_group(pair, i):
                u, g = i % 2, pair * G + i
                t = ch.did(nc.vector.tensor_tensor(hi_mask[:, u], iota[:, 0:NT].unsqueeze(1).to_broadcast([P, G_TILES, NT]),
                                                   rec[:, group_tiles(pair, i), CHI].unsqueeze(2).to_broadcast([P, G_TILES, NT]),
                                                   ALU.is_equal))
                ch.need(t)
                dve.wait_ge(got_ready, g + 3)
                nc.vector.tensor_tensor(masked[:, u], got[:, :, 0:NT * D].rearrange("p c (h d) -> p c h d", d=D),
                                        hi_mask[:, u].unsqueeze(3).to_broadcast([P, G_TILES, NT, D]), ALU.mult).then_inc(masked_ready, 1)
                dve.wait_ge(masked_ready, g + 2)
                return ch.did(nc.vector.tensor_reduce(t_col[:, i * G_TILES:(i + 1) * G_TILES, :],
                                                      masked[:, u].rearrange("p c h d -> p c d h"), AX.X, ALU.add))

            def move(pair):
                e = bass.ds(pair * PAIR, PAIR)
                dve.wait_ge(t_came, (pair + 1) * (16 * GATHERED))
                t = ch.did(nc.vector.scalar_tensor_tensor(out=moved[:, :, :], in0=rec[:, e, A0:A0 + D], scalar=1.0 / (KS - 1),
                                                          in1=t_col[:, :, :], op0=ALU.mult, op1=ALU.add))
                ch.need(t)
                dve.sem_inc(t_taken, 1)
                t = ch.did(nc.vector.tensor_tensor(moved[:, :, :], moved[:, :, :], t_row[:, e, :], ALU.subtract))
                ch.need(t)
                t = ch.did(nc.vector.tensor_scalar(moved[:, :, :], moved[:, :, :], 0.0, 1.0, ALU.max, ALU.min))
                ch.need(t)
                return ch.did(nc.vector.tensor_scalar(moved[:, :, :], moved[:, :, :], float(KS - 1), None, ALU.mult))

            for g in range(G):
                t = mask_group(0, g)
            ch.need(t)
            dve.wait_ge(t_row_copied, ROW_STEPS)
            ch.need(move(0))
            start, per = ch.n, HATS + 1 + 2 * G + 4
            used = used_pairs(dve, pairs)
            with dve.Fori(0, BT // 2) as it, dve.If(it < used):
                ch.turn(start, it, per)
                ch.need((s_dve, ch.now()))
                t = hats(ch, moved[:, :, :], [P, PAIR, D, KS], hat_consts, up, down, up,
                         rec[:, bass.ds(it * PAIR, PAIR), VALID])
                hat = up
                ch.need(t)
                t = ch.did(nc.vector.tensor_tensor(hat01[:, :, :].rearrange("p t (a b) -> p t a b", a=KS),
                                                   hat[:, :, 0, :].unsqueeze(3).to_broadcast([P, PAIR, KS, KS]),
                                                   hat[:, :, 1, :].unsqueeze(2).to_broadcast([P, PAIR, KS, KS]),
                                                   ALU.mult))
                ch.need(t)
                for i in range(U):
                    ts = slice(i * UT, (i + 1) * UT)
                    dve.wait_ge(unit_done, it * U + i + 1)
                    nc.vector.tensor_tensor(basis[:, i % R].rearrange("p t (a b) -> p t a b", b=KS),
                                            hat01[:, ts, :].unsqueeze(3).to_broadcast([P, UT, KS * KS, KS]),
                                            hat[:, ts, 2, :].unsqueeze(2).to_broadcast([P, UT, KS * KS, KS]),
                                            ALU.mult).then_inc(basis_ready, 1)
                    if i > FIRST:
                        mask_group(it + 1, i - FIRST - 1)
                t = mask_group(it + 1, G - 1)
                ch.need(t)
                move(it + 1)
            ch.close(start, BT // 2, per)

        @block.scalar
        def _(act):
            act.dma_start(wt[:, :], weights.rearrange("k i o -> k (i o)")).then_inc(weights_in, 16)
            act.sem_inc(unit_copied, 2)
            act.sem_inc(away_ready, 1)

            def one_hot(g, i):
                u = i % 2
                act.wait_ge(bc_ready, g + 3)
                nc.scalar.activation(away[:, u], lo_bc[:, :, :], ACT.Abs, bias=npid[:, :]).then_inc(away_ready, 1)
                hold(act, got_ready, g + 1, held["act"])
                act.wait_ge(away_ready, g + 2)
                nc.scalar.activation(hot[:, u], away[:, u], ACT.Relu, scale=-1.0, bias=one[:, :]).then_inc(hot_ready, 1)

            for i in range(G + 1):
                one_hot(i, i)
            t_row_flat = t_row[:, 0:ST, :].rearrange("p t d -> p (t d)")
            for i in range(ROW_STEPS):
                act.wait_ge(t_row_ready, i + 1)
                nc.scalar.copy(t_row_flat[:, i * ROW_COLS:(i + 1) * ROW_COLS], row_ps[:, i % 4, 0:ROW_COLS]).then_inc(t_row_copied, 1)
            used = used_pairs(act, pairs)
            with act.Fori(0, BT // 2) as it, act.If(it < used):
                for i in range(U):
                    act.wait_ge(unit_done, it * U + i + R + 1)
                    nc.scalar.copy(agg[:, i * UT:(i + 1) * UT].rearrange("p t q f -> p (t q f)"),
                                   agg_ps[:K, i % 2, :]).then_inc(unit_copied, 1)
                    if i >= FIRST:
                        one_hot((it + 1) * G + i - FIRST + 1, i - FIRST + 1)
                act.wait_ge(rows_ready, it + 1)
                nc.scalar.copy(rows_t[:, :, :, :].rearrange("p u q t -> p u t q"),
                               rows_ps.rearrange("p (u t q) -> p u t q", u=2, q=NQ)).then_inc(rows_copied, 1)
                hold(act, turned, it + 1, held["act"])
                nc.scalar.copy(blocks[:, bass.ds(it * 2, 2), 0:F], turned_ps.rearrange("p (t f) -> p t f", t=2))

        @block.tensor
        def _(pe):
            pe.sem_inc(unit_done, R)
            pe.sem_inc(bc_ready, 2)
            pe.sem_inc(got_ready, 2)
            pe.wait_ge(s_const, 1)

            def turn_low(g, i):
                hold(pe, low_ready, g + 1, held["pe"])
                hold(pe, away_ready, g + 1, held["pe"])
                for j in range(G_TILES):
                    last = nc.tensor.transpose(lo_bc[:, j, :], low[:, i % 2, j:j + 1].to_broadcast([P, P]), ident_b[:, :])
                last.then_inc(bc_ready, 1)

            def fetch(g, i):
                hold(pe, hot_ready, g + 1, held["pe"])
                hold(pe, masked_ready, g + 1, held["pe"])
                for j in range(G_TILES):
                    for part in range(3):
                        last = nc.tensor.matmul(got[:, j, 0:NT * D], hot[:, i % 2, j, :], t_part[:, part, :],
                                                start=(part == 0), stop=(part == 2))
                last.then_inc(got_ready, 1)

            turn_low(0, 0)
            pe.wait_ge(parts_ready, 5)
            for g in range(G):
                turn_low(g + 1, g + 1)
                fetch(g, g)
            pe.wait_ge(expand_ready, 3)
            pe.wait_ge(quad_in, 16 * NQ)
            for i in range(ROW_STEPS):
                if i >= 4:
                    pe.wait_ge(t_row_copied, i - 3)
                nc.tensor.matmul(row_ps[:, i % 4, 0:ROW_COLS], expand[:, :], t_quad[:, i * ROW_COLS:(i + 1) * ROW_COLS],
                                 start=True, stop=True).then_inc(t_row_ready, 1)
            pe.wait_ge(t_row_copied, ROW_STEPS)
            pe.wait_ge(weights_in, 16)
            used = used_pairs(pe, pairs)
            with pe.Fori(0, BT // 2) as it, pe.If(it < used):
                for i in range(U):
                    unit = it * U + i
                    hold(pe, basis_ready, unit + 1, held["pe"])
                    hold(pe, apart_ready, unit + 2 * NU + 1, held["pe"])
                    hold(pe, unit_copied, unit + 1, held["pe"])
                    for j in range(UT):
                        last = nc.tensor.matmul(agg_ps[:K, i % 2, j * NQ * F:(j + 1) * NQ * F], basis[:, i % R, j, :],
                                                apart[:, i % R, j].rearrange("p q f -> p (q f)"), start=True, stop=True)
                    last.then_inc(unit_done, 1)
                    if i >= FIRST:
                        turn_low((it + 1) * G + i - FIRST + 1, i - FIRST + 1)
                        fetch((it + 1) * G + i - FIRST, i - FIRST)
                hold(pe, unit_copied, it * U + U + 2, held["pe"])
                flat = agg[:, :, :, :].rearrange("p t q f -> p (t q) f")
                for f in range(F):
                    last = nc.tensor.matmul(rows_ps, wt[:, f * F:(f + 1) * F], flat[:, :, f], start=(f == 0), stop=(f == F - 1))
                last.then_inc(rows_ready, 1)
                hold(pe, rows_copied, it + 1, held["pe"])
                for u in range(2):
                    last = nc.tensor.transpose(turned_ps[:, u * F:(u + 1) * F], rows_t[:, u].rearrange("p q t -> p (q t)"),
                                               ident[:F, :F])
                last.then_inc(turned, 1)


def used_pairs(eng, pairs):
    return eng.value_load(pairs[0:1, 0:1], min_val=1, max_val=BT // 2)


def t_node(nc, sb, ps, sem, hid, wt3, bt3, wt4, bt4, ident, t_sb, t_nodes):
    with ExitStack() as c:
        hid_t = sb("hid_t", [FH, NT * P], F32, c)
        pos, neg, act3 = [sb(n, [FH, NT * P], F32, c) for n in ("t_pos", "t_neg", "act3")]
        tr_ps = ps("tr_ps", [P, 2, 512], F32, c)
        w3_ps = ps("w3_ps", [P, 2, 512], F32, c)
        w4_ps = ps("w4_ps", [P, 512], F32, c)
        s_tr, s_trc, s_w3, s_neg, s_exp, s_act3, s_w4, s_tsb, s_st = [sem("t_" + n) for n in (
            "transposed", "transposed_copied", "w3_ready", "neg_ready", "exp_ready", "act3_ready", "w4_ready", "sb", "stored")]
        GR = [(i, min(i + 4, NT)) for i in range(0, NT, 4)]
        block = c.enter_context(nc.Block())

        @block.tensor
        def _(pe):
            for i, (a, b) in enumerate(GR):
                if i >= 2:
                    pe.wait_ge(s_trc, i - 1)
                for n in range(a, b):
                    last = nc.tensor.transpose(tr_ps[0:FH, i % 2, (n - a) * P:(n - a + 1) * P], hid[:, n, :], ident[:, :])
                last.then_inc(s_tr, 1)
            for i, (a, b) in enumerate(GR):
                pe.wait_ge(s_trc, i + 1)
                if i >= 2:
                    pe.wait_ge(s_neg, i - 1)
                nc.tensor.matmul(w3_ps[0:FH, i % 2, 0:(b - a) * P], wt3[:, :], hid_t[:, a * P:b * P],
                                 start=True, stop=True).then_inc(s_w3, 1)
            pe.wait_ge(s_act3, len(GR))
            for n in range(NT):
                last = nc.tensor.matmul(w4_ps[:, n * D:(n + 1) * D], act3[:, n * P:(n + 1) * P], wt4[:, :], start=True, stop=True)
            last.then_inc(s_w4, 1)

        @block.scalar
        def _(act):
            for i, (a, b) in enumerate(GR):
                act.wait_ge(s_tr, i + 1)
                nc.scalar.copy(hid_t[:, a * P:b * P], tr_ps[0:FH, i % 2, 0:(b - a) * P]).then_inc(s_trc, 1)
            for i, (a, b) in enumerate(GR):
                act.wait_ge(s_neg, i + 1)
                nc.scalar.activation(neg[:, a * P:b * P], neg[:, a * P:b * P], ACT.Exp).then_inc(s_exp, 1)

        @block.vector
        def _(dve):
            for i, (a, b) in enumerate(GR):
                dve.wait_ge(s_w3, i + 1)
                y = w3_ps[0:FH, i % 2, 0:(b - a) * P]
                nc.vector.tensor_scalar(pos[:, a * P:b * P], y, bt3[:, :], 0.0, ALU.add, ALU.max)
                nc.vector.tensor_scalar(neg[:, a * P:b * P], y, bt3[:, :], 0.0, ALU.add, ALU.min).then_inc(s_neg, 1)
            for i, (a, b) in enumerate(GR):
                dve.wait_ge(s_exp, i + 1)
                nc.vector.scalar_tensor_tensor(out=act3[:, a * P:b * P], in0=neg[:, a * P:b * P], scalar=-1.0,
                                               in1=pos[:, a * P:b * P], op0=ALU.add, op1=ALU.add).then_inc(s_act3, 1)
            dve.wait_ge(s_w4, 1)
            nc.vector.tensor_tensor(t_sb[:, 0:NT, :], w4_ps[:, 0:NT * D].rearrange("p (t d) -> p t d", d=D),
                                    bt4[:, :].unsqueeze(1).to_broadcast([P, NT, D]), ALU.add).then_inc(s_tsb, 1)

        @block.sync
        def _(sp):
            sp.wait_ge(s_tsb, 1)
            sp.dma_start(t_nodes.rearrange("(t p) d -> p t d", p=P), t_sb[:, 0:NT, :]).then_inc(s_st, 16)
            sp.wait_ge(s_st, 16)


_INS = ["x", "src", "dst", "edge_attr_3"] + ["L0_gnn_" + n for n in (
    "stn1_w", "stn1_b", "stn2_w", "stn2_b", "stn3_w", "stn3_b", "stn4_w", "stn4_b", "conv_w", "conv_b")]


def kernel(**inputs):
    import numpy as np
    import concourse.bacc as bacc
    from concourse.bass_utils import run_bass_kernel_spmd

    nc = bacc.Bacc("TRN2", target_bir_lowering=False, num_devices=1)
    arrays, args = {}, []
    for name in _INS:
        a = np.ascontiguousarray(inputs[name])
        arrays[f"in_{name}"] = a
        args.append(nc.dram_tensor(f"in_{name}", a.shape, mybir.dt.from_np(a.dtype), kind="ExternalInput").ap())
    args.append(nc.dram_tensor("out", (N, FIN), F32, kind="ExternalOutput").ap())
    spline_net(nc, *args)
    r = run_bass_kernel_spmd(nc, [arrays], core_ids=[0])
    return r.results[0]["out"]
```
